# Optimizing a Trainium2 kernel written in Bass

```python
import numpy as np
import jax
import jax.numpy as jnp

def _softmax(x, axis=-1):
    return jax.nn.softmax(x, axis=axis)

def _gelu(x):
    return jax.nn.gelu(x, approximate=True)

def _silu(x):
    return jax.nn.silu(x)

def _sigmoid(x):
    return jax.nn.sigmoid(x)

def _layernorm(x, axis=-1, eps=1e-05):
    m = jnp.mean(x, axis=axis, keepdims=True)
    v = jnp.var(x, axis=axis, keepdims=True)
    return (x - m) / jnp.sqrt(v + eps)

def _scatter_add(tgt, idx, src, axis=0):
    return tgt.at[idx].add(src)

def _segment_sum(src, seg, n):
    return jax.ops.segment_sum(src, seg, n)
kernel_name = 'mk_flamingo_gated_d2_seqx_r4_4bfe82'

def setup_inputs(seed: int=0):
    np.random.seed(seed)
    _w = jnp.asarray

    def _rec_inputs():
        import jax
        import jax.numpy as jnp
        _rk = jax.random.key(seed)
        x = -0.0003929 + 0.9999 * jax.random.normal(jax.random.fold_in(_rk, 1), (4, 1024, 256), jnp.float32)
        _lenS = 1024 - jax.random.randint(jax.random.fold_in(_rk, 7), (4,), 0, max(1, 1024 // 4) + 1, jnp.int32)
        _lenS2 = 77 - jax.random.randint(jax.random.fold_in(_rk, 8), (4,), 0, max(1, 77 // 4) + 1, jnp.int32)
        _ctx_1024P = jax.random.normal(jax.random.fold_in(_rk, 11), (4, 16, 256), jnp.float32)
        _ctx_1024c = jax.random.dirichlet(jax.random.fold_in(_rk, 511), 0.3 * jnp.ones((16,), jnp.float32), (4, 77))
        _ctx_1024t = jnp.einsum('bsk,bkd->bsd', _ctx_1024c, _ctx_1024P)
        _ctx_1024t = _ctx_1024t * jax.lax.rsqrt(jnp.mean(jnp.square(_ctx_1024t)) + 1e-12) * 0.953939
        ctx_1024 = 4.13588e-05 + 0.999923 * (_ctx_1024t + 0.3 * jax.random.normal(jax.random.fold_in(_rk, 611), (4, 77, 256), jnp.float32))
        _validS = jnp.arange(1024)[None, :] < _lenS[:, None]
        _validS2 = jnp.arange(77)[None, :] < _lenS2[:, None]
        _causal = jnp.tril(jnp.ones((1024, 1024), dtype=bool))
        mask_BxS2_bf0 = jnp.logical_not(jnp.ones((4, 77), dtype=bool))
        _g = jax.random.normal(jax.random.fold_in(_rk, 9001), (2, 2), jnp.float32)
        _g = jnp.sign(_g) * jnp.maximum(jnp.abs(_g), 1.0) + (_g == 0) * 1.0
        g_xattn = _g[0]
        g_ffn = _g[1]
        return (x, ctx_1024, mask_BxS2_bf0, g_xattn, g_ffn)
    x, ctx_1024, mask_BxS2_bf0, g_xattn, g_ffn = _rec_inputs()

    def _L0_xattn_setup():
        import jax, jax.numpy as jnp
        import numpy as np
        H = 256
        B = 8
        L_CHAR = 512
        L_SUB = 256

        def _linear(x, W, b):
            return jnp.einsum('blh,oh->blo', x, W) + b

        def _interp_linear(x, out_len):
            L_in = x.shape[1]
            pos = (jnp.arange(out_len, dtype=x.dtype) + 0.5) * (L_in / out_len) - 0.5
            pos = jnp.clip(pos, 0.0, L_in - 1)
            lo = jnp.floor(pos).astype(jnp.int32)
            hi = jnp.minimum(lo + 1, L_in - 1)
            w = (pos - lo.astype(x.dtype))[None, :, None]
            return x[:, lo] * (1 - w) + x[:, hi] * w
        key = jax.random.key(seed)
        ks = jax.random.split(key, 18)
        s = 0.02
        inp = {'char_emb': jax.random.normal(ks[0], (B, L_CHAR, H), jnp.float32), 'subword_emb': jax.random.normal(ks[1], (B, L_SUB, H), jnp.float32)}
        names = ['Wq_c', 'Wk_s', 'Wv_s', 'Wq_s', 'Wk_c', 'Wv_c']
        for i, n in enumerate(names):
            inp[n] = jax.random.normal(ks[2 + 2 * i], (H, H), jnp.float32) * s
            inp['b' + n[1:]] = jax.random.normal(ks[3 + 2 * i], (H,), jnp.float32) * s
        inp['Wg'] = jax.random.normal(ks[14], (H, 2 * H), jnp.float32) * s
        inp['bg'] = jax.random.normal(ks[15], (H,), jnp.float32) * s
        return inp
    _L0_xattn_all = _L0_xattn_setup()
    _L0_xattn_in = {k: v for k, v in _L0_xattn_all.items() if k in ('Wq_c', 'bq_c', 'Wk_s', 'bk_s', 'Wv_s', 'bv_s', 'Wq_s', 'bq_s', 'Wk_c', 'bk_c', 'Wv_c', 'bv_c', 'Wg', 'bg')}
    del _L0_xattn_all

    def _L0_ffn_setup():
        import jax, jax.numpy as jnp
        import numpy as np
        B, S, D, H, DOUT, E, K = (4, 512, 256, 256, 256, 8, 2)
        key = jax.random.key(seed)
        k1, k2, k3, k4 = jax.random.split(key, 4)
        x = jax.random.normal(k1, (B, S, D), dtype=jnp.float32)
        Wr = jax.random.normal(k2, (D, E), dtype=jnp.float32) * 0.02
        Wi = jax.random.normal(k3, (E, D, H), dtype=jnp.float32) * 0.02
        Wo = jax.random.normal(k4, (E, H, DOUT), dtype=jnp.float32) * 0.02
        return {'x': x, 'Wr': Wr, 'Wi': Wi, 'Wo': Wo}
    _L0_ffn_all = _L0_ffn_setup()
    _L0_ffn_in = {k: v for k, v in _L0_ffn_all.items() if k in ('Wr', 'Wi', 'Wo')}
    del _L0_ffn_all

    def _L1_xattn_setup():
        import jax, jax.numpy as jnp
        import numpy as np
        B, LX, LY, D = (32, 256, 128, 256)
        key = jax.random.key(seed)
        k1, k2, k3, k4 = jax.random.split(key, 4)
        x = jax.random.normal(k1, (B, LX, D), dtype=jnp.float32)
        y = jax.random.normal(k2, (B, LY, D), dtype=jnp.float32)
        y_mask = jnp.zeros((B, LY), dtype=bool)
        W = jax.random.normal(k3, (D, D), dtype=jnp.float32) * (1.0 / np.sqrt(D))
        b = jax.random.normal(k4, (D,), dtype=jnp.float32) * 0.01
        return {'x': x, 'y': y, 'y_mask': y_mask, 'W': W, 'b': b}
    _L1_xattn_all = _L1_xattn_setup()
    _L1_xattn_in = {k: v for k, v in _L1_xattn_all.items() if k in ('W', 'b')}
    del _L1_xattn_all

    def _L1_ffn_setup():
        import jax, jax.numpy as jnp
        import numpy as np
        D_IN, D_HID = (256, 1024)

        def _ternary(key, shape):
            return jax.random.randint(key, shape, -1, 2).astype(jnp.float32)

        def _tlin(x, w, s):
            return jnp.einsum('bsi,oi->bso', x, w) * s
        key = jax.random.key(seed)
        ks = jax.random.split(key, 12)
        inv = lambda fan: 1.0 / np.sqrt(fan).astype(np.float32)
        return {'x': jax.random.normal(ks[0], (4, 512, D_IN), dtype=jnp.float32), 'w1_w': _ternary(ks[1], (D_HID, D_IN)), 'w1_s': jax.random.uniform(ks[2], (D_HID,), dtype=jnp.float32) * inv(D_IN), 'w2_w': _ternary(ks[3], (D_HID, D_IN)), 'w2_s': jax.random.uniform(ks[4], (D_HID,), dtype=jnp.float32) * inv(D_IN), 'h1_w': _ternary(ks[5], (D_HID, D_HID)), 'h1_s': jax.random.uniform(ks[6], (D_HID,), dtype=jnp.float32) * inv(D_HID), 'h2_w': _ternary(ks[7], (D_HID, D_HID)), 'h2_s': jax.random.uniform(ks[8], (D_HID,), dtype=jnp.float32) * inv(D_HID), 'w3_w': _ternary(ks[9], (D_IN, D_HID)), 'w3_s': jax.random.uniform(ks[10], (D_IN,), dtype=jnp.float32) * inv(D_HID)}
    _L1_ffn_all = _L1_ffn_setup()
    _L1_ffn_in = {k: v for k, v in _L1_ffn_all.items() if k in ('w1_w', 'w1_s', 'w2_w', 'w2_s', 'h1_w', 'h1_s', 'h2_w', 'h2_s', 'w3_w', 'w3_s')}
    del _L1_ffn_all
    return {'x': x, 'ctx_1024': ctx_1024, 'mask_BxS2_bf0': mask_BxS2_bf0, 'g_xattn': g_xattn, 'g_ffn': g_ffn, 'L0_xattn_Wq_c': _L0_xattn_in['Wq_c'], 'L0_xattn_bq_c': _L0_xattn_in['bq_c'], 'L0_xattn_Wk_s': _L0_xattn_in['Wk_s'], 'L0_xattn_bk_s': _L0_xattn_in['bk_s'], 'L0_xattn_Wv_s': _L0_xattn_in['Wv_s'], 'L0_xattn_bv_s': _L0_xattn_in['bv_s'], 'L0_xattn_Wq_s': _L0_xattn_in['Wq_s'], 'L0_xattn_bq_s': _L0_xattn_in['bq_s'], 'L0_xattn_Wk_c': _L0_xattn_in['Wk_c'], 'L0_xattn_bk_c': _L0_xattn_in['bk_c'], 'L0_xattn_Wv_c': _L0_xattn_in['Wv_c'], 'L0_xattn_bv_c': _L0_xattn_in['bv_c'], 'L0_xattn_Wg': _L0_xattn_in['Wg'], 'L0_xattn_bg': _L0_xattn_in['bg'], 'L0_ffn_Wr': _L0_ffn_in['Wr'], 'L0_ffn_Wi': _L0_ffn_in['Wi'], 'L0_ffn_Wo': _L0_ffn_in['Wo'], 'L1_xattn_W': _L1_xattn_in['W'], 'L1_xattn_b': _L1_xattn_in['b'], 'L1_ffn_w1_w': _L1_ffn_in['w1_w'], 'L1_ffn_w1_s': _L1_ffn_in['w1_s'], 'L1_ffn_w2_w': _L1_ffn_in['w2_w'], 'L1_ffn_w2_s': _L1_ffn_in['w2_s'], 'L1_ffn_h1_w': _L1_ffn_in['h1_w'], 'L1_ffn_h1_s': _L1_ffn_in['h1_s'], 'L1_ffn_h2_w': _L1_ffn_in['h2_w'], 'L1_ffn_h2_s': _L1_ffn_in['h2_s'], 'L1_ffn_w3_w': _L1_ffn_in['w3_w'], 'L1_ffn_w3_s': _L1_ffn_in['w3_s']}

def reference(x, ctx_1024, mask_BxS2_bf0, g_xattn, g_ffn, L0_xattn_Wq_c, L0_xattn_bq_c, L0_xattn_Wk_s, L0_xattn_bk_s, L0_xattn_Wv_s, L0_xattn_bv_s, L0_xattn_Wq_s, L0_xattn_bq_s, L0_xattn_Wk_c, L0_xattn_bk_c, L0_xattn_Wv_c, L0_xattn_bv_c, L0_xattn_Wg, L0_xattn_bg, L0_ffn_Wr, L0_ffn_Wi, L0_ffn_Wo, L1_xattn_W, L1_xattn_b, L1_ffn_w1_w, L1_ffn_w1_s, L1_ffn_w2_w, L1_ffn_w2_s, L1_ffn_h1_w, L1_ffn_h1_s, L1_ffn_h2_w, L1_ffn_h2_s, L1_ffn_w3_w, L1_ffn_w3_s):
    import jax
    import jax.numpy as jnp

    def _L0_xattn_ref(char_emb, subword_emb, Wq_c, bq_c, Wk_s, bk_s, Wv_s, bv_s, Wq_s, bq_s, Wk_c, bk_c, Wv_c, bv_c, Wg, bg):
        import jax, jax.numpy as jnp
        import numpy as np
        H = 256
        B = 8
        L_CHAR = 512
        L_SUB = 256

        def _linear(x, W, b):
            return jnp.einsum('blh,oh->blo', x, W) + b

        def _interp_linear(x, out_len):
            L_in = x.shape[1]
            pos = (jnp.arange(out_len, dtype=x.dtype) + 0.5) * (L_in / out_len) - 0.5
            pos = jnp.clip(pos, 0.0, L_in - 1)
            lo = jnp.floor(pos).astype(jnp.int32)
            hi = jnp.minimum(lo + 1, L_in - 1)
            w = (pos - lo.astype(x.dtype))[None, :, None]
            return x[:, lo] * (1 - w) + x[:, hi] * w
        h = char_emb.shape[-1]
        scale = 1.0 / jnp.sqrt(jnp.asarray(h, char_emb.dtype))
        Q_char = _linear(char_emb, Wq_c, bq_c)
        K_sub = _linear(subword_emb, Wk_s, bk_s)
        V_sub = _linear(subword_emb, Wv_s, bv_s)
        scores = jnp.einsum('bqh,bkh->bqk', Q_char, K_sub) * scale
        char2sub = jnp.einsum('bqk,bkh->bqh', jax.nn.softmax(scores, axis=-1), V_sub)
        Q_sub = _linear(subword_emb, Wq_s, bq_s)
        K_char = _linear(char_emb, Wk_c, bk_c)
        V_char = _linear(char_emb, Wv_c, bv_c)
        scores2 = jnp.einsum('bqh,bkh->bqk', Q_sub, K_char) * scale
        sub2char = jnp.einsum('bqk,bkh->bqh', jax.nn.softmax(scores2, axis=-1), V_char)
        L_char = char_emb.shape[1]
        if sub2char.shape[1] != L_char:
            sub2char = _interp_linear(sub2char, L_char)
        gate_in = jnp.concatenate([char2sub, sub2char], axis=-1)
        gate = jax.nn.sigmoid(jnp.einsum('blh,oh->blo', gate_in, Wg) + bg)
        return gate * char2sub + (1 - gate) * sub2char

    def _L0_ffn_ref(x, Wr, Wi, Wo):
        import jax, jax.numpy as jnp
        import numpy as np
        B, S, D, H, DOUT, E, K = (4, 512, 256, 256, 256, 8, 2)
        b, s, d = x.shape
        e_cnt, _, h = Wi.shape
        dout = Wo.shape[2]
        xf = x.reshape(-1, d)
        T = xf.shape[0]
        probs = jax.nn.softmax(xf @ Wr, axis=-1)
        topk_p, topk_i = jax.lax.top_k(probs, K)
        mask = topk_i[:, :, None] == jnp.arange(e_cnt)[None, None, :]
        hmix = jnp.zeros((T, K, h), dtype=xf.dtype)
        for e in range(e_cnt):
            he = xf @ Wi[e]
            hmix = hmix + jnp.where(mask[:, :, e][:, :, None], he[:, None, :], 0.0)
        o = jnp.zeros((T, K, dout), dtype=xf.dtype)
        for e in range(e_cnt):
            oe = jnp.einsum('tkh,hd->tkd', hmix, Wo[e])
            o = o + jnp.where(mask[:, :, e][:, :, None], oe, 0.0)
        out = jnp.sum(o * topk_p[:, :, None], axis=1)
        return out.reshape(b, s, dout)

    def _L1_xattn_ref(x, y, y_mask, W, b):
        import jax, jax.numpy as jnp
        import numpy as np
        B, LX, LY, D = (32, 256, 128, 256)
        x_proj = jax.nn.relu(jnp.einsum('bxd,ed->bxe', x, W) + b)
        y_proj = jax.nn.relu(jnp.einsum('byd,ed->bye', y, W) + b)
        scores = jnp.einsum('bxd,byd->bxy', x_proj, y_proj)
        scores = jnp.where(y_mask[:, None, :], -jnp.inf, scores)
        att = jax.nn.softmax(scores, axis=-1)
        return jnp.einsum('bxy,byd->bxd', att, y)

    def _L1_ffn_ref(x, w1_w, w1_s, w2_w, w2_s, h1_w, h1_s, h2_w, h2_s, w3_w, w3_s):
        import jax, jax.numpy as jnp
        import numpy as np
        D_IN, D_HID = (256, 1024)

        def _ternary(key, shape):
            return jax.random.randint(key, shape, -1, 2).astype(jnp.float32)

        def _tlin(x, w, s):
            return jnp.einsum('bsi,oi->bso', x, w) * s
        h = jax.nn.silu(_tlin(x, w1_w, w1_s)) * _tlin(x, w2_w, w2_s)
        h = jax.nn.gelu(_tlin(h, h1_w, h1_s), approximate=False)
        h = jax.nn.gelu(_tlin(h, h2_w, h2_s), approximate=False)
        return _tlin(h, w3_w, w3_s)
    x = x + jnp.tanh(g_xattn[0]) * _L0_xattn_ref(_layernorm(x, axis=-1), ctx_1024, L0_xattn_Wq_c, L0_xattn_bq_c, L0_xattn_Wk_s, L0_xattn_bk_s, L0_xattn_Wv_s, L0_xattn_bv_s, L0_xattn_Wq_s, L0_xattn_bq_s, L0_xattn_Wk_c, L0_xattn_bk_c, L0_xattn_Wv_c, L0_xattn_bv_c, L0_xattn_Wg, L0_xattn_bg)
    x = x + jnp.tanh(g_ffn[0]) * _L0_ffn_ref(_layernorm(x, axis=-1), L0_ffn_Wr, L0_ffn_Wi, L0_ffn_Wo)
    x = x + jnp.tanh(g_xattn[1]) * _L1_xattn_ref(_layernorm(x, axis=-1), ctx_1024, mask_BxS2_bf0, L1_xattn_W, L1_xattn_b)
    x = x + jnp.tanh(g_ffn[1]) * _L1_ffn_ref(_layernorm(x, axis=-1), L1_ffn_w1_w, L1_ffn_w1_s, L1_ffn_w2_w, L1_ffn_w2_s, L1_ffn_h1_w, L1_ffn_h1_s, L1_ffn_h2_w, L1_ffn_h2_s, L1_ffn_w3_w, L1_ffn_w3_s)
    return x

_drawn_inputs = setup_inputs


def setup_inputs(seed=0):
    import zlib

    import numpy as np

    out = dict(_drawn_inputs(seed))
    spreads = {'g_ffn': (-1.0, 0.2)}
    factors = {}
    for name, (base, spread) in spreads.items():
        noise = np.random.default_rng([zlib.crc32(name.encode()), seed]).standard_normal(out[name].shape)
        drawn = base * np.exp(spread * noise) if base else spread * noise
        out[name] = jnp.asarray(drawn.astype(out[name].dtype))
    for name, factor in factors.items():
        out[name] = (out[name] * factor).astype(out[name].dtype)
    return out
```

```python
from contextlib import ExitStack

import numpy as np

import concourse.bass as bass
from concourse import mybir

F32 = mybir.dt.float32
F32R = mybir.dt.float32r
U8 = mybir.dt.uint8
ALU = mybir.AluOpType
ACT = mybir.ActivationFunctionType
X = mybir.AxisListType.X

P = 128
B, S, D, L = 4, 1024, 256, 77
KC = D // P
JT = S // P
NT = B * JT
G = 4
NG = NT // G
GN = G * P
E = 8
HID = 1024
HC = HID // P
BL = B * L
EPS = 1e-5
FAR = -3.0e38
TAKEN = 3.0e38
SCALE = float(D) ** -0.5

COLS = ["bk_s", "bq_s", "bv_s", "bv_c", "bq_c", "bk_c", "b1"]
ROWS = ["bv_s", "bg", "bv_c"]
AW = ["Wk_sT", "Wq_sT", "Wv_sT", "Wq_c", "Wk_c", "Wv_cT", "WgT0", "WgT1", "W1T"]


def program(nc, d):
    ctx = ExitStack()
    with ctx:
        base = -(-nc.sbuf_base // 32) * 32
        room = {"x": (0, 32768), "small": (32768, 40960), "weights": (40960, 131072),
                "work": (131072, 212800)}
        cursor = {k: v[0] for k, v in room.items()}

        def place(region, name, shape, dt=F32, at=None):
            size = int(np.prod(shape[1:])) * (1 if dt == U8 else 4)
            size = -(-size // 32) * 32
            start = cursor[region] if at is None else at
            assert start + size <= room[region][1], (name, start + size)
            cursor[region] = start + size
            return nc.alloc_sbuf_tensor_at(name, shape, dt, offset=base + start)

        def sem(name):
            return ctx.enter_context(nc.semaphore(name))

        x = place("x", "x_residual", [P, NT, D])

        ident = place("small", "identity", [P, P])
        stat = place("small", "ln_stats", [P, JT, 6])
        agg = place("small", "ln_aggregate", [P, JT, 2])
        mv = place("small", "ln_mean_var", [P, NT, 2])
        veps = place("small", "ln_var_eps", [P, NT])
        rstd = place("small", "ln_rstd", [P, NT])
        eps_t = place("small", "eps", [P, JT])
        half_t = place("small", "minus_half", [P, JT])
        graw = place("small", "gates_raw", [P, 4])
        gt = place("small", "gates_tanh", [P, 4])
        gh = place("small", "gates_half", [P, 2])
        cols = place("small", "bias_columns", [P, len(COLS), KC])
        sc1 = place("small", "mlp_scales", [P, 4, HC])
        sc3 = place("small", "mlp_out_scale", [P, D])
        ones = place("small", "ones_row", [1, P])

        wexp_h = place("weights", "expert_high", [P, KC, E * D], F32R)
        wexp_l = place("weights", "expert_low", [P, KC, E * D], F32R)
        wi_at = cursor["weights"]
        wi = place("weights", "expert_in", [P, KC, E, D])
        wo = place("weights", "expert_out", [P, KC, E, D])
        wo_end = cursor["weights"]
        mlp_at = room["weights"][0]
        w1 = place("weights", "mlp_w1", [P, KC, HID], at=mlp_at)
        w2 = place("weights", "mlp_w2", [P, KC, HID])
        h1 = place("weights", "mlp_h1", [P, HC, HID])
        h2 = place("weights", "mlp_h2", [P, HC, HID])
        w3 = place("weights", "mlp_w3", [P, HC, D])

        wk = room["work"][0]
        rows = place("work", "bias_rows", [1, len(ROWS), D])
        aw = place("work", "attention_weights", [P, len(AW), KC, D])
        ctxT = place("work", "context_T", [P, KC, BL])
        ctxr = place("work", "context", [L, B, D])
        maskT = place("work", "mask_T", [L, B], U8)
        maskr = place("work", "mask_row", [1, BL], U8)
        keep = place("work", "keep", [L, B])
        mrow = place("work", "mask_bias_row", [1, BL])
        yk = place("work", "context_kept", [L, B, D + 1])
        VT = place("work", "values_T", [P, KC, BL])
        ypT = place("work", "context_projected_T", [P, KC, BL])
        A1 = place("work", "score_map", [P, KC, BL])
        A2 = place("work", "score_map_back", [P, KC, BL])
        A2b = place("work", "score_map_back_of_batch", [P, KC, L])
        brow = place("work", "score_bias_row", [1, BL])
        c2 = place("work", "score_bias_back", [L, B])
        xn = place("work", "x_normalised", [P, JT, D])
        xnT = place("work", "x_normalised_T", [P, KC, S])
        small_at = cursor["work"]
        cursor["weights"] = wo_end
        KT = place("weights", "keys_T", [P, KC, BL])
        QT = place("weights", "queries_T", [P, KC, BL])
        VV = place("weights", "values_and_gate", [L, B, 2 * D])
        IT = place("weights", "interpolation_T", [L, S])
        mx2 = place("weights", "max_back", [L, 4])
        rs2 = place("weights", "sum_back", [L, 4])
        nm1 = place("weights", "neg_max", [P, JT])
        rs1 = place("weights", "sum_probs", [P, JT])
        ri1 = place("weights", "inv_sum", [P, JT])
        r2n = place("weights", "pooled", [L, D])
        t2T = place("weights", "pooled_T", [P, KC, L])
        sT = place("weights", "sub2char_T", [P, KC, L])
        SX = place("weights", "sub2char_and_gate", [L, 2 * D])
        SM = place("weights", "sub2char_gated", [L, D])
        E1 = place("weights", "probs", [P, JT, L], at=wi_at)
        P2 = place("weights", "probs_back", [L, S])
        P1T = nc.alloc_sbuf_tensor_at("probs_T", [L, S], F32, offset=base + cursor["weights"] - 4 * S)
        P2T = place("weights", "probs_back_T", [P, JT, L])
        th = place("weights", "gate_tanh", [P, 2, D])
        u1 = place("weights", "update", [P, 2, D])
        wr = place("work", "router", [P, KC, E], at=small_at)
        wrh = place("work", "router_high", [P, KC, E], F32R)
        wrl = place("work", "router_low", [P, KC, E], F32R)
        xTh = place("work", "x_T_high", [P, 2, KC, P], F32R)
        xTl = place("work", "x_T_low", [P, 2, KC, P], F32R)
        lg = place("work", "logits", [P, 2, 2 * E])
        top = place("work", "top8", [P, 2, E])
        want = place("work", "to_mark", [P, 2, E])
        marked = place("work", "marked", [P, 2, 2 * E])
        nml = place("work", "neg_max_logit", [P, 2])
        pe_ = place("work", "expert_exp", [P, 2, E])
        sme = place("work", "expert_sum", [P, 2])
        rie = place("work", "expert_inv", [P, 2])
        pm = place("work", "expert_masked", [P, 2, E])
        coef = place("work", "expert_weight", [P, 2, E])
        xpT = place("work", "x_projected_T", [P, 2, KC, GN], at=small_at)
        EC = place("work", "probs_c", [P, 2, G, L])
        PT = place("work", "probs_c_T", [L, 2, GN])
        nmc = place("work", "neg_max_c", [P, 2, G])
        ric = place("work", "inv_sum_c", [P, 2])
        rig = place("work", "inv_sum_gated", [P, 2])
        ha = place("work", "hidden_a", [P, HC, GN], at=wk)
        hb = place("work", "hidden_b", [P, HC, GN])
        xd = place("work", "x_norm_d", [P, G, D])
        xdT = place("work", "x_norm_d_T", [P, KC, GN])
        sil = place("work", "silu", [P, 2, GN])
        ud = place("work", "update_d", [P, 2, D])

        ps = ctx.enter_context(nc.psum_tensor("psum", [P, 8, 512], F32))

        small_in = sem("small_inputs_loaded")
        aw_in = sem("attention_weights_loaded")
        x_in = sem("x_loaded")
        exp_in = sem("expert_weights_loaded")
        mlp_in = [sem(f"mlp_weights_loaded_{k}") for k in range(5)]
        out_done = sem("output_stored")
        gate_ready = sem("gates_ready")
        const_ready = sem("constants_ready")
        dstep = sem("vector_step_done")
        astep = sem("scalar_step_done")
        pstep = sem("pool_step_done")
        proj = sem("projection_in_psum")
        proj_v = sem("projection_saved_by_vector")
        proj_s = sem("projection_saved_by_scalar")
        map_ps = sem("score_maps_in_psum")
        map_v = sem("score_maps_saved")
        val_ps = sem("values_in_psum")
        val_v = sem("values_saved")
        ex_ps = sem("expert_product_in_psum")
        ex_h = sem("expert_high_saved")
        ex_l = sem("expert_low_saved")
        stats = sem("ln_stats_ready")
        inv = sem("ln_rstd_ready")
        xn_r = sem("x_normalised_ready")
        tp = sem("x_transposed_in_psum")
        xT_r = sem("x_transposed_saved")
        xupd = sem("x_updated")
        s2_ps = sem("scores_back_in_psum")
        s2_b = sem("scores_back_bias_ready")
        p2_r = sem("probs_back_ready")
        a2_r = sem("score_map_back_copied")
        s1_ps = sem("scores_in_psum")
        nm_r = sem("neg_max_ready")
        e1_r = sem("probs_ready")
        e1n = sem("probs_normalised")
        p2t_ps = sem("probs_back_T_in_psum")
        p2t_v = sem("probs_back_T_saved")
        r2_ps = sem("pooled_in_psum")
        r2_v = sem("pooled_saved")
        p1t_ps = sem("probs_T_in_psum")
        p1t_v = sem("probs_T_saved")
        t2_ps = sem("pooled_T_in_psum")
        t2_v = sem("pooled_T_saved")
        so_ps = sem("sub2char_in_psum")
        so_v = sem("sub2char_saved")
        st_ps = sem("sub2char_T_in_psum")
        st_v = sem("sub2char_T_saved")
        sg_ps = sem("sub2char_gate_in_psum")
        sg_v = sem("sub2char_gate_saved")
        fin = sem("gated_sum_in_psum")
        th_r = sem("gate_tanh_ready")
        up_r = sem("update_ready")
        xh_r = sem("x_T_high_ready")
        rt_ps = sem("router_logits_in_psum")
        lg_r = sem("router_bias_ready")
        ee_r = sem("router_exp_ready")
        y_ps = sem("expert_outputs_in_psum")
        y_v = sem("expert_outputs_used")
        xp_ps = sem("x_projected_in_psum")
        xp_r = sem("x_projected_saved")
        sc_ps = sem("scores_c_in_psum")
        mc_r = sem("neg_max_c_ready")
        ec_r = sem("probs_c_ready")
        pt_ps = sem("probs_c_T_in_psum")
        pt_r = sem("probs_c_T_saved")
        o_ps = sem("attended_in_psum")
        d1_ps = sem("mlp_first_in_psum")
        sil_r = sem("silu_ready")
        h_r = sem("gated_hidden_ready")
        d2_ps = sem("mlp_hidden_in_psum")
        g_r = sem("gelu_ready")
        d4_ps = sem("mlp_output_in_psum")

        def col(name, m):
            return cols[:, COLS.index(name), m:m + 1]

        def row(name):
            return rows[:, ROWS.index(name), :]

        def wa(name):
            return aw[:, AW.index(name)]

        class Steps:

            def __init__(self, eng, s):
                self.eng, self.s, self.start, self.n = eng, s, 0, 0

            def mark(self, ins):
                ins.then_inc(self.s, 1)
                self.n += 1
                return self.n

            def wait(self, n=None):
                self.eng.wait_ge(self.s, self.start + (self.n if n is None else n))

            def link(self, ins):
                self.mark(ins)
                self.wait()

            def enter(self, i, per):
                self.first = self.start + self.n
                self.start, self.n, self.per = self.first + i * per, 0, per

            def leave(self, passes):
                assert self.n == self.per, (self.n, self.per)
                self.start, self.n = self.first + passes * self.per, 0

        block = ctx.enter_context(nc.Block())

        @block.sync
        def _(sp):
            sp.dma_start(aw[:], d["aw"]).then_inc(aw_in, 16)
            for t, n in ((ctxT, "ctxT"), (ctxr, "ctx"), (cols, "cols"), (rows, "rows"), (ident, "ident"),
                         (maskT, "maskT"), (maskr, "maskr"), (wr, "Wr"), (sc1, "scales")):
                sp.dma_start(t[:], d[n]).then_inc(small_in, 16)
            sp.dma_start(graw[:], d["gates"].partition_broadcast(P)).then_inc(small_in, 16)
            sp.dma_start(sc3[:], d["w3_s"].partition_broadcast(P)).then_inc(small_in, 16)
            for b in range(B):
                sp.dma_start(x[:, b * JT:(b + 1) * JT, :], d["x"][b].rearrange("(p j) c -> p j c", p=P)
                             ).then_inc(x_in, 16)
            sp.dma_start(IT[:], d["interp"]).then_inc(aw_in, 16)
            sp.dma_start(wi[:], d["Wi"]).then_inc(exp_in, 16)
            sp.dma_start(wo[:], d["Wo"]).then_inc(exp_in, 16)
            sp.wait_ge(y_ps, 4 * NT)
            for k, (t, n) in enumerate(((w1, "w1"), (w2, "w2"), (h1, "h1"), (h2, "h2"), (w3, "w3"))):
                sp.dma_start(t[:], d[n]).then_inc(mlp_in[k], 16)
            with sp.Fori(0, NG) as n:
                sp.wait_ge(xupd, XUPD_C + G + n * G)
                src = x[:, bass.ds(n * G, G), :]
                dst = d["out"][bass.ds(n, 1)].rearrange("o p j c -> p (o j) c")
                sp.dma_start(dst, src).then_inc(out_done, 16)
            sp.wait_ge(out_done, 16 * NG)

        N_SMALL = 11 * 16

        @block.tensor
        def _(pe):
            mm = pe.matmul

            def transposes(src, t0, slot):
                for k in range(KC):
                    last = pe.transpose(ps[:, slot, k * P:(k + 1) * P], src[:, k * P:(k + 1) * P], ident[:])
                last.then_inc(tp, 1)

            pe.wait_ge(aw_in, 32)
            pe.wait_ge(small_in, N_SMALL)
            for n, w in enumerate(("Wk_sT", "Wq_sT", "Wv_sT", "W1T")):
                for m in range(KC):
                    for k in range(KC):
                        last = mm(ps[:, 2 * n + m, 0:BL], wa(w)[:, k, m * P:(m + 1) * P], ctxT[:, k, :],
                                  start=(k == 0), stop=(k == KC - 1))
                    last.then_inc(proj, 1)
            pe.wait_ge(proj_v, 4)
            for n, (w, src) in enumerate((("Wq_c", KT), ("Wk_c", QT))):
                for m in range(KC):
                    for k in range(KC):
                        last = mm(ps[:, 2 * n + m, 0:BL], wa(w)[:, k, m * P:(m + 1) * P], src[:, k, :],
                                  start=(k == 0), stop=(k == KC - 1))
                    last.then_inc(map_ps, 1)
            pe.wait_ge(proj_v, 6)
            for k in range(KC):
                last = mm(ps[0:1, 4, 0:BL], col("bq_c", k), KT[:, k, :], start=(k == 0), stop=(k == KC - 1))
            last.then_inc(map_ps, 1)
            for b in range(B):
                for k in range(KC):
                    last = mm(ps[0:L, 5, b:b + 1], QT[:, k, b * L:(b + 1) * L], col("bk_c", k),
                              start=(k == 0), stop=(k == KC - 1))
            last.then_inc(map_ps, 1)
            pe.wait_ge(proj_s, 2)
            pe.wait_ge(const_ready, 1)
            for b in range(B):
                if b >= 2:
                    pe.wait_ge(val_v, 2 * (b - 1))
                bank = 6 + b % 2
                for half, (src, w, bias) in enumerate(((ctxT, "Wv_sT", "bv_s"), (VT, "WgT0", "bg"))):
                    o = ps[0:L, bank, half * D:(half + 1) * D]
                    for k in range(KC):
                        mm(o, src[:, k, b * L:(b + 1) * L], wa(w)[:, k, :], start=(k == 0), stop=False)
                    last = mm(o, ones[0:1, 0:L], row(bias), start=False, stop=True)
                last.then_inc(val_ps, 1)
            pe.wait_ge(exp_in, 32)
            pe.wait_ge(map_v, 6)
            for e in range(E):
                if e >= 4:
                    pe.wait_ge(ex_l, e - 3)
                for m in range(KC):
                    for k in range(KC):
                        last = mm(ps[:, e % 4, m * D:(m + 1) * D], wi[:, k, e, m * P:(m + 1) * P], wo[:, k, e, :],
                                  start=(k == 0), stop=(k == KC - 1))
                last.then_inc(ex_ps, 1)
            pe.wait_ge(ex_l, E)
            pe.wait_ge(val_v, 2 * B)

            with pe.Fori(0, B) as b:
                for j in range(JT):
                    pe.wait_ge(xn_r, b * JT + (j + 1))
                    if j >= 2:
                        pe.wait_ge(xT_r, b * JT + (j - 1))
                    transposes(xn[:, j, :], None, j % 2)
                pe.wait_ge(xT_r, (b + 1) * JT)
                pe.wait_ge(a2_r, b + 1)
                for h in range(2):
                    for k in range(KC):
                        last = mm(ps[0:L, 2 + h, :], A2b[:, k, :], xnT[:, k, h * 512:(h + 1) * 512],
                                  start=(k == 0), stop=(k == KC - 1))
                last.then_inc(s2_ps, 1)
                for j in range(JT):
                    o = ps[:, 4 + j // G, (j % G) * P:(j % G) * P + L]
                    for k in range(KC):
                        mm(o, xnT[:, k, j * P:(j + 1) * P], A1[:, k, bass.ds(b * L, L)], start=(k == 0), stop=False)
                    last = mm(o, ones[:], brow[0:1, bass.ds(b * L, L)], start=False, stop=True)
                    if j % G == G - 1:
                        last.then_inc(s1_ps, 1)
                pe.wait_ge(p2_r, 2 * b + 2)
                for j in range(JT):
                    last = pe.transpose(ps[:, 6 + j // G, (j % G) * L:(j % G + 1) * L],
                                        P2[:, j * P:(j + 1) * P], ident[0:L, 0:L])
                    if j % G == G - 1:
                        last.then_inc(p2t_ps, 1)
                pe.wait_ge(p2t_v, 2 * b + 2)
                for j in range(JT):
                    last = mm(ps[0:L, 6, 0:D], P2T[:, j, :], xn[:, j, :], start=(j == 0), stop=(j == JT - 1))
                last.then_inc(r2_ps, 1)
                for q in range(2):
                    pe.wait_ge(e1n, b * JT + (q + 1) * G)
                    for j in range(G):
                        last = pe.transpose(ps[0:L, 4 + q, j * P:(j + 1) * P], E1[:, q * G + j, :], ident[:])
                    last.then_inc(p1t_ps, 1)
                pe.wait_ge(r2_v, b + 1)
                for k in range(KC):
                    last = pe.transpose(ps[:, 7, k * L:(k + 1) * L], r2n[:, k * P:(k + 1) * P], ident[0:L, 0:L])
                last.then_inc(t2_ps, 1)
                pe.wait_ge(t2_v, b + 1)
                for k in range(KC):
                    mm(ps[0:L, 6, 0:D], t2T[:, k, :], wa("Wv_cT")[:, k, :], start=(k == 0), stop=False)
                mm(ps[0:L, 6, 0:D], ones[0:1, 0:L], row("bv_c"), start=False, stop=True).then_inc(so_ps, 1)
                for m in range(KC):
                    for k in range(KC):
                        last = mm(ps[:, 7, m * L:(m + 1) * L], wa("Wv_cT")[:, k, m * P:(m + 1) * P], t2T[:, k, :],
                                  start=(k == 0), stop=(k == KC - 1))
                last.then_inc(st_ps, 1)
                pe.wait_ge(st_v, 2 * b + 2)
                for m in range(KC):
                    last = mm(ps[0:L, 7, 0:D], sT[:, m, :], wa("WgT1")[:, m, :], start=(m == 0), stop=(m == KC - 1))
                last.then_inc(sg_ps, 1)
                pe.wait_ge(p1t_v, 2 * b + 2)
                pe.wait_ge(so_v, 2 * b + 2)
                pe.wait_ge(sg_v, b + 1)
                for j in range(JT):
                    if j >= 2:
                        pe.wait_ge(up_r, b * JT + (j - 1))
                    t = slice(j * P, (j + 1) * P)
                    mm(ps[:, j % 2, :], P1T[:, t], VV[:, bass.ds(b, 1), :].rearrange("p o c -> p (o c)"),
                       start=True, stop=False)
                    mm(ps[:, j % 2, :], IT[:, t], SX[:], start=False, stop=True)
                    mm(ps[:, 2 + j % 2, 0:D], IT[:, t], SM[:], start=True, stop=True).then_inc(fin, 1)
                pe.wait_ge(up_r, (b + 1) * JT)

            def b_transpose(t, s):
                pe.wait_ge(xn_r, NT + 1 + t)
                pe.wait_ge(xT_r, NT - 1 + t)
                transposes(xn[:, s, :], None, s)

            def b_route(t, s):
                pe.wait_ge(xT_r, NT + 1 + t)
                pe.wait_ge(lg_r, t) if not isinstance(t, int) or t > 0 else None
                n = 0
                for k in range(KC):
                    for a, c in ((xTh, wrh), (xTl, wrh), (xTh, wrl)):
                        last = mm(ps[:, 2, 0:E], a[:, s, k, :], c[:, k, :], start=(n == 0), stop=(n == 3 * KC - 1))
                        n += 1
                last.then_inc(rt_ps, 1)

            def b_experts(t, s, pair):
                if not isinstance(t, int) or t > 0:
                    pe.wait_ge(y_v, 4 * t - 3 + pair)
                n = 0
                for k in range(KC):
                    for a, c in ((xTh, wexp_h), (xTh, wexp_l), (xTl, wexp_h)):
                        last = mm(ps[:, 4 + pair, :], a[:, s, k, :], c[:, k, pair * 2 * D:(pair + 1) * 2 * D],
                                  start=(n == 0), stop=(n == 3 * KC - 1))
                        n += 1
                last.then_inc(y_ps, 1)

            def b_tile(t, s, ahead):
                if ahead:
                    b_transpose(t + 1, 1 - s)
                b_experts(t, s, 0)
                b_experts(t, s, 1)
                if ahead:
                    b_route(t + 1, 1 - s)
                b_experts(t, s, 2)
                b_experts(t, s, 3)

            b_transpose(0, 0)
            b_route(0, 0)
            b_tile(0, 0, True)
            with pe.Fori(0, NT // 2 - 1) as i:
                b_tile(2 * i + 1, 1, True)
                b_tile(2 * i + 2, 0, True)
            b_tile(NT - 1, 1, False)

            def c_project(g, s):
                for j in range(G):
                    pe.wait_ge(xn_r, 2 * NT + 1 + j + G * g)
                    pe.wait_ge(xT_r, 2 * NT - 1 + j + G * g)
                    transposes(xn[:, s * G + j, :], None, j % 2)
                pe.wait_ge(xT_r, 2 * NT + G + G * g)
                for m in range(KC):
                    if not isinstance(g, int) or g > 0:
                        pe.wait_ge(xp_r, 2 * g - 1 + m)
                    for k in range(KC):
                        last = mm(ps[:, 2 + m, :], wa("W1T")[:, k, m * P:(m + 1) * P],
                                  xnT[:, k, s * GN:(s + 1) * GN], start=(k == 0), stop=(k == KC - 1))
                    last.then_inc(xp_ps, 1)

            def c_scores(g, s, b):
                pe.wait_ge(xp_r, 2 * g + 2)
                if not isinstance(g, int) or g > 0:
                    pe.wait_ge(ec_r, G * g)
                for j in range(G):
                    o = ps[:, 4, j * P:j * P + L]
                    for k in range(KC):
                        mm(o, xpT[:, s, k, j * P:(j + 1) * P], ypT[:, k, bass.ds(b * L, L)],
                           start=(k == 0), stop=False)
                    last = mm(o, ones[:], mrow[0:1, bass.ds(b * L, L)], start=False, stop=True)
                last.then_inc(sc_ps, 1)

            def c_attend(g, s, b):
                pe.wait_ge(ec_r, G * g + G)
                if not isinstance(g, int) or g > 0:
                    pe.wait_ge(pt_r, g)
                for j in range(G):
                    last = pe.transpose(ps[0:L, 5, j * P:(j + 1) * P], EC[:, s, j, :], ident[:])
                last.then_inc(pt_ps, 1)
                pe.wait_ge(pt_r, g + 1)
                for j in range(G):
                    pe.wait_ge(xupd, XUPD_A - 1 + G * g + j)
                    mm(ps[:, 6 + j % 2, 0:D + 1], PT[:, s, j * P:(j + 1) * P],
                       yk[:, bass.ds(b, 1), :].rearrange("p o c -> p (o c)"), start=True, stop=True).then_inc(o_ps, 1)

            def c_group(g, s, b, b_next):
                if b_next is not None:
                    c_project(g + 1, 1 - s)
                c_attend(g, s, b)
                if b_next is not None:
                    c_scores(g + 1, 1 - s, b_next)

            c_project(0, 0)
            c_scores(0, 0, 0)
            c_group(0, 0, 0, 0)
            with pe.Fori(0, B - 1) as b:
                c_group(2 * b + 1, 1, b, b + 1)
                c_group(2 * b + 2, 0, b + 1, b + 1)
            c_group(NG - 1, 1, B - 1, None)

            def d_transpose(n):
                for j in range(G):
                    pe.wait_ge(xn_r, 3 * NT + 1 + j + G * n)
                    pe.wait_ge(xT_r, 3 * NT - 1 + j + G * n)
                    transposes(xd[:, j, :], None, j % 2)

            def d_group(n, ahead):
                pe.wait_ge(xT_r, 3 * NT + G + G * n)
                for c in range(HC):
                    a = 2 + 2 * (c % 2)
                    if c >= 2:
                        pe.wait_ge(h_r, HC * n + c - 1)
                    for w, bank in ((w1, a), (w2, a + 1)):
                        for k in range(KC):
                            last = mm(ps[:, bank, :], w[:, k, c * P:(c + 1) * P], xdT[:, k, :],
                                      start=(k == 0), stop=(k == KC - 1))
                    last.then_inc(d1_ps, 1)
                for layer, (w, src) in enumerate(((h1, ha), (h2, hb))):
                    for c in range(HC):
                        q = 2 * HC * n + HC * layer + c
                        if layer or c >= 2:
                            pe.wait_ge(g_r, q - 1)
                        for k in range(HC):
                            if c == 0:
                                pe.wait_ge(*((g_r, 2 * HC * n + k + 1) if layer else (h_r, HC * n + k + 1)))
                            last = mm(ps[:, 6 + c % 2, :], w[:, k, c * P:(c + 1) * P], src[:, k, :],
                                      start=(k == 0), stop=(k == HC - 1))
                        last.then_inc(d2_ps, 1)
                if ahead:
                    d_transpose(n + 1)
                pe.wait_ge(g_r, 2 * HC * n + 2 * HC)
                if ahead:
                    pe.wait_ge(xT_r, 3 * NT + 2 * G + G * n)
                for j in range(G):
                    if j >= 2:
                        pe.wait_ge(up_r, NT + G * n + j - 1)
                    for k in range(HC):
                        last = mm(ps[:, j % 2, 0:D], ha[:, k, j * P:(j + 1) * P], w3[:, k, :],
                                  start=(k == 0), stop=(k == HC - 1))
                    last.then_inc(d4_ps, 1)
                pe.wait_ge(up_r, NT + G * n + G)

            for k in range(5):
                pe.wait_ge(mlp_in[k], 16)
            d_transpose(0)
            with pe.Fori(0, NG - 1) as n:
                d_group(n, True)
            d_group(NG - 1, False)

        @block.scalar
        def _(act):
            act.wait_ge(small_in, N_SMALL)
            act.activation(gt[:], graw[:], ACT.Tanh).then_inc(gate_ready, 1)
            for m in range(KC):
                act.wait_ge(proj, 7 + m)
                act.activation(ypT[:, m, :], ps[:, 6 + m, 0:BL], ACT.Relu, bias=col("b1", m)).then_inc(proj_s, 1)
            for e in range(E):
                act.wait_ge(ex_ps, e + 1)
                act.activation(wexp_h[:, :, e * D:(e + 1) * D],
                               ps[:, e % 4, :].rearrange("p (m c) -> p m c", m=KC), ACT.Copy).then_inc(ex_h, 1)
            with act.Fori(0, B) as b:
                for j in range(JT):
                    act.wait_ge(tp, b * JT + (j + 1))
                    act.activation(xnT[:, :, j * P:(j + 1) * P],
                                   ps[:, j % 2, 0:D].rearrange("p (k c) -> p k c", k=KC), ACT.Copy).then_inc(xT_r, 1)
                act.wait_ge(s2_b, b + 1)
                for h in range(2):
                    act.activation(P2[:, h * 512:(h + 1) * 512], ps[0:L, 2 + h, :], ACT.Exp, bias=mx2[:, 2:3],
                                   scale=1.0, accum_out=rs2[:, h:h + 1]).then_inc(p2_r, 1)
                for j in range(JT):
                    act.wait_ge(nm_r, 2 * b + (j // G + 1))
                    act.activation(E1[:, j, :], ps[:, 4 + j // G, (j % G) * P:(j % G) * P + L], ACT.Exp,
                                   bias=nm1[:, j:j + 1], scale=1.0, accum_out=rs1[:, j:j + 1]).then_inc(e1_r, 1)
                act.wait_ge(p2t_ps, 2 * b + 2)
                for q in range(2):
                    act.wait_ge(p1t_ps, 2 * b + (q + 1))
                    act.activation(P1T[:, q * GN:(q + 1) * GN], ps[0:L, 4 + q, :], ACT.Copy).then_inc(p1t_v, 1)
                for j in range(JT):
                    act.wait_ge(fin, b * JT + (j + 1))
                    if j >= 2:
                        act.wait_ge(up_r, b * JT + (j - 1))
                    act.activation(th[:, j % 2, :], ps[:, j % 2, D:2 * D], ACT.Tanh, scale=0.5).then_inc(th_r, 1)

            def b_high(t, s):
                act.wait_ge(tp, NT + 1 + t)
                act.activation(xTh[:, s], ps[:, s, 0:D].rearrange("p (k c) -> p k c", k=KC), ACT.Copy
                               ).then_inc(xh_r, 1)

            def b_exp(t, s):
                act.wait_ge(lg_r, t + 1)
                act.activation(pe_[:, s, :], lg[:, s, 0:E], ACT.Exp, bias=nml[:, s:s + 1], scale=1.0,
                               accum_out=sme[:, s:s + 1]).then_inc(ee_r, 1)

            b_high(0, 0)
            b_exp(0, 0)
            b_high(1, 1)
            b_exp(1, 1)
            with act.Fori(0, NT // 2 - 1) as i:
                for s in range(2):
                    b_high(2 * i + 2 + s, s)
                    b_exp(2 * i + 2 + s, s)

            def c_save(g, s):
                for j in range(G):
                    act.wait_ge(tp, 2 * NT + 1 + G * g + j)
                    act.activation(xnT[:, :, s * GN + j * P:s * GN + (j + 1) * P],
                                   ps[:, j % 2, 0:D].rearrange("p (k c) -> p k c", k=KC), ACT.Copy).then_inc(xT_r, 1)
                for m in range(KC):
                    act.wait_ge(xp_ps, 2 * g + m + 1)
                    act.activation(xpT[:, s, m, :], ps[:, 2 + m, :], ACT.Relu, bias=col("b1", m)).then_inc(xp_r, 1)

            def c_exp(g, s):
                act.wait_ge(mc_r, g + 1)
                for j in range(G):
                    act.activation(EC[:, s, j, :], ps[:, 4, j * P:j * P + L], ACT.Exp, bias=nmc[:, s, j:j + 1],
                                   scale=1.0).then_inc(ec_r, 1)

            with act.Fori(0, B) as b:
                for s in range(2):
                    c_save(2 * b + s, s)
                    c_exp(2 * b + s, s)

            def d_save(n):
                for j in range(G):
                    act.wait_ge(tp, 3 * NT + 1 + G * n + j)
                    act.activation(xdT[:, :, j * P:(j + 1) * P],
                                   ps[:, j % 2, 0:D].rearrange("p (k c) -> p k c", k=KC), ACT.Copy).then_inc(xT_r, 1)

            def d_group(n, ahead):
                for c in range(HC):
                    act.wait_ge(d1_ps, HC * n + c + 1)
                    if c >= 2:
                        act.wait_ge(h_r, HC * n + c - 1)
                    act.activation(sil[:, c % 2, :], ps[:, 2 + 2 * (c % 2), :], ACT.Silu,
                                   scale=sc1[:, 0, c:c + 1]).then_inc(sil_r, 1)
                for layer, dst in enumerate((hb, ha)):
                    for c in range(HC):
                        act.wait_ge(d2_ps, 2 * HC * n + HC * layer + c + 1)
                        act.activation(dst[:, c, :], ps[:, 6 + c % 2, :], ACT.Gelu,
                                       scale=sc1[:, 2 + layer, c:c + 1]).then_inc(g_r, 1)
                if ahead:
                    d_save(n + 1)

            d_save(0)
            with act.Fori(0, NG - 1) as n:
                d_group(n, True)
            d_group(NG - 1, False)

        @block.vector
        def _(dve):
            st = Steps(dve, dstep)

            def wait_alone(s, value):
                if not isinstance(value, int):
                    dve.compute_val(value)
                dve.wait_ge(const_ready, 3)
                dve.wait_ge(s, value)

            def steps_alone():
                wait_alone(st.s, st.start + st.n)

            def measure(tile, k):
                st.mark(dve.bn_stats(stat[:, k, :], x[:, bass.ds(tile, 1), :].rearrange("p o c -> p (o c)")))

            def aggregate(t0, n, k):
                steps_alone()
                for j in range(n):
                    st.mark(dve.bn_aggr(agg[:, k + j, :], stat[:, k + j, :]))
                steps_alone()
                dve.tensor_copy(mv[:, bass.ds(t0, n), :], agg[:, k:k + n, :]).then_inc(stats, 1)

            def normalise(tile, dst):
                dve.tensor_scalar(dst, x[:, bass.ds(tile, 1), :].rearrange("p o c -> p (o c)"),
                                  mv[:, bass.ds(tile, 1), 0:1].rearrange("p o c -> p (o c)"),
                                  rstd[:, bass.ds(tile, 1)], ALU.subtract, ALU.mult).then_inc(xn_r, 1)

            dve.memset(ones[:], 1.0).then_inc(const_ready, 1)
            dve.memset(eps_t[:], EPS).then_inc(const_ready, 1)
            dve.memset(half_t[:], -0.5).then_inc(const_ready, 1)
            dve.wait_ge(small_in, N_SMALL)
            dve.wait_ge(gate_ready, 1)
            st.link(dve.tensor_scalar(gh[:, 0:1], gt[:, 0:1], 0.5, None, ALU.mult))
            st.link(dve.tensor_scalar(gh[:, 1:2], gt[:, 0:1], -0.5, None, ALU.mult))
            st.link(dve.tensor_scalar(sc3[:], sc3[:], gt[:, 3:4], None, ALU.mult))
            st.link(dve.tensor_scalar(keep[:], maskT[:], -1.0, 1.0, ALU.mult, ALU.add))
            st.mark(dve.tensor_scalar(mrow[:], maskr[:], FAR, None, ALU.mult))
            for b in range(B):
                st.mark(dve.tensor_scalar(yk[:, b, 0:D], ctxr[:, b, :], keep[:, b:b + 1], None, ALU.mult))
                st.mark(dve.tensor_copy(yk[:, b, D:D + 1], keep[:, b:b + 1]))
            for n, (dst, bias) in enumerate(((KT, "bk_s"), (QT, "bq_s"), (VT, "bv_s"))):
                for m in range(KC):
                    dve.wait_ge(proj, 2 * n + m + 1)
                    dve.tensor_scalar(dst[:, m, :], ps[:, 2 * n + m, 0:BL], col(bias, m), None, ALU.add
                                      ).then_inc(proj_v, 1)
            for n, dst in enumerate((A1, A2)):
                for m in range(KC):
                    dve.wait_ge(map_ps, 2 * n + m + 1)
                    dve.tensor_scalar(dst[:, m, :], ps[:, 2 * n + m, 0:BL], SCALE, None, ALU.mult).then_inc(map_v, 1)
            dve.wait_ge(map_ps, 5)
            dve.tensor_scalar(brow[:], ps[0:1, 4, 0:BL], SCALE, None, ALU.mult).then_inc(map_v, 1)
            dve.wait_ge(map_ps, 6)
            dve.tensor_scalar(c2[:], ps[0:L, 5, 0:B], SCALE, None, ALU.mult).then_inc(map_v, 1)
            for b in range(B):
                dve.wait_ge(val_ps, b + 1)
                dve.tensor_scalar(VV[:, b, 0:D], ps[0:L, 6 + b % 2, 0:D], gh[0:L, 0:1], None, ALU.mult
                                  ).then_inc(val_v, 1)
                dve.tensor_copy(VV[:, b, D:2 * D], ps[0:L, 6 + b % 2, D:2 * D]).then_inc(val_v, 1)
            dve.wait_ge(x_in, 64)
            for j in range(JT):
                measure(j, j)
            aggregate(0, JT, 0)
            for e in range(E):
                dve.wait_ge(ex_h, e + 1)
                dve.tensor_tensor(wexp_l[:, :, e * D:(e + 1) * D],
                                  ps[:, e % 4, :].rearrange("p (m c) -> p m c", m=KC),
                                  wexp_h[:, :, e * D:(e + 1) * D].bitcast(F32), ALU.subtract).then_inc(ex_l, 1)

            def a_batch(b, ahead):
                dve.wait_ge(map_v, 6)
                dve.tensor_copy(A2b[:], A2[:, :, bass.ds(b * L, L)]).then_inc(a2_r, 1)
                dve.wait_ge(inv, 3 * b + 1)
                for j in range(JT):
                    normalise(b * JT + j, xn[:, j, :])
                dve.wait_ge(s2_ps, b + 1)
                st.link(dve.tensor_reduce(mx2[:, 0:1], ps[0:L, 2:4, :], mybir.AxisListType.XY, ALU.max))
                st.link(dve.tensor_scalar(mx2[:, 1:2], mx2[:, 0:1], c2[:, bass.ds(b, 1)], None, ALU.add))
                dve.tensor_tensor(mx2[:, 2:3], c2[:, bass.ds(b, 1)], mx2[:, 1:2], ALU.subtract).then_inc(s2_b, 1)
                for q in range(2):
                    dve.wait_ge(s1_ps, 2 * b + (q + 1))
                    dve.tensor_reduce(nm1[:, q * G:(q + 1) * G],
                                      ps[:, 4 + q, :].rearrange("p (j c) -> p j c", j=G)[:, :, 0:L], X, ALU.max,
                                      negate=True).then_inc(nm_r, 1)
                for q in range(2):
                    dve.wait_ge(p2t_ps, 2 * b + (q + 1))
                    dve.tensor_copy(P2T[:, q * G:(q + 1) * G, :],
                                    ps[:, 6 + q, 0:G * L].rearrange("p (j c) -> p j c", j=G)).then_inc(p2t_v, 1)
                dve.wait_ge(p2_r, 2 * b + 2)
                st.link(dve.tensor_tensor(rs2[:, 2:3], rs2[:, 0:1], rs2[:, 1:2], ALU.add))
                st.link(dve.reciprocal(rs2[:, 3:4], rs2[:, 2:3]))
                for q in range(2):
                    dve.wait_ge(e1_r, b * JT + (q + 1) * G)
                    st.link(dve.reciprocal(ri1[:, q * G:(q + 1) * G], rs1[:, q * G:(q + 1) * G]))
                    for j in range(q * G, (q + 1) * G):
                        dve.tensor_scalar(E1[:, j, :], E1[:, j, :], ri1[:, j:j + 1], None, ALU.mult).then_inc(e1n, 1)
                dve.wait_ge(r2_ps, b + 1)
                dve.tensor_scalar(r2n[:], ps[0:L, 6, 0:D], rs2[:, 3:4], None, ALU.mult).then_inc(r2_v, 1)
                dve.wait_ge(t2_ps, b + 1)
                dve.tensor_copy(t2T[:], ps[:, 7, 0:KC * L].rearrange("p (k c) -> p k c", k=KC)).then_inc(t2_v, 1)
                dve.wait_ge(st_ps, b + 1)
                for m in range(KC):
                    dve.tensor_scalar(sT[:, m, :], ps[:, 7, m * L:(m + 1) * L], col("bv_c", m), None, ALU.add
                                      ).then_inc(st_v, 1)
                dve.wait_ge(so_ps, b + 1)
                dve.tensor_scalar(SX[:, 0:D], ps[0:L, 6, 0:D], gh[0:L, 1:2], None, ALU.mult).then_inc(so_v, 1)
                dve.tensor_scalar(SM[:], ps[0:L, 6, 0:D], gt[0:L, 0:1], None, ALU.mult).then_inc(so_v, 1)
                dve.wait_ge(sg_ps, b + 1)
                dve.tensor_copy(SX[:, D:2 * D], ps[0:L, 7, 0:D]).then_inc(sg_v, 1)
                if ahead:
                    for j in range(JT):
                        measure(b * JT + (JT + j), j)
                    aggregate(b * JT + JT, JT, 0)
                for j in range(JT):
                    dve.wait_ge(th_r, b * JT + (j + 1))
                    if j >= 2:
                        wait_alone(xupd, b * JT + (j - 1))
                    st.link(dve.scalar_tensor_tensor(u1[:, j % 2, :], th[:, j % 2, :], 1.0, ps[:, j % 2, 0:D],
                                                     ALU.add, ALU.mult))
                    dve.tensor_tensor(u1[:, j % 2, :], u1[:, j % 2, :], ps[:, 2 + j % 2, 0:D], ALU.add
                                      ).then_inc(up_r, 1)
                    if j >= 2:
                        measure(b * JT + (j - 2), j - 2)
                    if j == G + 1:
                        aggregate(b * JT, G, 0)
                for j in range(JT - 2, JT):
                    wait_alone(xupd, b * JT + (j + 1))
                    measure(b * JT + j, j)
                aggregate(b * JT + G, G, G)

            per = 2 + 2 + 2 + 2 * JT + JT + 2 * JT
            with dve.Fori(0, B - 1) as b:
                st.enter(b, per)
                a_batch(b, True)
            st.leave(B - 1)
            a_batch(B - 1, False)

            st.link(dve.tensor_copy(wrh[:], wr[:]))
            st.link(dve.tensor_tensor(wrl[:], wr[:], wrh[:].bitcast(F32), ALU.subtract))
            for s in range(2):
                st.link(dve.memset(lg[:, s, E:2 * E], FAR))
                st.link(dve.memset(want[:, s, :], FAR))

            def b_norm(t, s):
                dve.wait_ge(tp, NT - 1 + t)
                normalise(t, xn[:, s, :])

            def b_low(t, s):
                dve.wait_ge(xh_r, t + 1)
                dve.tensor_tensor(xTl[:, s], ps[:, s, 0:D].rearrange("p (k c) -> p k c", k=KC),
                                  xTh[:, s].bitcast(F32), ALU.subtract).then_inc(xT_r, 1)

            def b_route(t, s):
                dve.wait_ge(rt_ps, t + 1)
                st.mark(dve.tensor_copy(lg[:, s, 0:E], ps[:, 2, 0:E]))
                steps_alone()
                st.link(dve.max(top[:, s, :], lg[:, s, 0:E]))
                dve.tensor_scalar(nml[:, s:s + 1], top[:, s, 0:1], -1.0, None, ALU.mult).then_inc(lg_r, 1)
                st.mark(dve.tensor_copy(want[:, s, 0:2], top[:, s, 0:2]))
                steps_alone()
                st.link(dve.match_replace(marked[:, s, :], want[:, s, :], lg[:, s, :], TAKEN))
                dve.wait_ge(ee_r, t + 1)
                st.mark(dve.scalar_tensor_tensor(pm[:, s, :], marked[:, s, 0:E], TAKEN, pe_[:, s, :],
                                                 ALU.is_ge, ALU.mult))
                st.link(dve.reciprocal(rie[:, s:s + 1], sme[:, s:s + 1]))
                st.link(dve.tensor_scalar(coef[:, s, :], pm[:, s, :], rie[:, s:s + 1], gt[:, 2:3], ALU.mult, ALU.mult))

            def b_add(t, s, pair):
                dve.wait_ge(y_ps, 4 * t + pair + 1)
                xt = x[:, bass.ds(t, 1), :].rearrange("p o c -> p (o c)")
                for h in range(2):
                    e = 2 * pair + h
                    ins = dve.scalar_tensor_tensor(xt, ps[:, 4 + pair, h * D:(h + 1) * D], coef[:, s, e:e + 1], xt,
                                                   ALU.mult, ALU.add)
                    if h == 0:
                        st.link(ins)
                    else:
                        ins.then_inc(y_v, 1)
                        wait_alone(y_v, 4 * t + pair + 1)

            def b_tile(t, s, ahead):
                if ahead > 1:
                    b_norm(t + 2, s)
                if ahead:
                    b_low(t + 1, 1 - s)
                b_add(t, s, 0)
                b_add(t, s, 1)
                if ahead:
                    b_route(t + 1, 1 - s)
                b_add(t, s, 2)
                b_add(t, s, 3)
                measure(t, s)
                if s:
                    aggregate(t - 1, 2, 0)

            dve.wait_ge(inv, INV_A)
            normalise(0, xn[:, 0, :])
            normalise(1, xn[:, 1, :])
            b_low(0, 0)
            b_route(0, 0)
            with dve.Fori(0, NT // 2 - 1) as i:
                st.enter(i, 2 * (7 + 4 + 2))
                b_tile(2 * i, 0, 2)
                b_tile(2 * i + 1, 1, 2)
            st.leave(NT // 2 - 1)
            b_tile(NT - 2, 0, 1)
            b_tile(NT - 1, 1, 0)

            def c_norm(g, s, n_inv):
                dve.wait_ge(inv, n_inv)
                for j in range(G):
                    normalise(G * g + j, xn[:, s * G + j, :])

            def c_max(g, s):
                dve.wait_ge(sc_ps, g + 1)
                dve.tensor_reduce(nmc[:, s, :], ps[:, 4, :].rearrange("p (j c) -> p j c", j=G)[:, :, 0:L], X, ALU.max,
                                  negate=True).then_inc(mc_r, 1)

            def c_group(g, s, ahead):
                if ahead:
                    c_norm(g + 1, 1 - s, INV_B)
                dve.wait_ge(pt_ps, g + 1)
                dve.tensor_copy(PT[:, s, :], ps[0:L, 5, :]).then_inc(pt_r, 1)
                for j in range(G):
                    t = G * g + j
                    q = j % 2
                    dve.wait_ge(o_ps, t + 1)
                    st.link(dve.reciprocal(ric[:, q:q + 1], ps[:, 6 + q, D:D + 1]))
                    st.link(dve.tensor_scalar(rig[:, q:q + 1], ric[:, q:q + 1], gt[:, 1:2], None, ALU.mult))
                    xt = x[:, bass.ds(t, 1), :].rearrange("p o c -> p (o c)")
                    dve.scalar_tensor_tensor(xt, ps[:, 6 + q, 0:D], rig[:, q:q + 1], xt, ALU.mult, ALU.add
                                             ).then_inc(xupd, 1)
                    wait_alone(xupd, XUPD_A + t + 1)
                    measure(t, j)
                aggregate(G * g, G, 0)
                if ahead:
                    c_max(g + 1, 1 - s)

            c_norm(0, 0, INV_B)
            c_max(0, 0)
            with dve.Fori(0, B - 1) as b:
                st.enter(b, 2 * G * 4)
                c_group(2 * b, 0, True)
                c_group(2 * b + 1, 1, True)
            st.leave(B - 1)
            c_group(NG - 2, 0, True)
            c_group(NG - 1, 1, False)

            def d_norm(n):
                for j in range(G):
                    normalise(G * n + j, xd[:, j, :])

            def d_group(n, ahead):
                for c in range(HC):
                    dve.wait_ge(sil_r, HC * n + c + 1)
                    dve.scalar_tensor_tensor(ha[:, c, :], ps[:, 3 + 2 * (c % 2), :], sc1[:, 1, c:c + 1],
                                             sil[:, c % 2, :], ALU.mult, ALU.mult).then_inc(h_r, 1)
                if ahead:
                    d_norm(n + 1)
                for j in range(G):
                    dve.wait_ge(d4_ps, G * n + j + 1)
                    dve.wait_ge(xupd, XUPD_C - 1 + G * n + j)
                    dve.tensor_tensor(ud[:, j % 2, :], ps[:, j % 2, 0:D], sc3[:], ALU.mult).then_inc(up_r, 1)

            dve.wait_ge(inv, INV_C)
            d_norm(0)
            with dve.Fori(0, NG - 1) as n:
                d_group(n, True)
            d_group(NG - 1, False)

        @block.gpsimd
        def _(pool):
            st = Steps(pool, pstep)

            def invert(t0, n, n_stats):
                pool.wait_ge(stats, n_stats)
                v = mv[:, bass.ds(t0, n), 1:2].rearrange("p t o -> p (t o)")
                st.link(pool.tensor_tensor(veps[:, bass.ds(t0, n)], v, eps_t[:, 0:n], ALU.add))
                pool.tensor_tensor(rstd[:, bass.ds(t0, n)], veps[:, bass.ds(t0, n)], half_t[:, 0:n], ALU.pow
                                   ).then_inc(inv, 1)

            pool.wait_ge(const_ready, 3)
            invert(0, JT, 1)

            def a_batch(b, ahead):
                if ahead:
                    invert(b * JT + JT, JT, 3 * b + 2)
                seen = 3 * b + (2 if ahead else 1)
                for j in range(JT):
                    pool.wait_ge(up_r, b * JT + (j + 1))
                    xt = x[:, bass.ds(b * JT + j, 1), :].rearrange("p o c -> p (o c)")
                    pool.tensor_tensor(xt, xt, u1[:, j % 2, :], ALU.add).then_inc(xupd, 1)
                    if j == JT - 2:
                        invert(b * JT, G, seen + 1)
                invert(b * JT + G, G, seen + 2)

            with pool.Fori(0, B - 1) as b:
                st.enter(b, 3)
                a_batch(b, True)
            st.leave(B - 1)
            a_batch(B - 1, False)
            with pool.Fori(0, NT // 2) as i:
                st.enter(i, 1)
                invert(2 * i, 2, INV_A + 1 + i)
            st.leave(NT // 2)
            with pool.Fori(0, NG) as g:
                st.enter(g, 1)
                invert(G * g, G, INV_B + 1 + g)
            st.leave(NG)
            with pool.Fori(0, NG) as n:
                for j in range(G):
                    pool.wait_ge(up_r, NT + 1 + G * n + j)
                    xt = x[:, bass.ds(G * n + j, 1), :].rearrange("p o c -> p (o c)")
                    pool.tensor_tensor(xt, xt, ud[:, j % 2, :], ALU.add).then_inc(xupd, 1)


XUPD_A, XUPD_C = NT, 2 * NT
INV_A = 1 + 3 * (B - 1) + 2
INV_B = INV_A + NT // 2
INV_C = INV_B + NG


def interpolation():
    pos = (np.arange(S, dtype=np.float32) + np.float32(0.5)) * np.float32(L / S) - np.float32(0.5)
    pos = np.clip(pos, np.float32(0), np.float32(L - 1))
    lo = np.floor(pos).astype(np.int32)
    hi = np.minimum(lo + 1, L - 1)
    w = (pos - lo.astype(np.float32)).astype(np.float32)
    m = np.zeros((L, S), np.float32)
    np.add.at(m, (lo, np.arange(S)), 1 - w)
    np.add.at(m, (hi, np.arange(S)), w)
    return np.ascontiguousarray(m.reshape(L, P, JT).transpose(0, 2, 1).reshape(L, S))


def kernel(**inputs):
    import concourse.bacc as bacc
    from concourse.bass_utils import run_bass_kernel_spmd as run

    a = {k: np.asarray(v) for k, v in inputs.items()}

    def chunks(w):
        return np.ascontiguousarray(w.reshape(-1, P, w.shape[-1]).transpose(1, 0, 2))

    def column(v):
        return np.ascontiguousarray(v.reshape(-1, P).T)

    pre = "L0_xattn_"
    wg = a[pre + "Wg"]
    weights = {"Wk_sT": a[pre + "Wk_s"].T, "Wq_sT": a[pre + "Wq_s"].T, "Wv_sT": a[pre + "Wv_s"].T,
               "Wq_c": a[pre + "Wq_c"], "Wk_c": a[pre + "Wk_c"], "Wv_cT": a[pre + "Wv_c"].T,
               "WgT0": wg[:, :D].T, "WgT1": wg[:, D:].T, "W1T": a["L1_xattn_W"].T}
    vectors = {n: a[pre + n] for n in COLS[:-1] + ["bg"]} | {"b1": a["L1_xattn_b"]}
    mask = a["mask_BxS2_bf0"]
    ctxt = a["ctx_1024"]
    f = "L1_ffn_"
    arrays = {
        "x": a["x"],
        "aw": np.stack([chunks(weights[n]) for n in AW], 1),
        "ctxT": chunks(ctxt.reshape(B * L, D).T),
        "ctx": np.ascontiguousarray(ctxt.transpose(1, 0, 2)),
        "cols": np.stack([column(vectors[n]) for n in COLS], 1),
        "rows": np.stack([vectors[n] for n in ROWS])[None],
        "ident": np.eye(P, dtype=np.float32),
        "maskT": np.ascontiguousarray(mask.T),
        "maskr": mask.reshape(1, B * L),
        "Wr": chunks(a["L0_ffn_Wr"]),
        "scales": np.stack([column(a[f + n]) for n in ("w1_s", "w2_s", "h1_s", "h2_s")], 1),
        "gates": np.concatenate([a["g_xattn"], a["g_ffn"]]),
        "w3_s": a[f + "w3_s"],
        "interp": interpolation(),
        "Wi": np.ascontiguousarray(a["L0_ffn_Wi"].transpose(2, 0, 1).reshape(KC, P, E, D).transpose(1, 0, 2, 3)),
        "Wo": np.ascontiguousarray(a["L0_ffn_Wo"].transpose(1, 0, 2).reshape(KC, P, E, D).transpose(1, 0, 2, 3)),
        "w1": chunks(a[f + "w1_w"].T), "w2": chunks(a[f + "w2_w"].T),
        "h1": chunks(a[f + "h1_w"].T), "h2": chunks(a[f + "h2_w"].T), "w3": chunks(a[f + "w3_w"].T),
    }
    nc = bacc.Bacc("TRN2", target_bir_lowering=False, num_devices=1)
    d = {n: nc.dram_tensor("in_" + n, v.shape, mybir.dt.from_np(v.dtype), kind="ExternalInput").ap()
         for n, v in arrays.items()}
    d["out"] = nc.dram_tensor("out", (NG, P, G, D), F32, kind="ExternalOutput").ap()
    program(nc, d)
    r = run(nc, [{"in_" + n: v for n, v in arrays.items()}], core_ids=[0])
    out = r.results[0]["out"].reshape(B, JT // G, P, G, D).transpose(0, 2, 1, 3, 4)
    return np.ascontiguousarray(out.reshape(B, S, D))
```

```python
from contextlib import ExitStack

import numpy as np

import concourse.bass as bass
from concourse import mybir

F32 = mybir.dt.float32
F32R = mybir.dt.float32r
BF16 = mybir.dt.bfloat16
I32 = mybir.dt.int32
U8 = mybir.dt.uint8
U16 = mybir.dt.uint16
ALU = mybir.AluOpType
ACT = mybir.ActivationFunctionType
X = mybir.AxisListType.X

P = 128
B, S, D, L = 4, 1024, 256, 77
KC = D // P
JT = S // P
NT = B * JT
G = 4
NG = NT // G
GN = G * P
E = 8
HID = 1024
HC = HID // P
BL = B * L
NW = (2 * KC + 2 * HC) * HID + HC * D
SLICE = 2048
REST_SLICES = (NW - HC * HID) // SLICE
NCHECK = NW // SLICE
EPS = 1e-5
FAR = -3.0e38
TAKEN = 3.0e38
SCALE = float(D) ** -0.5

LP = 96
COLS = ["bk_s", "bq_s", "bv_s", "bv_c", "bq_c", "bk_c", "b1"]
ROWS = ["bv_s", "bg", "bv_c"]
REST = ["w1", "w2", "w3", "h1"]
AW = ["Wk_sT", "Wq_sT", "Wv_sT", "W1T", "Wq_c", "Wk_c", "Wv_cT", "WgT0", "WgT1"]

XUPD_A, XUPD_C = NT, 2 * NT
STATS_A = 2 * B + B
UP_A = NT


def program(nc, d):
    ctx = ExitStack()
    with ctx:
        base = -(-nc.sbuf_base // 32) * 32
        room = {"x": (0, 32768), "small": (32768, 40960), "weights": (40960, 131072),
                "work": (131072, 212800)}
        cursor = {k: v[0] for k, v in room.items()}
        bytes_of = {U8: 1, U16: 2, BF16: 2}

        def place(region, name, shape, dt=F32, at=None):
            size = int(np.prod(shape[1:])) * bytes_of.get(dt, 4)
            size = -(-size // 32) * 32
            start = cursor[region] if at is None else at
            assert start + size <= room[region][1], (name, start + size)
            cursor[region] = start + size
            return nc.alloc_sbuf_tensor_at(name, shape, dt, offset=base + start)

        def sem(name):
            return ctx.enter_context(nc.semaphore(name))

        x = place("x", "x_residual", [P, NT, D])

        ident = place("small", "identity", [P, P])
        stat = place("small", "ln_stats", [P, JT, 6])
        agg = place("small", "ln_aggregate", [P, JT, 2])
        mv = place("small", "ln_mean_var", [P, NT, 2])
        veps = place("small", "ln_var_eps", [P, NT])
        rstd = place("small", "ln_rstd", [P, NT])
        eps_t = place("small", "eps", [P, JT])
        half_t = place("small", "minus_half", [P, JT])
        graw = place("small", "gates_raw", [P, 4])
        gt = place("small", "gates_tanh", [P, 4])
        gh = place("small", "gate_half", [P, 1])
        cols = place("small", "bias_columns", [P, len(COLS), KC])
        sc1 = place("small", "mlp_scales", [P, 4, HC])
        sc3 = place("small", "mlp_out_scale", [P, D])
        ones = place("small", "ones_row", [1, P])
        onec = place("small", "ones_column", [P, 1])
        lowsum = place("small", "low_half_sums", [P, NCHECK])
        lowcol = place("small", "low_half_sum", [P, 1])
        flag = place("small", "weights_not_short", [1, 1])

        wexp_h = place("weights", "expert_high", [P, KC, E * D], F32R)
        wexp_l = place("weights", "expert_low", [P, KC, E * D], F32R)
        wi_at = cursor["weights"]
        wi = place("weights", "expert_in", [P, KC, E, D])
        wo_at = cursor["weights"]
        wo = place("weights", "expert_out", [P, KC, E, D])
        KT = place("weights", "keys_T", [P, KC, BL])
        QT = place("weights", "queries_T", [P, KC, BL])
        VV = place("weights", "values_and_gate", [LP, B, 2 * D])
        IT = place("weights", "interpolation_T", [LP, S])
        mx2 = place("weights", "max_back", [L, 4])
        rs2 = place("weights", "sum_back", [L, 4])
        nm1 = place("weights", "neg_max", [P, JT])
        rs1 = place("weights", "sum_probs", [P, JT])
        ri1 = place("weights", "inv_sum", [P, JT])
        r2n = place("weights", "pooled", [L, D])
        t2T = place("weights", "pooled_T", [P, KC, L])
        sT = place("weights", "sub2char_T", [P, KC, L])
        E1 = place("weights", "probs", [P, JT, L], at=wi_at)
        P2 = place("weights", "probs_back", [L, S])
        P2T = place("weights", "probs_back_T", [P, JT, L])
        th = place("weights", "gate_tanh", [P, 2, D])
        ssb = place("weights", "sub2char_of_tile", [P, 2, D])
        u1 = place("weights", "update", [P, 2, D])
        P1T = place("weights", "probs_T", [LP, S], at=wo_at)
        s1s = place("weights", "scores_T", [L, S])
        SS = place("weights", "sub2char_and_gate", [LP, B, 2 * D])
        h2_at, rest_at = room["weights"][0], wi_at
        n_h2, n_rest = HC * HID, NW - HC * HID
        h2_raw = place("weights", "mlp_h2", [P, n_h2], at=h2_at)
        h2_round = place("weights", "mlp_h2_rounded", [P, n_h2], F32R, at=h2_at)
        rest_raw = place("weights", "mlp_rest", [P, n_rest], at=rest_at)
        rest_round = place("weights", "mlp_rest_rounded", [P, n_rest], F32R, at=rest_at)
        mlp_f, mlp_r, at = {}, {}, 0
        for n, rows_k, width in (("w1", KC, HID), ("w2", KC, HID), ("h1", HC, HID), ("w3", HC, D)):
            for into, t in ((mlp_f, rest_raw), (mlp_r, rest_round)):
                into[n] = t[:, at:at + rows_k * width].rearrange("p (k c) -> p k c", k=rows_k)
            at += rows_k * width
        for into, t in ((mlp_f, h2_raw), (mlp_r, h2_round)):
            into["h2"] = t[:].rearrange("p (k c) -> p k c", k=HC)
        assert n_h2 * 4 <= wi_at - h2_at and n_rest % SLICE == 0 and n_h2 % SLICE == 0

        wk = room["work"][0]
        rows = place("work", "bias_rows", [1, len(ROWS), D])
        aw = place("work", "attention_weights", [P, len(AW), KC, D])
        ctxT = place("work", "context_T", [P, KC, BL])
        ctxr = place("work", "context", [L, B, D])
        maskT = place("work", "mask_T", [L, B], U8)
        keep = place("work", "keep", [L, B])
        mcol = place("work", "mask_bias", [L, B])
        yk = place("work", "context_kept", [LP, B, D + 1])
        VT = place("work", "values_T", [P, KC, BL])
        ypT = place("work", "context_projected_T", [P, KC, BL])
        A1 = place("work", "score_map", [P, KC, BL])
        A2 = place("work", "score_map_back", [P, KC, BL])
        A1b = place("work", "score_map_of_batch", [P, KC, L])
        A2b = place("work", "score_map_back_of_batch", [P, KC, L])
        yTb = place("work", "context_projected_of_batch", [P, KC, L])
        c1 = place("work", "score_bias", [L, B])
        c2 = place("work", "score_bias_back", [L, B])
        c1b = place("work", "score_bias_of_batch", [L, 1])
        mcolb = place("work", "mask_bias_of_batch", [L, 1])
        dump = place("work", "examined", [P, SLICE], BF16)
        xn = place("work", "x_normalised", [P, JT, D])
        xt_at = cursor["work"]
        xnT = place("work", "x_normalised_T", [P, KC, S])
        xTh = place("work", "x_T_high", [P, 2, KC, GN], F32R, at=xt_at)
        xTl = place("work", "x_T_low", [P, 2, KC, GN], F32R)
        wr = place("work", "router", [P, KC, E])
        wrh = place("work", "router_high", [P, KC, E], F32R)
        wrl = place("work", "router_low", [P, KC, E], F32R)
        lgT = place("work", "logits_T", [E, GN])
        lg = place("work", "logits", [P, G, 2 * E])
        top = place("work", "top8", [P, G, E])
        want = place("work", "to_mark", [P, G, E])
        marked = place("work", "marked", [P, G, 2 * E])
        lsub = place("work", "logits_less_max", [P, G, E])
        pex = place("work", "expert_exp", [P, G, E])
        sme = place("work", "expert_sum", [P, G])
        rie = place("work", "expert_inv", [P, G])
        rig = place("work", "expert_inv_gated", [P, G])
        pm = place("work", "expert_masked", [P, G, E])
        coef = place("work", "expert_weight", [P, 2, G, E])
        xcT = place("work", "x_norm_c_T", [P, KC, GN], at=xt_at)
        xpT = place("work", "x_projected_T", [P, KC, GN])
        scT = place("work", "scores_c_T", [L, GN])
        EC = place("work", "probs_c", [P, G, L])
        PT = place("work", "probs_c_T", [LP, GN])
        nmc = place("work", "neg_max_c", [P, G])
        ric = place("work", "inv_sum_c", [P, G])
        rcg = place("work", "inv_sum_gated", [P, G])
        ha_h = place("work", "hidden_a_high", [P, HC, GN], F32R, at=wk)
        ha_at = cursor["work"]
        ha_l = place("work", "hidden_a_low", [P, HC, GN], F32R)
        ha_f = place("work", "hidden_a", [P, HC, GN], at=ha_at)
        hb_at = cursor["work"]
        hb_h = place("work", "hidden_b_high", [P, HC, GN], F32R)
        xd = place("work", "x_norm_d", [P, G, D], at=hb_at)
        hbl_at = hb_at + HC * GN * 4
        hb_l = place("work", "hidden_b_low", [P, HC, GN], F32R, at=hbl_at)
        hb_f = place("work", "hidden_b", [P, HC, GN], at=hbl_at)
        xdT_h = place("work", "x_norm_d_T_high", [P, KC, GN], F32R)
        xdl_at = cursor["work"]
        xdT_l = place("work", "x_norm_d_T_low", [P, KC, GN], F32R)
        xdT_f = place("work", "x_norm_d_T", [P, KC, GN], at=xdl_at)
        ud = place("work", "update_d", [P, 2, D])

        ps = ctx.enter_context(nc.psum_tensor("psum", [P, 8, 512], F32))

        small_in = sem("small_inputs_loaded")
        aw1_in = sem("projection_weights_loaded")
        aw2_in = sem("map_weights_loaded")
        it_in = sem("interpolation_loaded")
        x_in = [sem(f"x_loaded_{b}") for b in range(B)]
        exp_in = sem("expert_weights_loaded")
        rest_in = sem("mlp_rest_loaded")
        h2_in = sem("mlp_h2_loaded")
        again_in = sem("mlp_weights_loaded_again")
        out_done = sem("output_stored")
        gate_ready = sem("gates_ready")
        const_ready = sem("constants_ready")
        zero_ready = sem("zero_rows_ready")
        dstep = sem("vector_step_done")
        pstep = sem("pool_step_done")
        proj = sem("projection_in_psum")
        proj_v = sem("projection_saved_by_vector")
        proj_s = sem("projection_saved_by_scalar")
        map_ps = sem("score_maps_in_psum")
        map_v = sem("score_maps_saved")
        val_ps = sem("values_in_psum")
        val_v = sem("values_saved")
        ex_ps = sem("expert_product_in_psum")
        ex_h = sem("expert_high_saved")
        ex_l = sem("expert_low_saved")
        stats = sem("ln_stats_ready")
        inv = sem("ln_rstd_ready")
        xn_r = sem("x_normalised_ready")
        tp = sem("x_transposed_in_psum")
        xT_r = sem("x_transposed_saved")
        xupd = sem("x_updated")
        map_b = sem("maps_of_batch_copied")
        s2_ps = sem("scores_back_in_psum")
        s2_b = sem("scores_back_bias_ready")
        p2_r = sem("probs_back_ready")
        s1_ps = sem("scores_T_in_psum")
        s1_s = sem("scores_T_saved")
        s1b_ps = sem("scores_in_psum")
        nm_r = sem("neg_max_ready")
        e1_r = sem("probs_ready")
        e1n = sem("probs_normalised")
        p2t_ps = sem("probs_back_T_in_psum")
        p2t_v = sem("probs_back_T_saved")
        r2_ps = sem("pooled_in_psum")
        r2_v = sem("pooled_saved")
        p1t_ps = sem("probs_T_in_psum")
        p1t_v = sem("probs_T_saved")
        t2_ps = sem("pooled_T_in_psum")
        t2_v = sem("pooled_T_saved")
        so_ps = sem("sub2char_in_psum")
        so_v = sem("sub2char_saved")
        st_ps = sem("sub2char_T_in_psum")
        st_v = sem("sub2char_T_saved")
        sg_ps = sem("sub2char_gate_in_psum")
        sg_v = sem("sub2char_gate_saved")
        fin = sem("both_ways_in_psum")
        th_r = sem("gate_tanh_ready")
        ss_r = sem("sub2char_of_tile_saved")
        up_r = sem("update_ready")
        xh_r = sem("x_T_high_ready")
        rt_ps = sem("router_logits_T_in_psum")
        rt_s = sem("router_logits_T_saved")
        rb_ps = sem("router_logits_in_psum")
        rb_v = sem("router_logits_used")
        lg_r = sem("router_exponent_ready")
        ee_r = sem("router_exp_ready")
        y_ps = sem("expert_outputs_in_psum")
        y_free = sem("expert_bank_free")
        xp_ps = sem("x_projected_in_psum")
        xp_r = sem("x_projected_saved")
        sc_ps = sem("scores_c_T_in_psum")
        sc_s = sem("scores_c_T_saved")
        sb_ps = sem("scores_c_in_psum")
        mc_r = sem("neg_max_c_ready")
        ec_r = sem("probs_c_ready")
        pt_ps = sem("probs_c_T_in_psum")
        pt_r = sem("probs_c_T_saved")
        o_ps = sem("attended_in_psum")
        yb_r = sem("context_projected_copied")
        ck_r = sem("weights_slice_examined")
        fl_v = sem("low_half_sum_ready")
        fl_ps = sem("flag_in_psum")
        fl_r = sem("flag_ready")
        d1_ps = sem("mlp_first_in_psum")
        sil_r = sem("silu_ready")
        h_r = sem("gated_hidden_ready")
        d2_ps = sem("mlp_hidden_in_psum")
        g_r = sem("gelu_ready")
        hi_r = sem("hidden_high_ready")
        lo_r = sem("hidden_low_ready")
        d4_ps = sem("mlp_output_in_psum")

        def col(name, m):
            return cols[:, COLS.index(name), m:m + 1]

        def row(name):
            return rows[:, ROWS.index(name), :]

        def wa(name):
            return aw[:, AW.index(name)]

        def of(t, i, *rest):
            return t[:, bass.ds(i, 1)].rearrange("p o c -> p (o c)")

        class Steps:

            def __init__(self, eng, s):
                self.eng, self.s, self.start, self.n = eng, s, 0, 0

            def mark(self, ins):
                ins.then_inc(self.s, 1)
                self.n += 1

            def wait(self):
                self.eng.wait_ge(self.s, self.start + self.n)

            def link(self, ins):
                self.mark(ins)
                self.wait()

            def enter(self, i, per):
                self.first = self.start + self.n
                self.start, self.n, self.per = self.first + i * per, 0, per

            def leave(self, passes):
                assert self.n == self.per, (self.n, self.per)
                self.start, self.n = self.first + passes * self.per, 0

        def weave(c, tile, step):
            for k in range(JT):
                tile(c - 1, k)
                step[k](c)
            for k in range(JT, len(step)):
                step[k](c)

        block = ctx.enter_context(nc.Block())

        @block.sync
        def _(sp):
            for t, n in ((ctxT, "ctxT"), (cols, "cols"), (ident, "ident"), (rows, "rows"), (ctxr, "ctx"),
                         (maskT, "maskT"), (wr, "Wr"), (sc1, "scales")):
                sp.dma_start(t[:], d[n]).then_inc(small_in, 16)
            sp.dma_start(graw[:], d["gates"].partition_broadcast(P)).then_inc(small_in, 16)
            sp.dma_start(sc3[:], d["w3_s"].partition_broadcast(P)).then_inc(small_in, 16)
            for b in range(B):
                sp.dma_start(x[:, b * JT:(b + 1) * JT, :], d["x"][b].rearrange("(p j) c -> p j c", p=P)
                             ).then_inc(x_in[b], 16)
            sp.wait_ge(fin, NT)
            sp.wait_ge(th_r, NT)
            sp.wait_ge(xupd, NT)
            for n in REST:
                sp.dma_start(mlp_f[n], d[n]).then_inc(rest_in, 16)
            sp.wait_ge(y_ps, 4 * NT)
            sp.dma_start(mlp_f["h2"], d["h2"]).then_inc(h2_in, 16)
            with sp.Fori(0, NG) as n:
                sp.wait_ge(xupd, XUPD_C + G + n * G)
                src = x[:, bass.ds(n * G, G), :]
                dst = d["out"][bass.ds(n, 1)].rearrange("o p j c -> p (o j) c")
                sp.dma_start(dst, src).then_inc(out_done, 16)
            sp.wait_ge(out_done, 16 * NG)

        N_SMALL = 10 * 16
        N_FIRST = 4

        @block.tensor
        def _(pe):
            mm = pe.matmul

            def transposes(src, slot):
                for k in range(KC):
                    last = pe.transpose(ps[:, slot, k * P:(k + 1) * P], src[:, k * P:(k + 1) * P], ident[:])
                last.then_inc(tp, 1)

            pe.wait_ge(aw1_in, 16)
            pe.wait_ge(small_in, N_SMALL)
            for n, w in enumerate(AW[:N_FIRST]):
                for m in range(KC):
                    for k in range(KC):
                        last = mm(ps[:, 2 * n + m, 0:BL], wa(w)[:, k, m * P:(m + 1) * P], ctxT[:, k, :],
                                  start=(k == 0), stop=(k == KC - 1))
                    last.then_inc(proj, 1)
            pe.wait_ge(aw2_in, 16)
            pe.wait_ge(proj_v, 4)
            for n, (w, src) in enumerate((("Wq_c", KT), ("Wk_c", QT))):
                for m in range(KC):
                    for k in range(KC):
                        last = mm(ps[:, 2 * n + m, 0:BL], wa(w)[:, k, m * P:(m + 1) * P], src[:, k, :],
                                  start=(k == 0), stop=(k == KC - 1))
                    last.then_inc(map_ps, 1)
            pe.wait_ge(proj_v, 6)
            for bank, src, bias in ((4, KT, "bq_c"), (5, QT, "bk_c")):
                for b in range(B):
                    for k in range(KC):
                        last = mm(ps[0:L, bank, b:b + 1], src[:, k, b * L:(b + 1) * L], col(bias, k),
                                  start=(k == 0), stop=(k == KC - 1))
                last.then_inc(map_ps, 1)
            pe.wait_ge(proj_s, 2)
            pe.wait_ge(const_ready, 1)
            for b in range(B):
                if b >= 2:
                    pe.wait_ge(val_v, 2 * (b - 1))
                bank = 6 + b % 2
                for half, (src, w, bias) in enumerate(((ctxT, "Wv_sT", "bv_s"), (VT, "WgT0", "bg"))):
                    o = ps[0:L, bank, half * D:(half + 1) * D]
                    for k in range(KC):
                        mm(o, src[:, k, b * L:(b + 1) * L], wa(w)[:, k, :], start=(k == 0), stop=False)
                    last = mm(o, ones[0:1, 0:L], row(bias), start=False, stop=True)
                last.then_inc(val_ps, 1)
            pe.wait_ge(exp_in, 32)
            pe.wait_ge(map_v, 6)
            for e in range(E):
                if e >= 4:
                    pe.wait_ge(ex_l, e - 3)
                for m in range(KC):
                    for k in range(KC):
                        last = mm(ps[:, e % 4, m * D:(m + 1) * D], wi[:, k, e, m * P:(m + 1) * P], wo[:, k, e, :],
                                  start=(k == 0), stop=(k == KC - 1))
                last.then_inc(ex_ps, 1)
            pe.wait_ge(ex_l, E)
            pe.wait_ge(val_v, 2 * B)

            def a_turn(c, q):
                for j in range(q * G, (q + 1) * G):
                    pe.wait_ge(xn_r, c * JT + (j + 1))
                    if j >= 2:
                        pe.wait_ge(xT_r, c * JT + (j - 1))
                    transposes(xn[:, j, :], 4 + j % 2)

            def a_back_scores(c):
                pe.wait_ge(xT_r, (c + 1) * JT)
                pe.wait_ge(map_b, 2 * c + 2)
                for h in range(2):
                    for k in range(KC):
                        last = mm(ps[0:L, 6 + h, :], A2b[:, k, :], xnT[:, k, h * 512:(h + 1) * 512],
                                  start=(k == 0), stop=(k == KC - 1))
                last.then_inc(s2_ps, 1)

            def a_scores_T(c):
                for h in range(2):
                    for k in range(KC):
                        last = mm(ps[0:L, 4 + h, :], A1b[:, k, :], xnT[:, k, h * 512:(h + 1) * 512],
                                  start=(k == 0), stop=(k == KC - 1))
                    last.then_inc(s1_ps, 1)

            def a_scores(c):
                pe.wait_ge(s1_s, 2 * c + 2)
                for j in range(JT):
                    last = pe.transpose(ps[:, 4 + j // G, (j % G) * L:(j % G + 1) * L],
                                        s1s[:, j * P:(j + 1) * P], ident[0:L, 0:L])
                    if j % G == G - 1:
                        last.then_inc(s1b_ps, 1)

            def a_probs_back_T(c):
                pe.wait_ge(p2_r, 2 * c + 2)
                for j in range(JT):
                    last = pe.transpose(ps[:, 6 + j // G, (j % G) * L:(j % G + 1) * L],
                                        P2[:, j * P:(j + 1) * P], ident[0:L, 0:L])
                    if j % G == G - 1:
                        last.then_inc(p2t_ps, 1)

            def a_pool(c):
                pe.wait_ge(p2t_v, 2 * c + 2)
                for j in range(JT):
                    last = mm(ps[0:L, 6, 0:D], P2T[:, j, :], xn[:, j, :], start=(j == 0), stop=(j == JT - 1))
                last.then_inc(r2_ps, 1)

            def a_pooled_T(c):
                pe.wait_ge(r2_v, c + 1)
                for k in range(KC):
                    last = pe.transpose(ps[:, 7, k * L:(k + 1) * L], r2n[:, k * P:(k + 1) * P], ident[0:L, 0:L])
                last.then_inc(t2_ps, 1)

            def a_sub2char(c):
                pe.wait_ge(t2_v, c + 1)
                for m in range(KC):
                    for k in range(KC):
                        last = mm(ps[:, 7, m * L:(m + 1) * L], wa("Wv_cT")[:, k, m * P:(m + 1) * P], t2T[:, k, :],
                                  start=(k == 0), stop=(k == KC - 1))
                last.then_inc(st_ps, 1)
                for k in range(KC):
                    mm(ps[0:L, 6, 0:D], t2T[:, k, :], wa("Wv_cT")[:, k, :], start=(k == 0), stop=False)
                mm(ps[0:L, 6, 0:D], ones[0:1, 0:L], row("bv_c"), start=False, stop=True).then_inc(so_ps, 1)

            def a_probs_T(c):
                for q in range(2):
                    pe.wait_ge(e1n, c * JT + (q + 1) * G)
                    for j in range(G):
                        last = pe.transpose(ps[0:L, 4 + q, j * P:(j + 1) * P], E1[:, q * G + j, :], ident[:])
                    last.then_inc(p1t_ps, 1)

            def a_sub2char_gate(c):
                pe.wait_ge(st_v, 2 * c + 2)
                for m in range(KC):
                    last = mm(ps[0:L, 7, 0:D], sT[:, m, :], wa("WgT1")[:, m, :], start=(m == 0), stop=(m == KC - 1))
                last.then_inc(sg_ps, 1)

            def a_sum(b, j):
                if j == 0:
                    pe.wait_ge(p1t_v, 2 * b + 2)
                    pe.wait_ge(so_v, b + 1)
                    pe.wait_ge(sg_v, b + 1)
                if j >= 2:
                    pe.wait_ge(up_r, b * JT + (j - 1))
                t = slice(j * P, (j + 1) * P)
                q = j % 2
                mm(ps[:, q, :], P1T[:, t], of(VV, b), start=True, stop=False)
                mm(ps[:, q, D:2 * D], IT[:, t], SS[:, bass.ds(b, 1), D:2 * D].rearrange("p o c -> p (o c)"),
                   start=False, stop=True)
                mm(ps[:, 2 + q, 0:D], IT[:, t], SS[:, bass.ds(b, 1), 0:D].rearrange("p o c -> p (o c)"),
                   start=True, stop=True).then_inc(fin, 1)

            steps = [lambda c: a_turn(c, 0), lambda c: a_turn(c, 1), a_back_scores, a_scores_T, a_scores,
                     a_probs_back_T, a_pool, a_pooled_T, a_sub2char, a_probs_T, a_sub2char_gate]
            pe.wait_ge(it_in, 16)
            pe.wait_ge(zero_ready, 4)
            for f in steps:
                f(0)
            with pe.Fori(1, B) as c:
                weave(c, a_sum, steps)
                pe.wait_ge(up_r, c * JT)
            for j in range(JT):
                a_sum(B - 1, j)
            pe.wait_ge(up_r, B * JT)

            def b_turn(g, s):
                for j in range(G):
                    pe.wait_ge(xn_r, NT + 1 + j + G * g)
                    pe.wait_ge(xT_r, NT - 1 + j + G * g)
                    transposes(xn[:, s * G + j, :], j % 2)

            def b_route_T(g, s):
                pe.wait_ge(xT_r, NT + G + G * g)
                n = 0
                for k in range(KC):
                    for a, c in ((xTh, wrh), (xTl, wrh), (xTh, wrl)):
                        last = mm(ps[0:E, 2, :], c[:, k, :], a[:, s, k, :], start=(n == 0), stop=(n == 3 * KC - 1))
                        n += 1
                last.then_inc(rt_ps, 1)

            def b_route(g):
                if not isinstance(g, int):
                    pe.compute_val(g + 1)
                pe.wait_ge(const_ready, 4)
                pe.wait_ge(rt_s, g + 1)
                for j in range(G):
                    last = pe.transpose(ps[:, 3, j * E:(j + 1) * E], lgT[:, j * P:(j + 1) * P], ident[0:E, 0:E])
                last.then_inc(rb_ps, 1)

            def b_experts(g, s, j):
                for pair in range(E // 2):
                    pe.wait_ge(y_free, 1 + pair + 4 * j + 4 * G * g)
                    n = 0
                    for k in range(KC):
                        for a, c in ((xTh, wexp_h), (xTh, wexp_l), (xTl, wexp_h)):
                            last = mm(ps[:, 4 + pair, :], a[:, s, k, j * P:(j + 1) * P],
                                      c[:, k, pair * 2 * D:(pair + 1) * 2 * D],
                                      start=(n == 0), stop=(n == 3 * KC - 1))
                            n += 1
                    last.then_inc(y_ps, 1)

            def b_group(g, s, ahead):
                b_experts(g, s, 0)
                if ahead:
                    b_turn(g + 1, 1 - s)
                b_experts(g, s, 1)
                if ahead:
                    b_route_T(g + 1, 1 - s)
                b_experts(g, s, 2)
                if ahead:
                    b_route(g + 1)
                b_experts(g, s, 3)

            b_turn(0, 0)
            b_route_T(0, 0)
            b_route(0)
            with pe.Fori(0, NG // 2 - 1) as i:
                b_group(2 * i, 0, True)
                b_group(2 * i + 1, 1, True)
            b_group(NG - 2, 0, True)
            b_group(NG - 1, 1, False)

            def c_turn(g, s):
                for j in range(G):
                    pe.wait_ge(xn_r, 2 * NT + 1 + j + G * g)
                    pe.wait_ge(xT_r, 2 * NT - 1 + j + G * g)
                    transposes(xn[:, s * G + j, :], j % 2)

            def c_project(g):
                pe.wait_ge(xT_r, 2 * NT + G + G * g)
                for m in range(KC):
                    for k in range(KC):
                        last = mm(ps[:, 2 + m, :], wa("W1T")[:, k, m * P:(m + 1) * P], xcT[:, k, :],
                                  start=(k == 0), stop=(k == KC - 1))
                    last.then_inc(xp_ps, 1)

            def c_scores_T(g, b):
                pe.wait_ge(yb_r, b + 1)
                for k in range(KC):
                    pe.wait_ge(xp_r, 2 * g + k + 1)
                    last = mm(ps[0:L, 4, :], yTb[:, k, :], xpT[:, k, :], start=(k == 0), stop=(k == KC - 1))
                last.then_inc(sc_ps, 1)

            def c_scores(g):
                pe.wait_ge(sc_s, g + 1)
                for j in range(G):
                    last = pe.transpose(ps[:, 5, j * L:(j + 1) * L], scT[:, j * P:(j + 1) * P], ident[0:L, 0:L])
                last.then_inc(sb_ps, 1)

            def c_probs_T(g):
                pe.wait_ge(ec_r, G * g + G)
                for j in range(G):
                    last = pe.transpose(ps[0:L, 6, j * P:(j + 1) * P], EC[:, j, :], ident[:])
                last.then_inc(pt_ps, 1)

            def c_attend(g, b):
                pe.wait_ge(pt_r, g + 1)
                for j in range(G):
                    if j >= 2:
                        pe.wait_ge(xupd, XUPD_A - 1 + j + G * g)
                    mm(ps[:, 6 + j % 2, 0:D + 1], PT[:, j * P:(j + 1) * P], of(yk, b),
                       start=True, stop=True).then_inc(o_ps, 1)

            def c_group(g, s, b, b_next):
                if b_next is not None:
                    c_turn(g + 1, 1 - s)
                c_scores(g)
                if b_next is not None:
                    c_project(g + 1)
                c_probs_T(g)
                if b_next is not None:
                    c_scores_T(g + 1, b_next)
                c_attend(g, b)
                pe.wait_ge(xupd, XUPD_A + G + G * g)

            c_turn(0, 0)
            c_project(0)
            c_scores_T(0, 0)
            with pe.Fori(0, B - 1) as b:
                c_group(2 * b, 0, b, b)
                c_group(2 * b + 1, 1, b, b + 1)
            c_group(NG - 2, 0, B - 1, B - 1)
            c_group(NG - 1, 1, B - 1, None)

            pe.wait_ge(fl_v, 1)
            mm(ps[0:1, 5, 0:1], lowcol[:], onec[:], start=True, stop=True).then_inc(fl_ps, 1)

            def stage_d(short):
                if short:
                    w = mlp_r
                    xT, ha, hb = (xdT_h, xdT_l), (ha_h, ha_l), (hb_h, hb_l)
                else:
                    w = mlp_f
                    xT, ha, hb = (xdT_f,), (ha_f,), (hb_f,)

                def product(o, stationary, moving, last_k, n_k, k):
                    parts = [(a, b) for a in stationary for b in moving]
                    for i, (a, b) in enumerate(parts):
                        last = mm(o, a, b, start=(k == 0 and i == 0), stop=(k == n_k - 1 and i == len(parts) - 1))
                    return last

                def turn(n):
                    for j in range(G):
                        pe.wait_ge(xn_r, 3 * NT + 1 + j + G * n)
                        pe.wait_ge(xT_r, 3 * NT - 1 + j + G * n)
                        transposes(xd[:, j, :], j % 2)

                def hidden_ready(n, layer, k):
                    if short:
                        pe.wait_ge(lo_r, 3 * HC * n + HC * layer + k + 1)
                    elif layer == 0:
                        pe.wait_ge(h_r, HC * n + k + 1)
                    else:
                        pe.wait_ge(g_r, 2 * HC * n + HC * (layer - 1) + k + 1)

                def group(n, ahead):
                    pe.wait_ge(xT_r, 3 * NT + G + G * n)
                    for c in range(HC):
                        a = 2 + 2 * (c % 2)
                        if c >= 2:
                            pe.wait_ge(h_r, HC * n + c - 1)
                        else:
                            pe.wait_ge(up_r, UP_A + G * n - 2 + 2 * c)
                        for name, bank in (("w1", a), ("w2", a + 1)):
                            for k in range(KC):
                                last = product(ps[:, bank, :], [w[name][:, k, c * P:(c + 1) * P]],
                                               [t[:, k, :] for t in xT], None, KC, k)
                        last.then_inc(d1_ps, 1)
                    for layer, (name, src) in enumerate((("h1", ha), ("h2", hb))):
                        for c in range(HC):
                            q = 2 * HC * n + HC * layer + c
                            if layer or c >= 2:
                                pe.wait_ge(g_r, q - 1)
                            for k in range(HC):
                                if c == 0:
                                    hidden_ready(n, layer, k)
                                last = product(ps[:, 6 + c % 2, :], [w[name][:, k, c * P:(c + 1) * P]],
                                               [t[:, k, :] for t in src], None, HC, k)
                            last.then_inc(d2_ps, 1)
                    for j in range(G):
                        if j == 2 and ahead:
                            turn(n + 1)
                        for k in range(HC):
                            if j == 0:
                                hidden_ready(n, 2, k)
                            last = product(ps[:, 2 + j, 0:D], [t[:, k, j * P:(j + 1) * P] for t in ha],
                                           [w["w3"][:, k, :]], None, HC, k)
                        last.then_inc(d4_ps, 1)

                turn(0)
                with pe.Fori(0, NG - 1) as n:
                    group(n, True)
                group(NG - 1, False)

            pe.wait_ge(fl_r, 1)
            long = pe.value_load(flag[:].bitcast(I32))
            with pe.If(long == 0):
                stage_d(True)
            with pe.Else():
                pe.wait_ge(again_in, 16 * (len(REST) + 1))
                stage_d(False)

        @block.scalar
        def _(act):
            act.dma_start(aw[:, 0:N_FIRST], d["aw"][:, 0:N_FIRST]).then_inc(aw1_in, 16)
            act.dma_start(aw[:, N_FIRST:], d["aw"][:, N_FIRST:]).then_inc(aw2_in, 16)
            act.dma_start(wi[:], d["Wi"]).then_inc(exp_in, 16)
            act.dma_start(wo[:], d["Wo"]).then_inc(exp_in, 16)
            act.dma_start(IT[:], d["interp"]).then_inc(it_in, 16)
            act.wait_ge(small_in, N_SMALL)
            act.activation(gt[:], graw[:], ACT.Tanh).then_inc(gate_ready, 1)
            for m in range(KC):
                act.wait_ge(proj, 7 + m)
                act.activation(ypT[:, m, :], ps[:, 6 + m, 0:BL], ACT.Relu, bias=col("b1", m)).then_inc(proj_s, 1)
            for e in range(E):
                act.wait_ge(ex_ps, e + 1)
                act.activation(wexp_h[:, :, e * D:(e + 1) * D],
                               ps[:, e % 4, :].rearrange("p (m c) -> p m c", m=KC), ACT.Copy).then_inc(ex_h, 1)

            def a_turn(c, q):
                for j in range(q * G, (q + 1) * G):
                    act.wait_ge(tp, c * JT + (j + 1))
                    act.activation(xnT[:, :, j * P:(j + 1) * P],
                                   ps[:, 4 + j % 2, 0:D].rearrange("p (k c) -> p k c", k=KC), ACT.Copy
                                   ).then_inc(xT_r, 1)

            def a_scores_T(c):
                for h in range(2):
                    act.wait_ge(s1_ps, 2 * c + h + 1)
                    act.activation(s1s[:, h * 512:(h + 1) * 512], ps[0:L, 4 + h, :], ACT.Identity,
                                   bias=c1b[:, 0:1]).then_inc(s1_s, 1)

            def a_exp_back(c):
                act.wait_ge(s2_b, c + 1)
                for h in range(2):
                    act.activation(P2[:, h * 512:(h + 1) * 512], ps[0:L, 6 + h, :], ACT.Exp, bias=mx2[:, 2:3],
                                   scale=1.0, accum_out=rs2[:, h:h + 1]).then_inc(p2_r, 1)

            def a_exp(c):
                for j in range(JT):
                    if j % G == 0:
                        act.wait_ge(nm_r, 2 * c + (j // G + 1))
                    act.activation(E1[:, j, :], ps[:, 4 + j // G, (j % G) * L:(j % G + 1) * L], ACT.Exp,
                                   bias=nm1[:, j:j + 1], scale=1.0, accum_out=rs1[:, j:j + 1]).then_inc(e1_r, 1)

            def a_probs_T(c):
                for q in range(2):
                    act.wait_ge(p1t_ps, 2 * c + (q + 1))
                    act.activation(P1T[0:L, q * GN:(q + 1) * GN], ps[0:L, 4 + q, :], ACT.Copy).then_inc(p1t_v, 1)

            def a_sum(b, j):
                q = j % 2
                act.wait_ge(fin, b * JT + (j + 1))
                if j >= 2:
                    act.wait_ge(up_r, b * JT + (j - 1))
                act.activation(ssb[:, q, :], ps[:, 2 + q, 0:D], ACT.Copy).then_inc(ss_r, 1)
                act.activation(th[:, q, :], ps[:, q, D:2 * D], ACT.Tanh, scale=0.5).then_inc(th_r, 1)

            def nothing(c):
                pass

            steps = [lambda c: a_turn(c, 0), lambda c: a_turn(c, 1), nothing, a_scores_T, a_exp_back,
                     a_exp, nothing, nothing, nothing, a_probs_T, nothing]
            act.wait_ge(zero_ready, 4)
            for f in steps:
                f(0)
            with act.Fori(1, B) as c:
                weave(c, a_sum, steps)
            for j in range(JT):
                a_sum(B - 1, j)

            def examine(raw, rounded, i, k):
                part = slice(i * SLICE, (i + 1) * SLICE) if isinstance(i, int) else bass.ds(i * SLICE, SLICE)
                low = raw[:, part].bitcast(U16).rearrange("p (n h) -> p n h", h=2)[:, :, 0:1]
                act.activation(dump[:], low.rearrange("p n o -> p (n o)"), ACT.Copy,
                               accum_out=lowsum[:, bass.ds(k, 1)]).then_inc(ck_r, 1)
                act.wait_ge(ck_r, 2 * k + 1)
                act.activation(rounded[:, part], raw[:, part], ACT.Copy).then_inc(ck_r, 1)
                act.wait_ge(ck_r, 2 * k + 2)

            def b_high(g, s):
                for j in range(G):
                    act.wait_ge(tp, NT + 1 + j + G * g)
                    act.activation(xTh[:, s, :, j * P:(j + 1) * P],
                                   ps[:, j % 2, 0:D].rearrange("p (k c) -> p k c", k=KC), ACT.Copy
                                   ).then_inc(xh_r, 1)

            def b_logits(g):
                act.wait_ge(rt_ps, g + 1)
                act.activation(lgT[:], ps[0:E, 2, :], ACT.Copy).then_inc(rt_s, 1)

            def b_exp(g):
                act.wait_ge(lg_r, g + 1)
                act.activation(pex[:], lsub[:], ACT.Exp).then_inc(ee_r, 1)

            def b_group(g, s):
                b_high(g, s)
                b_logits(g)
                b_exp(g)

            b_group(0, 0)
            act.wait_ge(rest_in, 16 * len(REST))
            with act.Fori(0, NG // 2 - 1) as i:
                b_group(2 * i + 1, 1)
                examine(rest_raw, rest_round, 2 * i, 2 * i)
                b_group(2 * i + 2, 0)
                examine(rest_raw, rest_round, 2 * i + 1, 2 * i + 1)
            b_group(NG - 1, 1)
            for i in range(NG - 2, REST_SLICES):
                examine(rest_raw, rest_round, i, i)

            def c_turn(g):
                for j in range(G):
                    act.wait_ge(tp, 2 * NT + 1 + j + G * g)
                    act.activation(xcT[:, :, j * P:(j + 1) * P],
                                   ps[:, j % 2, 0:D].rearrange("p (k c) -> p k c", k=KC), ACT.Copy).then_inc(xT_r, 1)

            def c_project(g):
                for m in range(KC):
                    act.wait_ge(xp_ps, 2 * g + m + 1)
                    act.activation(xpT[:, m, :], ps[:, 2 + m, :], ACT.Relu, bias=col("b1", m)).then_inc(xp_r, 1)

            def c_scores_T(g, b):
                act.wait_ge(sc_ps, g + 1)
                act.wait_ge(yb_r, b + 1)
                act.activation(scT[:], ps[0:L, 4, :], ACT.Identity, bias=mcolb[:, 0:1]).then_inc(sc_s, 1)

            def c_exp(g):
                act.wait_ge(mc_r, g + 1)
                for j in range(G):
                    act.activation(EC[:, j, :], ps[:, 5, j * L:(j + 1) * L], ACT.Exp, bias=nmc[:, j:j + 1],
                                   scale=1.0).then_inc(ec_r, 1)

            def c_group(g, b_next, check):
                ahead = b_next is not None
                if ahead:
                    c_turn(g + 1)
                c_exp(g)
                if ahead:
                    c_project(g + 1)
                if ahead:
                    c_scores_T(g + 1, b_next)
                if check is not None:
                    examine(h2_raw, h2_round, check, REST_SLICES + check)

            c_turn(0)
            c_project(0)
            c_scores_T(0, 0)
            act.wait_ge(xupd, XUPD_A)
            with act.Fori(0, 2) as b:
                c_group(2 * b, b, None)
                c_group(2 * b + 1, b + 1, None)
            act.wait_ge(h2_in, 16)
            c_group(NG - 4, B - 2, 0)
            c_group(NG - 3, B - 1, 1)
            c_group(NG - 2, B - 1, 2)
            c_group(NG - 1, None, 3)
            act.wait_ge(fl_ps, 1)
            act.activation(flag[:], ps[0:1, 5, 0:1], ACT.Copy).then_inc(fl_r, 1)

            def stage_d(short):
                def turn(n):
                    for j in range(G):
                        act.wait_ge(tp, 3 * NT + 1 + j + G * n)
                        dst, done = (xdT_h, xh_r) if short else (xdT_f, xT_r)
                        act.activation(dst[:, :, j * P:(j + 1) * P],
                                       ps[:, j % 2, 0:D].rearrange("p (k c) -> p k c", k=KC), ACT.Copy
                                       ).then_inc(done, 1)

                def high(c, full, part, ready, count):
                    if short:
                        act.wait_ge(ready, count)
                        act.activation(part[:, c, :], full[:, c, :], ACT.Copy).then_inc(hi_r, 1)

                def group(n, ahead):
                    for c in range(HC):
                        act.wait_ge(d1_ps, HC * n + c + 1)
                        act.activation(ha_f[:, c, :], ps[:, 2 + 2 * (c % 2), :], ACT.Silu,
                                       scale=sc1[:, 0, c:c + 1]).then_inc(sil_r, 1)
                        if c >= 1:
                            high(c - 1, ha_f, ha_h, h_r, HC * n + c)
                    high(HC - 1, ha_f, ha_h, h_r, HC * n + HC)
                    for layer, (full, part) in enumerate(((hb_f, hb_h), (ha_f, ha_h))):
                        for c in range(HC):
                            q = 2 * HC * n + HC * layer + c + 1
                            act.wait_ge(d2_ps, q)
                            act.activation(full[:, c, :], ps[:, 6 + c % 2, :], ACT.Gelu,
                                           scale=sc1[:, 2 + layer, c:c + 1]).then_inc(g_r, 1)
                            high(c, full, part, g_r, q)
                    if ahead:
                        turn(n + 1)

                turn(0)
                with act.Fori(0, NG - 1) as n:
                    group(n, True)
                group(NG - 1, False)

            act.wait_ge(fl_r, 1)
            long = act.value_load(flag[:].bitcast(I32))
            with act.If(long == 0):
                stage_d(True)
            with act.Else():
                for n in REST + ["h2"]:
                    act.dma_start(mlp_f[n], d[n]).then_inc(again_in, 16)
                stage_d(False)

        @block.vector
        def _(dve):
            st = Steps(dve, dstep)

            def wait_alone(s, value):
                if not isinstance(value, int):
                    dve.compute_val(value)
                dve.wait_ge(const_ready, 3)
                dve.wait_ge(s, value)

            def steps_alone():
                wait_alone(st.s, st.start + st.n)

            def measure(tile, k):
                st.mark(dve.bn_stats(stat[:, k, :], of(x, tile)))

            def aggregate(t0, n, k):
                steps_alone()
                for j in range(n):
                    st.mark(dve.bn_aggr(agg[:, k + j, :], stat[:, k + j, :]))
                steps_alone()
                dve.tensor_copy(mv[:, bass.ds(t0, n), :], agg[:, k:k + n, :]).then_inc(stats, 1)

            def normalise(tile, dst):
                dve.tensor_scalar(dst, of(x, tile), mv[:, bass.ds(tile, 1), 0:1].rearrange("p o c -> p (o c)"),
                                  rstd[:, bass.ds(tile, 1)], ALU.subtract, ALU.mult).then_inc(xn_r, 1)

            dve.memset(ones[:], 1.0).then_inc(const_ready, 1)
            dve.memset(eps_t[:], EPS).then_inc(const_ready, 1)
            dve.memset(half_t[:], -0.5).then_inc(const_ready, 1)
            dve.memset(onec[:], 1.0).then_inc(const_ready, 1)
            dve.memset(VV[64:LP], 0.0).then_inc(zero_ready, 1)
            dve.memset(yk[64:LP], 0.0).then_inc(zero_ready, 1)
            dve.wait_ge(zero_ready, 2)
            dve.wait_ge(small_in, N_SMALL)
            dve.wait_ge(gate_ready, 1)
            st.link(dve.tensor_scalar(gh[:], gt[:, 0:1], 0.5, None, ALU.mult))
            st.link(dve.tensor_scalar(sc3[:], sc3[:], gt[:, 3:4], None, ALU.mult))
            st.link(dve.tensor_scalar(keep[:], maskT[:], -1.0, 1.0, ALU.mult, ALU.add))
            st.mark(dve.tensor_scalar(mcol[:], maskT[:], FAR, None, ALU.mult))
            for b in range(B):
                st.mark(dve.tensor_scalar(yk[0:L, b, 0:D], ctxr[:, b, :], keep[:, b:b + 1], None, ALU.mult))
                st.mark(dve.tensor_copy(yk[0:L, b, D:D + 1], keep[:, b:b + 1]))
            for n, (dst, bias) in enumerate(((KT, "bk_s"), (QT, "bq_s"), (VT, "bv_s"))):
                for m in range(KC):
                    dve.wait_ge(proj, 2 * n + m + 1)
                    dve.tensor_scalar(dst[:, m, :], ps[:, 2 * n + m, 0:BL], col(bias, m), None, ALU.add
                                      ).then_inc(proj_v, 1)
            for n, dst in enumerate((A1, A2)):
                for m in range(KC):
                    dve.wait_ge(map_ps, 2 * n + m + 1)
                    dve.tensor_scalar(dst[:, m, :], ps[:, 2 * n + m, 0:BL], SCALE, None, ALU.mult).then_inc(map_v, 1)
            for n, (bank, dst) in enumerate(((4, c1), (5, c2))):
                dve.wait_ge(map_ps, 5 + n)
                dve.tensor_scalar(dst[:], ps[0:L, bank, 0:B], SCALE, None, ALU.mult).then_inc(map_v, 1)
            for b in range(B):
                dve.wait_ge(val_ps, b + 1)
                dve.tensor_scalar(VV[0:L, b, 0:D], ps[0:L, 6 + b % 2, 0:D], gh[0:L, 0:1], None, ALU.mult
                                  ).then_inc(val_v, 1)
                dve.tensor_copy(VV[0:L, b, D:2 * D], ps[0:L, 6 + b % 2, D:2 * D]).then_inc(val_v, 1)
            for b in range(B):
                if b:
                    for e in range((b - 1) * 3, min(b * 3, E)):
                        dve.wait_ge(ex_h, e + 1)
                        dve.tensor_tensor(wexp_l[:, :, e * D:(e + 1) * D],
                                          ps[:, e % 4, :].rearrange("p (m c) -> p m c", m=KC),
                                          wexp_h[:, :, e * D:(e + 1) * D].bitcast(F32), ALU.subtract
                                          ).then_inc(ex_l, 1)
                dve.wait_ge(x_in[b], 16)
                for j in range(JT):
                    measure(b * JT + j, j)
                aggregate(b * JT, JT, 0)
            dve.wait_ge(ex_ps, E)
            dve.memset(P1T[64:LP], 0.0).then_inc(zero_ready, 1)
            dve.memset(SS[64:LP], 0.0).then_inc(zero_ready, 1)
            dve.wait_ge(zero_ready, 4)
            dve.wait_ge(map_v, 6)

            def a_start(c):
                st.mark(dve.tensor_copy(c1b[:], c1[:, bass.ds(c, 1)]))
                st.wait()
                dve.tensor_copy(A1b[:], A1[:, :, bass.ds(c * L, L)]).then_inc(map_b, 1)
                dve.tensor_copy(A2b[:], A2[:, :, bass.ds(c * L, L)]).then_inc(map_b, 1)
                for j in range(JT):
                    normalise(c * JT + j, xn[:, j, :])

            def a_max_back(c):
                dve.wait_ge(s2_ps, c + 1)
                st.link(dve.tensor_reduce(mx2[:, 0:1], ps[0:L, 6:8, :], mybir.AxisListType.XY, ALU.max))
                st.link(dve.tensor_scalar(mx2[:, 1:2], mx2[:, 0:1], c2[:, bass.ds(c, 1)], None, ALU.add))
                dve.tensor_tensor(mx2[:, 2:3], c2[:, bass.ds(c, 1)], mx2[:, 1:2], ALU.subtract).then_inc(s2_b, 1)

            def a_max(c):
                for q in range(2):
                    dve.wait_ge(s1b_ps, 2 * c + (q + 1))
                    dve.tensor_reduce(nm1[:, q * G:(q + 1) * G],
                                      ps[:, 4 + q, 0:G * L].rearrange("p (j c) -> p j c", j=G), X, ALU.max,
                                      negate=True).then_inc(nm_r, 1)

            def a_probs_back_T(c):
                for q in range(2):
                    dve.wait_ge(p2t_ps, 2 * c + (q + 1))
                    dve.tensor_copy(P2T[:, q * G:(q + 1) * G, :],
                                    ps[:, 6 + q, 0:G * L].rearrange("p (j c) -> p j c", j=G)).then_inc(p2t_v, 1)
                st.link(dve.tensor_tensor(rs2[:, 2:3], rs2[:, 0:1], rs2[:, 1:2], ALU.add))
                st.link(dve.reciprocal(rs2[:, 3:4], rs2[:, 2:3]))

            def a_pool(c):
                for q in range(2):
                    dve.wait_ge(e1_r, c * JT + (q + 1) * G)
                    st.link(dve.reciprocal(ri1[:, q * G:(q + 1) * G], rs1[:, q * G:(q + 1) * G]))
                    for j in range(q * G, (q + 1) * G):
                        dve.tensor_scalar(E1[:, j, :], E1[:, j, :], ri1[:, j:j + 1], None, ALU.mult).then_inc(e1n, 1)
                dve.wait_ge(r2_ps, c + 1)
                dve.tensor_scalar(r2n[:], ps[0:L, 6, 0:D], rs2[:, 3:4], None, ALU.mult).then_inc(r2_v, 1)

            def a_pooled_T(c):
                dve.wait_ge(t2_ps, c + 1)
                dve.tensor_copy(t2T[:], ps[:, 7, 0:KC * L].rearrange("p (k c) -> p k c", k=KC)).then_inc(t2_v, 1)

            def a_sub2char(c):
                dve.wait_ge(st_ps, c + 1)
                for m in range(KC):
                    dve.tensor_scalar(sT[:, m, :], ps[:, 7, m * L:(m + 1) * L], col("bv_c", m), None, ALU.add
                                      ).then_inc(st_v, 1)
                dve.wait_ge(so_ps, c + 1)
                dve.tensor_scalar(SS[0:L, bass.ds(c, 1), 0:D].rearrange("p o c -> p (o c)"), ps[0:L, 6, 0:D],
                                  gh[0:L, 0:1], None, ALU.mult).then_inc(so_v, 1)

            def a_sub2char_gate(c):
                dve.wait_ge(sg_ps, c + 1)
                dve.tensor_copy(SS[0:L, bass.ds(c, 1), D:2 * D].rearrange("p o c -> p (o c)"), ps[0:L, 7, 0:D]
                                ).then_inc(sg_v, 1)

            def a_sum(b, j):
                q = j % 2
                dve.wait_ge(th_r, b * JT + (j + 1))
                if j >= 2:
                    wait_alone(xupd, b * JT + (j - 1))
                st.link(dve.tensor_tensor(u1[:, q, :], ps[:, q, 0:D], ssb[:, q, :], ALU.subtract))
                st.link(dve.scalar_tensor_tensor(u1[:, q, :], th[:, q, :], 1.0, u1[:, q, :], ALU.add, ALU.mult))
                dve.scalar_tensor_tensor(u1[:, q, :], ssb[:, q, :], 2.0, u1[:, q, :], ALU.mult, ALU.add
                                         ).then_inc(up_r, 1)
                if j >= 2:
                    measure(b * JT + (j - 2), j - 2)
                if j == G + 1:
                    aggregate(b * JT, G, 0)
                if j == JT - 1:
                    for i in range(JT - 2, JT):
                        wait_alone(xupd, b * JT + (i + 1))
                        measure(b * JT + i, i)
                    aggregate(b * JT + G, G, G)

            def nothing(c):
                pass

            steps = [nothing, nothing, a_max_back, nothing, a_max, a_probs_back_T, a_pool, a_pooled_T,
                     a_sub2char, nothing, a_sub2char_gate]
            dve.wait_ge(inv, B)
            a_start(0)
            for f in steps:
                f(0)
            with dve.Fori(1, B) as c:
                st.enter(c - 1, A_STEPS)
                a_start(c)
                weave(c, a_sum, steps)
            st.leave(B - 1)
            for j in range(JT):
                a_sum(B - 1, j)

            st.link(dve.tensor_copy(wrh[:], wr[:]))
            st.link(dve.tensor_tensor(wrl[:], wr[:], wrh[:].bitcast(F32), ALU.subtract))
            dve.memset(lg[:, 0:2, :], FAR).then_inc(y_free, 1)
            dve.memset(lg[:, 2:4, :], FAR).then_inc(y_free, 1)
            dve.memset(want[:, 0:2, :], FAR).then_inc(y_free, 1)
            dve.memset(want[:, 2:4, :], FAR).then_inc(y_free, 1)
            dve.wait_ge(y_free, 4)

            def b_norm(g, s):
                dve.wait_ge(tp, NT - G + G * g)
                for j in range(G):
                    normalise(G * g + j, xn[:, s * G + j, :])

            def b_low(g, s):
                for j in range(G):
                    dve.wait_ge(xh_r, G * g + j + 1)
                    t = slice(j * P, (j + 1) * P)
                    dve.tensor_tensor(xTl[:, s, :, t], ps[:, j % 2, 0:D].rearrange("p (k c) -> p k c", k=KC),
                                      xTh[:, s, :, t].bitcast(F32), ALU.subtract).then_inc(xT_r, 1)

            def b_route(g, s):
                dve.wait_ge(rb_ps, g + 1)
                st.mark(dve.tensor_copy(lg[:, :, 0:E], ps[:, 3, 0:G * E].rearrange("p (j e) -> p j e", j=G)))
                steps_alone()
                for j in range(G):
                    st.mark(dve.max(top[:, j, :], lg[:, j, 0:E]))
                st.wait()
                dve.tensor_tensor(lsub[:], lg[:, :, 0:E], top[:, :, 0:1].broadcast_to([P, G, E]), ALU.subtract
                                  ).then_inc(lg_r, 1)
                st.mark(dve.tensor_copy(want[:, :, 0:2], top[:, :, 0:2]))
                steps_alone()
                for j in range(G):
                    st.mark(dve.match_replace(marked[:, j, :], want[:, j, :], lg[:, j, :], TAKEN))
                dve.wait_ge(ee_r, g + 1)
                st.link(dve.tensor_reduce(sme[:], pex[:], X, ALU.add))
                st.mark(dve.scalar_tensor_tensor(pm[:], marked[:, :, 0:E], TAKEN, pex[:], ALU.is_ge, ALU.mult))
                st.link(dve.reciprocal(rie[:], sme[:]))
                st.link(dve.tensor_scalar(rig[:], rie[:], gt[:, 2:3], None, ALU.mult))
                st.link(dve.tensor_tensor(coef[:, s], pm[:], rig[:].unsqueeze(2).broadcast_to([P, G, E]), ALU.mult))

            def b_add(g, s, j):
                t = G * g + j
                for pair in range(E // 2):
                    dve.wait_ge(y_ps, 4 * t + pair + 1)
                    for h in range(2):
                        e = 2 * pair + h
                        ins = dve.scalar_tensor_tensor(of(x, t), ps[:, 4 + pair, h * D:(h + 1) * D],
                                                       coef[:, s, j, e:e + 1], of(x, t), ALU.mult, ALU.add)
                        if h == 0:
                            st.link(ins)
                        else:
                            ins.then_inc(y_free, 1)
                            wait_alone(y_free, 4 * t + pair + 5)
                measure(t, j)

            def b_group(g, s, ahead):
                if ahead:
                    b_norm(g + 1, 1 - s)
                b_add(g, s, 0)
                if ahead:
                    b_low(g + 1, 1 - s)
                b_add(g, s, 1)
                b_add(g, s, 2)
                if ahead:
                    b_route(g + 1, 1 - s)
                b_add(g, s, 3)
                aggregate(G * g, G, 0)

            dve.wait_ge(inv, INV_A)
            b_norm(0, 0)
            b_low(0, 0)
            b_route(0, 0)
            with dve.Fori(0, NG // 2 - 1) as i:
                st.enter(i, 2 * B_STEPS)
                b_group(2 * i, 0, True)
                b_group(2 * i + 1, 1, True)
            st.leave(NG // 2 - 1)
            b_group(NG - 2, 0, True)
            b_group(NG - 1, 1, False)

            def c_batch(b):
                st.link(dve.tensor_copy(mcolb[:], mcol[:, bass.ds(b, 1)]))
                dve.tensor_copy(yTb[:], ypT[:, :, bass.ds(b * L, L)]).then_inc(yb_r, 1)

            def c_norm(g, s):
                dve.wait_ge(tp, 2 * NT - G + G * g)
                for j in range(G):
                    normalise(G * g + j, xn[:, s * G + j, :])

            def c_max(g):
                dve.wait_ge(sb_ps, g + 1)
                dve.tensor_reduce(nmc[:], ps[:, 5, 0:G * L].rearrange("p (j c) -> p j c", j=G), X, ALU.max,
                                  negate=True).then_inc(mc_r, 1)

            def c_group(g, s, ahead, b_next):
                if ahead:
                    c_norm(g + 1, 1 - s)
                c_max(g)
                if b_next is not None:
                    dve.wait_ge(sc_s, g + 1)
                    c_batch(b_next)
                dve.wait_ge(pt_ps, g + 1)
                dve.tensor_copy(PT[0:L, :], ps[0:L, 6, :]).then_inc(pt_r, 1)
                for j in range(G):
                    t = G * g + j
                    q = j % 2
                    dve.wait_ge(o_ps, t + 1)
                    st.link(dve.reciprocal(ric[:, j:j + 1], ps[:, 6 + q, D:D + 1]))
                    st.link(dve.tensor_scalar(rcg[:, j:j + 1], ric[:, j:j + 1], gt[:, 1:2], None, ALU.mult))
                    dve.scalar_tensor_tensor(of(x, t), ps[:, 6 + q, 0:D], rcg[:, j:j + 1], of(x, t),
                                             ALU.mult, ALU.add).then_inc(xupd, 1)
                    if j:
                        wait_alone(xupd, XUPD_A + t)
                        measure(t - 1, j - 1)
                wait_alone(xupd, XUPD_A + G + G * g)
                measure(G * g + G - 1, G - 1)
                aggregate(G * g, G, 0)

            dve.wait_ge(inv, INV_B)
            dve.memset(PT[64:LP], 0.0).then_inc(zero_ready, 1)
            dve.wait_ge(zero_ready, 5)
            c_batch(0)
            c_norm(0, 0)
            with dve.Fori(0, B - 1) as b:
                st.enter(b, C_STEPS)
                c_group(2 * b, 0, True, None)
                c_group(2 * b + 1, 1, True, b + 1)
            st.leave(B - 1)
            c_group(NG - 2, 0, True, None)
            c_group(NG - 1, 1, False, None)
            dve.wait_ge(ck_r, 2 * NCHECK)
            dve.tensor_reduce(lowcol[:], lowsum[:], X, ALU.add).then_inc(fl_v, 1)

            def stage_d(short):
                def norm(n):
                    for j in range(G):
                        normalise(G * n + j, xd[:, j, :])

                def low_turn(n):
                    if short:
                        for j in range(G):
                            dve.wait_ge(xh_r, NT + G * n + j + 1)
                            t = slice(j * P, (j + 1) * P)
                            dve.tensor_tensor(xdT_l[:, :, t], ps[:, j % 2, 0:D].rearrange("p (k c) -> p k c", k=KC),
                                              xdT_h[:, :, t].bitcast(F32), ALU.subtract).then_inc(xT_r, 1)

                def low(c, full, part, rest, n_high):
                    if short:
                        dve.wait_ge(hi_r, n_high)
                        dve.tensor_tensor(rest[:, c, :], full[:, c, :], part[:, c, :].bitcast(F32), ALU.subtract
                                          ).then_inc(lo_r, 1)

                def update(n, j):
                    dve.wait_ge(d4_ps, G * n + j + 1)
                    dve.wait_ge(xupd, XUPD_C - 1 + j + G * n)
                    dve.tensor_tensor(ud[:, j % 2, :], ps[:, 2 + j, 0:D], sc3[:], ALU.mult).then_inc(up_r, 1)

                def group(n, ahead):
                    for c in range(HC):
                        dve.wait_ge(sil_r, HC * n + c + 1)
                        dve.scalar_tensor_tensor(ha_f[:, c, :], ps[:, 3 + 2 * (c % 2), :], sc1[:, 1, c:c + 1],
                                                 ha_f[:, c, :], ALU.mult, ALU.mult).then_inc(h_r, 1)
                        if c:
                            low(c - 1, ha_f, ha_h, ha_l, 3 * HC * n + c)
                    low(HC - 1, ha_f, ha_h, ha_l, 3 * HC * n + HC)
                    for layer, (full, part, rest) in enumerate(((hb_f, hb_h, hb_l), (ha_f, ha_h, ha_l))):
                        for c in range(HC):
                            low(c, full, part, rest, 3 * HC * n + HC * (layer + 1) + c + 1)
                    if ahead:
                        dve.wait_ge(d2_ps, 2 * HC * n + 2 * HC)
                        norm(n + 1)
                    update(n, 0)
                    update(n, 1)
                    if ahead:
                        low_turn(n + 1)
                    update(n, 2)
                    update(n, 3)

                norm(0)
                low_turn(0)
                with dve.Fori(0, NG - 1) as n:
                    group(n, True)
                group(NG - 1, False)

            dve.wait_ge(inv, INV_C)
            dve.wait_ge(fl_r, 1)
            long = dve.value_load(flag[:].bitcast(I32))
            with dve.If(long == 0):
                stage_d(True)
            with dve.Else():
                stage_d(False)

        @block.gpsimd
        def _(pool):
            st = Steps(pool, pstep)

            def invert(t0, n, n_stats):
                pool.wait_ge(stats, n_stats)
                v = mv[:, bass.ds(t0, n), 1:2].rearrange("p t o -> p (t o)")
                st.link(pool.tensor_tensor(veps[:, bass.ds(t0, n)], v, eps_t[:, 0:n], ALU.add))
                pool.tensor_tensor(rstd[:, bass.ds(t0, n)], veps[:, bass.ds(t0, n)], half_t[:, 0:n], ALU.pow
                                   ).then_inc(inv, 1)

            pool.wait_ge(const_ready, 3)
            for b in range(B):
                invert(b * JT, JT, b + 1)
            with pool.Fori(0, B) as b:
                st.enter(b, 2)
                for j in range(JT):
                    pool.wait_ge(up_r, b * JT + (j + 1))
                    xt = of(x, b * JT + j)
                    pool.tensor_tensor(xt, xt, u1[:, j % 2, :], ALU.add).then_inc(xupd, 1)
                    if j == JT - 2:
                        invert(b * JT, G, 2 * b + B + 1)
                invert(b * JT + G, G, 2 * b + B + 2)
            st.leave(B)
            with pool.Fori(0, 2 * NG) as i:
                st.enter(i, 1)
                pool.wait_ge(stats, STATS_A + 1 + i)
                t0 = G * (i % NG)
                invert(t0, G, STATS_A + 1 + i)
            st.leave(2 * NG)
            with pool.Fori(0, NG) as n:
                for j in range(G):
                    pool.wait_ge(up_r, UP_A + 1 + G * n + j)
                    xt = of(x, G * n + j)
                    pool.tensor_tensor(xt, xt, ud[:, j % 2, :], ALU.add).then_inc(xupd, 1)


INV_A = B + 2 * B
INV_B = INV_A + NG
INV_C = INV_B + NG
A_STEPS = 1 + 2 + 2 + 2 + 2 * JT + JT + JT
B_STEPS = 1 + G + 1 + G + 1 + 1 + 1 + 1 + 1 + 4 * G + G + G
C_STEPS = 2 * (2 * G + G + G) + 1


def interpolation():
    pos = (np.arange(S, dtype=np.float32) + np.float32(0.5)) * np.float32(L / S) - np.float32(0.5)
    pos = np.clip(pos, np.float32(0), np.float32(L - 1))
    lo = np.floor(pos).astype(np.int32)
    hi = np.minimum(lo + 1, L - 1)
    w = (pos - lo.astype(np.float32)).astype(np.float32)
    m = np.zeros((LP, S), np.float32)
    np.add.at(m, (lo, np.arange(S)), 1 - w)
    np.add.at(m, (hi, np.arange(S)), w)
    return np.ascontiguousarray(m.reshape(LP, P, JT).transpose(0, 2, 1).reshape(LP, S))


def kernel(**inputs):
    import concourse.bacc as bacc
    from concourse.bass_utils import run_bass_kernel_spmd as run

    a = {k: np.asarray(v) for k, v in inputs.items()}

    def chunks(w):
        return np.ascontiguousarray(w.reshape(-1, P, w.shape[-1]).transpose(1, 0, 2))

    def column(v):
        return np.ascontiguousarray(v.reshape(-1, P).T)

    pre = "L0_xattn_"
    wg = a[pre + "Wg"]
    weights = {"Wk_sT": a[pre + "Wk_s"].T, "Wq_sT": a[pre + "Wq_s"].T, "Wv_sT": a[pre + "Wv_s"].T,
               "Wq_c": a[pre + "Wq_c"], "Wk_c": a[pre + "Wk_c"], "Wv_cT": a[pre + "Wv_c"].T,
               "WgT0": wg[:, :D].T, "WgT1": wg[:, D:].T, "W1T": a["L1_xattn_W"].T}
    vectors = {n: a[pre + n] for n in COLS[:-1] + ["bg"]} | {"b1": a["L1_xattn_b"]}
    mask = a["mask_BxS2_bf0"]
    ctxt = a["ctx_1024"]
    f = "L1_ffn_"
    arrays = {
        "x": a["x"],
        "aw": np.stack([chunks(weights[n]) for n in AW], 1),
        "ctxT": chunks(ctxt.reshape(B * L, D).T),
        "ctx": np.ascontiguousarray(ctxt.transpose(1, 0, 2)),
        "cols": np.stack([column(vectors[n]) for n in COLS], 1),
        "rows": np.stack([vectors[n] for n in ROWS])[None],
        "ident": np.eye(P, dtype=np.float32),
        "maskT": np.ascontiguousarray(mask.T),
        "Wr": chunks(a["L0_ffn_Wr"]),
        "scales": np.stack([column(a[f + n]) for n in ("w1_s", "w2_s", "h1_s", "h2_s")], 1),
        "gates": np.concatenate([a["g_xattn"], a["g_ffn"]]),
        "w3_s": a[f + "w3_s"],
        "interp": interpolation(),
        "Wi": np.ascontiguousarray(a["L0_ffn_Wi"].transpose(2, 0, 1).reshape(KC, P, E, D).transpose(1, 0, 2, 3)),
        "Wo": np.ascontiguousarray(a["L0_ffn_Wo"].transpose(1, 0, 2).reshape(KC, P, E, D).transpose(1, 0, 2, 3)),
        "w1": chunks(a[f + "w1_w"].T), "w2": chunks(a[f + "w2_w"].T),
        "h1": chunks(a[f + "h1_w"].T), "h2": chunks(a[f + "h2_w"].T), "w3": chunks(a[f + "w3_w"].T),
    }
    nc = bacc.Bacc("TRN2", target_bir_lowering=False, num_devices=1)
    d = {n: nc.dram_tensor("in_" + n, v.shape, mybir.dt.from_np(v.dtype), kind="ExternalInput").ap()
         for n, v in arrays.items()}
    d["out"] = nc.dram_tensor("out", (NG, P, G, D), F32, kind="ExternalOutput").ap()
    program(nc, d)
    r = run(nc, [{"in_" + n: v for n, v in arrays.items()}], core_ids=[0])
    out = r.results[0]["out"].reshape(B, JT // G, P, G, D).transpose(0, 2, 1, 3, 4)
    return np.ascontiguousarray(out.reshape(B, S, D))
```

```python
from contextlib import ExitStack

import numpy as np

import concourse.bass as bass
from concourse import mybir

F32 = mybir.dt.float32
F32R = mybir.dt.float32r
BF16 = mybir.dt.bfloat16
I32 = mybir.dt.int32
U8 = mybir.dt.uint8
U16 = mybir.dt.uint16
ALU = mybir.AluOpType
ACT = mybir.ActivationFunctionType
X = mybir.AxisListType.X

P = 128
B, S, D, L = 4, 1024, 256, 77
KC = D // P
JT = S // P
NT = B * JT
G = 4
NG = NT // G
GN = G * P
E = 8
HID = 1024
HC = HID // P
BL = B * L
NW = (2 * KC + 2 * HC) * HID + HC * D
SLICE = 2048
REST_SLICES = (NW - HC * HID) // SLICE
NCHECK = NW // SLICE
EPS = 1e-5
FAR = -3.0e38
TAKEN = 3.0e38
SCALE = float(D) ** -0.5

LP = 96
COLS = ["bk_s", "bq_s", "bv_s", "bv_c", "bq_c", "bk_c", "b1"]
ROWS = ["bv_s", "bg", "bv_c"]
REST = ["w1", "w2", "w3", "h1"]
AW = ["Wk_sT", "Wq_sT", "Wv_sT", "W1T", "Wq_c", "Wk_c", "Wv_cT", "WgT0", "WgT1"]

EXPERTS_AFTER = {0: (0, 1), 1: (2, 3), 2: (4, 5), 3: (6,), 4: (7,)}

TILE_BEFORE = (0, 1, 4, 5, 6, 8, 8, 9)

XUPD_A = NT
STATS_A = 2 * B + B
UP_A = NT


def program(nc, d):
    ctx = ExitStack()
    with ctx:
        base = -(-nc.sbuf_base // 32) * 32
        room = {"x": (0, 32768), "small": (32768, 40960), "weights": (40960, 131072),
                "work": (131072, 212800)}
        cursor = {k: v[0] for k, v in room.items()}
        bytes_of = {U8: 1, U16: 2, BF16: 2}

        def place(region, name, shape, dt=F32, at=None):
            size = int(np.prod(shape[1:])) * bytes_of.get(dt, 4)
            size = -(-size // 32) * 32
            start = cursor[region] if at is None else at
            assert start + size <= room[region][1], (name, start + size)
            cursor[region] = start + size
            return nc.alloc_sbuf_tensor_at(name, shape, dt, offset=base + start)

        def sem(name):
            return ctx.enter_context(nc.semaphore(name))

        x = place("x", "x_residual", [P, NT, D])

        ident = place("small", "identity", [P, P])
        stat = place("small", "ln_stats", [P, JT, 6])
        agg = place("small", "ln_aggregate", [P, JT, 2])
        mv = place("small", "ln_mean_var", [P, NT, 2])
        veps = place("small", "ln_var_eps", [P, NT])
        rstd = place("small", "ln_rstd", [P, NT])
        eps_t = place("small", "eps", [P, JT])
        half_t = place("small", "minus_half", [P, JT])
        graw = place("small", "gates_raw", [P, 4])
        gt = place("small", "gates_tanh", [P, 4])
        gh = place("small", "gate_half", [P, 1])
        cols = place("small", "bias_columns", [P, len(COLS), KC])
        sc1 = place("small", "mlp_scales", [P, 4, HC])
        sc3 = place("small", "mlp_out_scale", [P, D])
        nmc = place("small", "neg_max_c", [P, G])
        ric = place("small", "inv_sum_c", [P, G])
        onec = place("small", "ones_column", [P, 1])
        lowsum = place("small", "low_half_sums", [P, NCHECK])
        lowcol = place("small", "low_half_sum", [P, 1])
        flag = place("small", "weights_not_short", [1, 1])

        wexp_h = place("weights", "expert_high", [P, KC, E * D], F32R)
        wexp_l = place("weights", "expert_low", [P, KC, E * D], F32R)
        wi_at = cursor["weights"]
        wi = place("weights", "expert_in", [P, KC, E, D])
        wo_at = cursor["weights"]
        wo = place("weights", "expert_out", [P, KC, E, D])
        KT = place("weights", "keys_T", [P, KC, BL])
        QT = place("weights", "queries_T", [P, KC, BL])
        VV = place("weights", "values_and_gate", [LP, B, 2 * D])
        IT = place("weights", "interpolation_T", [LP, S])
        mx2 = place("weights", "max_back", [L, 4])
        rs2 = place("weights", "sum_back", [L, 4])
        nm1 = place("weights", "neg_max", [P, JT])
        rs1 = place("weights", "sum_probs", [P, JT])
        ri1 = place("weights", "inv_sum", [P, JT])
        r2n = place("weights", "pooled", [L, D])
        t2T = place("weights", "pooled_T", [P, KC, L])
        sT = place("weights", "sub2char_T", [P, KC, L])
        E1 = place("weights", "probs", [P, JT, L], at=wi_at)
        P2T = place("weights", "probs_back_T", [P, JT, L])
        th = place("weights", "gate_tanh", [P, 2, D])
        ssb = place("weights", "sub2char_of_tile", [P, 2, D])
        u1 = place("weights", "update", [P, 2, D])
        P1T = place("weights", "probs_T", [LP, S], at=wo_at)
        SS = place("weights", "sub2char_and_gate", [LP, B, 2 * D])
        h2_at, rest_at = room["weights"][0], wi_at
        n_h2, n_rest = HC * HID, NW - HC * HID
        h2_raw = place("weights", "mlp_h2", [P, n_h2], at=h2_at)
        h2_round = place("weights", "mlp_h2_rounded", [P, n_h2], F32R, at=h2_at)
        rest_raw = place("weights", "mlp_rest", [P, n_rest], at=rest_at)
        rest_round = place("weights", "mlp_rest_rounded", [P, n_rest], F32R, at=rest_at)
        mlp_f, mlp_r, at = {}, {}, 0
        for n, rows_k, width in (("w1", KC, HID), ("w2", KC, HID), ("h1", HC, HID), ("w3", HC, D)):
            for into, t in ((mlp_f, rest_raw), (mlp_r, rest_round)):
                into[n] = t[:, at:at + rows_k * width].rearrange("p (k c) -> p k c", k=rows_k)
            at += rows_k * width
        for into, t in ((mlp_f, h2_raw), (mlp_r, h2_round)):
            into["h2"] = t[:].rearrange("p (k c) -> p k c", k=HC)
        assert n_h2 * 4 <= wi_at - h2_at and n_rest % SLICE == 0 and n_h2 % SLICE == 0

        wk = room["work"][0]
        rows = place("work", "bias_rows", [L, len(ROWS), D])
        aw_at = cursor["work"]
        aw = place("work", "attention_weights", [P, len(AW), KC, D])
        yk = place("work", "context_kept", [LP, B, D + 1])
        yTb = place("work", "context_projected_of_batch", [P, KC, L])
        mcolb = place("work", "mask_bias_of_batch", [L, 1])
        dead_at = cursor["work"]
        ctxT = place("work", "context_T", [P, KC, BL])
        ctxr = place("work", "context", [L, B, D])
        VT = place("work", "values_T", [P, KC, BL])
        A1 = place("work", "score_map", [P, KC, BL])
        A2 = place("work", "score_map_back", [P, KC, BL])
        maskT = place("work", "mask_T", [L, B], U8)
        keep = place("work", "keep", [L, B])
        mcol = place("work", "mask_bias", [L, B])
        ypT = place("work", "context_projected_T", [P, KC, BL])
        A1b = place("work", "score_map_of_batch", [P, KC, L])
        A2b = place("work", "score_map_back_of_batch", [P, KC, L])
        c1 = place("work", "score_bias", [L, B])
        c2 = place("work", "score_bias_back", [L, B])
        c1b = place("work", "score_bias_of_batch", [L, 1])
        dump = place("work", "examined", [P, SLICE], BF16)
        xn = place("work", "x_normalised", [P, JT, D])
        xt_at = cursor["work"]
        xnT = place("work", "x_normalised_T", [P, KC, S])
        s1s = place("work", "scores_T", [L, S])
        P2 = place("work", "probs_back", [L, S])
        xTh = place("work", "x_T_high", [P, 2, KC, GN], F32R, at=xt_at)
        xTl = place("work", "x_T_low", [P, 2, KC, GN], F32R)
        wr = place("work", "router", [P, KC, E])
        wrh = place("work", "router_high", [P, KC, E], F32R)
        wrl = place("work", "router_low", [P, KC, E], F32R)
        lgT = place("work", "logits_T", [E, GN])
        lg = place("work", "logits", [P, G, 2 * E])
        top = place("work", "top8", [P, G, E])
        want = place("work", "to_mark", [P, G, E])
        marked = place("work", "marked", [P, G, 2 * E])
        lsub = place("work", "logits_less_max", [P, G, E])
        pex = place("work", "expert_exp", [P, G, E])
        sme = place("work", "expert_sum", [P, G])
        rie = place("work", "expert_inv", [P, G])
        rig = place("work", "expert_inv_gated", [P, G])
        pm = place("work", "expert_masked", [P, G, E])
        coef = place("work", "expert_weight", [P, 2, G, E])
        EC = place("work", "probs_c", [P, G, L], at=aw_at)
        PT = place("work", "probs_c_T", [LP, GN])
        assert cursor["work"] <= aw_at + AW.index("W1T") * KC * D * 4
        xcT = place("work", "x_norm_c_T", [P, KC, GN], at=aw_at + (AW.index("W1T") + 1) * KC * D * 4)
        xpT = place("work", "x_projected_T", [P, KC, GN])
        scT = place("work", "scores_c_T", [L, GN])
        assert cursor["work"] <= dead_at
        xnc = place("work", "x_norm_c", [P, G, D], at=dead_at)
        h2_part = place("work", "mlp_h2_slice", [P, SLICE])
        hb_h = place("work", "hidden_b_high", [P, HC, GN], F32R, at=wk)
        hb_at = cursor["work"]
        hb_l = place("work", "hidden_b_low", [P, HC, GN], F32R)
        ha_at = cursor["work"]
        xd = place("work", "x_norm_d", [P, G, D], at=ha_at - G * D * 4)
        assert dead_at + G * D * 4 <= ha_at and dead_at <= ha_at - G * D * 4
        hb_f = place("work", "hidden_b", [P, HC, GN], at=hb_at)
        ha_h = place("work", "hidden_a_high", [P, HC, GN], F32R)
        hal_at = cursor["work"]
        ha_l = place("work", "hidden_a_low", [P, HC, GN], F32R)
        ha_f = place("work", "hidden_a", [P, HC, GN], at=hal_at)
        xdT_h = place("work", "x_norm_d_T_high", [P, KC, GN], F32R)
        xdl_at = cursor["work"]
        xdT_l = place("work", "x_norm_d_T_low", [P, KC, GN], F32R)
        xdT_f = place("work", "x_norm_d_T", [P, KC, GN], at=xdl_at)
        ud = place("work", "update_d", [P, 2, D])

        ps = ctx.enter_context(nc.psum_tensor("psum", [P, 8, 512], F32))

        ctx_in = sem("context_T_loaded")
        aw0_in = sem("first_weight_loaded")
        small_in = sem("small_inputs_loaded")
        aw1_in = sem("projection_weights_loaded")
        aw2_in = sem("map_weights_loaded")
        it_in = sem("interpolation_loaded")
        x_in = [sem(f"x_loaded_{b}") for b in range(B)]
        exp_in = sem("expert_weights_loaded")
        rest_in = sem("mlp_rest_loaded")
        h2_in = sem("mlp_h2_loaded")
        again_in = sem("mlp_weights_loaded_again")
        out_done = sem("output_stored")
        gate_ready = sem("gates_ready")
        const_ready = sem("constants_ready")
        zero_ready = sem("zero_rows_ready")
        dstep = sem("vector_step_done")
        pstep = sem("pool_step_done")
        proj = sem("projection_in_psum")
        proj_v = sem("projection_saved_by_vector")
        proj_s = sem("projection_saved_by_scalar")
        map_ps = sem("score_maps_in_psum")
        map_v = sem("score_maps_saved")
        val_ps = sem("values_in_psum")
        val_v = sem("values_saved")
        ex_ps = sem("expert_product_in_psum")
        ex_h = sem("expert_high_saved")
        ex_l = sem("expert_low_saved")
        stats = sem("ln_stats_ready")
        inv = sem("ln_rstd_ready")
        xn_r = sem("x_normalised_ready")
        tp = sem("x_transposed_in_psum")
        xT_r = sem("x_transposed_saved")
        xupd = sem("x_updated")
        map_b = sem("maps_of_batch_copied")
        s2_ps = sem("scores_back_in_psum")
        s2_b = sem("scores_back_bias_ready")
        p2_r = sem("probs_back_ready")
        s1_ps = sem("scores_T_in_psum")
        s1_s = sem("scores_T_saved")
        s1b_ps = sem("scores_in_psum")
        nm_r = sem("neg_max_ready")
        e1_r = sem("probs_ready")
        e1n = sem("probs_normalised")
        p2t_ps = sem("probs_back_T_in_psum")
        p2t_v = sem("probs_back_T_saved")
        r2_ps = sem("pooled_in_psum")
        r2_v = sem("pooled_saved")
        p1t_ps = sem("probs_T_in_psum")
        p1t_v = sem("probs_T_saved")
        t2_ps = sem("pooled_T_in_psum")
        t2_v = sem("pooled_T_saved")
        so_ps = sem("sub2char_in_psum")
        so_v = sem("sub2char_saved")
        st_ps = sem("sub2char_T_in_psum")
        st_v = sem("sub2char_T_saved")
        sg_ps = sem("sub2char_gate_in_psum")
        sg_v = sem("sub2char_gate_saved")
        fin = sem("both_ways_in_psum")
        th_r = sem("gate_tanh_ready")
        dif_r = sem("both_ways_subtracted")
        ss_r = sem("sub2char_of_tile_saved")
        up_r = sem("update_ready")
        xh_r = sem("x_T_high_ready")
        rt_ps = sem("router_logits_T_in_psum")
        rt_s = sem("router_logits_T_saved")
        rb_ps = sem("router_logits_in_psum")
        lg_r = sem("router_exponent_ready")
        ee_r = sem("router_exp_ready")
        y_ps = sem("expert_outputs_in_psum")
        y_free = sem("expert_bank_free")
        xp_ps = sem("x_projected_in_psum")
        xp_r = sem("x_projected_saved")
        sc_ps = sem("scores_c_T_in_psum")
        sc_s = sem("scores_c_T_saved")
        sb_ps = sem("scores_c_in_psum")
        mc_r = sem("neg_max_c_ready")
        ec_r = sem("probs_c_ready")
        pt_ps = sem("probs_c_T_in_psum")
        pt_r = sem("probs_c_T_saved")
        o_ps = sem("attended_in_psum")
        yb_r = sem("context_projected_copied")
        tpc = sem("x_transposed_c_in_psum")
        xnc_r = sem("x_normalised_c_ready")
        xTc_r = sem("x_transposed_c_saved")
        xupc = sem("x_updated_c")
        stats_c = sem("ln_stats_c_ready")
        inv_c = sem("ln_rstd_c_ready")
        ck_r = sem("weights_slice_examined")
        rd_r = sem("weights_slice_rounded")
        part_in = sem("mlp_h2_slice_loaded")
        h2_rd = sem("mlp_h2_slice_rounded")
        fl_v = sem("low_half_sum_ready")
        fl_ps = sem("flag_in_psum")
        fl_r = sem("flag_ready")
        d1_ps = sem("mlp_first_in_psum")
        sil_r = sem("silu_ready")
        h_r = sem("gated_hidden_ready")
        d2_ps = sem("mlp_hidden_in_psum")
        g_r = sem("gelu_ready")
        hi_r = sem("hidden_high_ready")
        lo_r = sem("hidden_low_ready")
        d4_ps = sem("mlp_output_in_psum")

        def col(name, m):
            return cols[:, COLS.index(name), m:m + 1]

        def row(name):
            return rows[:, ROWS.index(name), :]

        def wa(name):
            return aw[:, AW.index(name)]

        def of(t, i, *rest):
            return t[:, bass.ds(i, 1)].rearrange("p o c -> p (o c)")

        class Steps:

            def __init__(self, eng, s):
                self.eng, self.s, self.start, self.n = eng, s, 0, 0

            def mark(self, ins):
                ins.then_inc(self.s, 1)
                self.n += 1

            def wait(self, back=0):
                self.eng.wait_ge(self.s, self.start + self.n - back)

            def link(self, ins):
                self.mark(ins)
                self.wait()

            def enter(self, i, per):
                self.first = self.start + self.n
                self.start, self.n, self.per = self.first + i * per, 0, per

            def leave(self, passes):
                assert self.n == self.per, (self.n, self.per)
                self.start, self.n = self.first + passes * self.per, 0

        def weave(c, tile, step):
            k = 0
            for i, f in enumerate(step):
                for _ in range(TILE_BEFORE.count(i)):
                    tile(c - 1, k)
                    k += 1
                f(c)
            assert k == JT

        def sum_banks(b, j):
            return (2, 3) if isinstance(b, int) and b == B - 1 else (j % 2, 2 + j % 2)

        def d_bank(c, first):
            return (4 if first else 2) + 2 * (c % 2)

        def pair_of(i):
            return 2 * (i // E) + i % 2, i % E // 2

        block = ctx.enter_context(nc.Block())

        @block.sync
        def _(sp):
            sp.dma_start(ctxT[:], d["ctxT"]).then_inc(ctx_in, 16)
            for t, n in ((cols, "cols"), (ident, "ident"), (ctxr, "ctx"),
                         (maskT, "maskT"), (wr, "Wr"), (sc1, "scales")):
                sp.dma_start(t[:], d[n]).then_inc(small_in, 16)
            sp.dma_start(rows[:], d["rows"].partition_broadcast(L)).then_inc(small_in, 16)
            sp.dma_start(graw[:], d["gates"].partition_broadcast(P)).then_inc(small_in, 16)
            sp.dma_start(sc3[:], d["w3_s"].partition_broadcast(P)).then_inc(small_in, 16)
            sp.wait_ge(aw1_in, 16)
            for b in range(B):
                if b == 1:
                    sp.dma_start(wi[:], d["Wi"]).then_inc(exp_in, 16)
                    sp.dma_start(wo[:], d["Wo"]).then_inc(exp_in, 16)
                sp.dma_start(x[:, b * JT:(b + 1) * JT, :], d["x"][b].rearrange("(p j) c -> p j c", p=P)
                             ).then_inc(x_in[b], 16)
            sp.wait_ge(fin, NT)
            sp.wait_ge(th_r, NT)
            sp.wait_ge(xupd, NT)
            for i, examined in enumerate((0, 1, 4, 7)):
                if i:
                    sp.wait_ge(ck_r, examined)
                rows_k = SLICE // HID
                sp.dma_start(h2_part[:].rearrange("p (k c) -> p k c", k=rows_k),
                             d["h2"][:, i * rows_k:(i + 1) * rows_k, :]).then_inc(part_in, 16)
                if i == 0:
                    for n in REST:
                        sp.dma_start(mlp_f[n], d[n]).then_inc(rest_in, 16)
            sp.wait_ge(y_ps, 4 * NT)
            sp.dma_start(mlp_f["h2"], d["h2"]).then_inc(h2_in, 16)
            with sp.Fori(0, NG) as n:
                sp.wait_ge(xupd, XUPD_A + G + n * G)
                src = x[:, bass.ds(n * G, G), :]
                dst = d["out"][bass.ds(n, 1)].rearrange("o p j c -> p (o j) c")
                sp.dma_start(dst, src).then_inc(out_done, 16)
            sp.wait_ge(out_done, 16 * NG)

        N_SMALL = 9 * 16
        N_FIRST = 4

        @block.tensor
        def _(pe):
            mm = pe.matmul

            def transposes(src, slot, done):
                for k in range(KC):
                    last = pe.transpose(ps[:, slot, k * P:(k + 1) * P], src[:, k * P:(k + 1) * P], ident[:])
                last.then_inc(done, 1)

            pe.wait_ge(ctx_in, 16)
            pe.wait_ge(aw0_in, 16)
            for n, w in enumerate(AW[:N_FIRST]):
                if n == 1:
                    pe.wait_ge(aw1_in, 16)
                for m in range(KC):
                    for k in range(KC):
                        last = mm(ps[:, 2 * n + m, 0:BL], wa(w)[:, k, m * P:(m + 1) * P], ctxT[:, k, :],
                                  start=(k == 0), stop=(k == KC - 1))
                    last.then_inc(proj, 1)
            pe.wait_ge(aw2_in, 16)
            pe.wait_ge(proj_v, 4)
            for n, (w, src) in enumerate((("Wq_c", KT), ("Wk_c", QT))):
                for m in range(KC):
                    for k in range(KC):
                        last = mm(ps[:, 2 * n + m, 0:BL], wa(w)[:, k, m * P:(m + 1) * P], src[:, k, :],
                                  start=(k == 0), stop=(k == KC - 1))
                    last.then_inc(map_ps, 1)
            pe.wait_ge(small_in, N_SMALL)
            pe.wait_ge(proj_v, 6)
            for bank, src, bias in ((4, KT, "bq_c"), (5, QT, "bk_c")):
                for b in range(B):
                    for k in range(KC):
                        last = mm(ps[0:L, bank, b:b + 1], src[:, k, b * L:(b + 1) * L], col(bias, k),
                                  start=(k == 0), stop=(k == KC - 1))
                last.then_inc(map_ps, 1)
            pe.wait_ge(proj_s, 2)
            for b in range(B):
                if b >= 2:
                    pe.wait_ge(val_v, 2 * (b - 1))
                bank = 6 + b % 2
                for half, (src, w) in enumerate(((ctxT, "Wv_sT"), (VT, "WgT0"))):
                    o = ps[0:L, bank, half * D:(half + 1) * D]
                    for k in range(KC):
                        last = mm(o, src[:, k, b * L:(b + 1) * L], wa(w)[:, k, :], start=(k == 0), stop=(k == KC - 1))
                last.then_inc(val_ps, 1)
            pe.wait_ge(val_v, 2 * B)

            def expert(e):
                if e == 0:
                    pe.wait_ge(exp_in, 32)
                    pe.wait_ge(map_v, 6)
                if e >= 4:
                    pe.wait_ge(ex_l, e - 3)
                for m in range(KC):
                    for k in range(KC):
                        last = mm(ps[:, e % 4, m * D:(m + 1) * D], wi[:, k, e, m * P:(m + 1) * P], wo[:, k, e, :],
                                  start=(k == 0), stop=(k == KC - 1))
                last.then_inc(ex_ps, 1)

            def a_turn(c, q):
                for j in range(q * G, (q + 1) * G):
                    pe.wait_ge(xn_r, c * JT + (j + 1))
                    if j >= 2:
                        pe.wait_ge(xT_r, c * JT + (j - 1))
                    transposes(xn[:, j, :], 4 + j % 2, tp)

            def a_back_scores(c):
                pe.wait_ge(xT_r, (c + 1) * JT)
                pe.wait_ge(map_b, 2 * c + 2)
                for h in range(2):
                    for k in range(KC):
                        last = mm(ps[0:L, 6 + h, :], A2b[:, k, :], xnT[:, k, h * 512:(h + 1) * 512],
                                  start=(k == 0), stop=(k == KC - 1))
                last.then_inc(s2_ps, 1)

            def a_scores_T(c):
                for h in range(2):
                    for k in range(KC):
                        last = mm(ps[0:L, 4 + h, :], A1b[:, k, :], xnT[:, k, h * 512:(h + 1) * 512],
                                  start=(k == 0), stop=(k == KC - 1))
                    last.then_inc(s1_ps, 1)

            def a_scores(c):
                pe.wait_ge(s1_s, 2 * c + 2)
                for j in range(JT):
                    last = pe.transpose(ps[:, 4 + j // G, (j % G) * L:(j % G + 1) * L],
                                        s1s[:, j * P:(j + 1) * P], ident[0:L, 0:L])
                    if j % G == G - 1:
                        last.then_inc(s1b_ps, 1)

            def a_probs_back_T(c):
                pe.wait_ge(p2_r, 2 * c + 2)
                for j in range(JT):
                    last = pe.transpose(ps[:, 6 + j // G, (j % G) * L:(j % G + 1) * L],
                                        P2[:, j * P:(j + 1) * P], ident[0:L, 0:L])
                    if j % G == G - 1:
                        last.then_inc(p2t_ps, 1)

            def a_pool(c):
                for j in range(JT):
                    if j % G == 0:
                        pe.wait_ge(p2t_v, 2 * c + (j // G + 1))
                    last = mm(ps[0:L, 6, 0:D], P2T[:, j, :], xn[:, j, :], start=(j == 0), stop=(j == JT - 1))
                last.then_inc(r2_ps, 1)

            def a_pooled_T(c):
                pe.wait_ge(r2_v, c + 1)
                for k in range(KC):
                    last = pe.transpose(ps[:, 7, k * L:(k + 1) * L], r2n[:, k * P:(k + 1) * P], ident[0:L, 0:L])
                last.then_inc(t2_ps, 1)

            def a_sub2char(c):
                pe.wait_ge(t2_v, c + 1)
                for m in range(KC):
                    for k in range(KC):
                        last = mm(ps[:, 7, m * L:(m + 1) * L], wa("Wv_cT")[:, k, m * P:(m + 1) * P], t2T[:, k, :],
                                  start=(k == 0), stop=(k == KC - 1))
                last.then_inc(st_ps, 1)
                for k in range(KC):
                    last = mm(ps[0:L, 6, 0:D], t2T[:, k, :], wa("Wv_cT")[:, k, :], start=(k == 0), stop=(k == KC - 1))
                last.then_inc(so_ps, 1)

            def a_probs_T(c):
                for q in range(2):
                    pe.wait_ge(e1n, c * JT + (q + 1) * G)
                    for j in range(G):
                        last = pe.transpose(ps[0:L, 4 + q, j * P:(j + 1) * P], E1[:, q * G + j, :], ident[:])
                    last.then_inc(p1t_ps, 1)

            def a_sub2char_gate(c):
                pe.wait_ge(st_v, 2 * c + 2)
                for m in range(KC):
                    last = mm(ps[0:L, 7, 0:D], sT[:, m, :], wa("WgT1")[:, m, :], start=(m == 0), stop=(m == KC - 1))
                last.then_inc(sg_ps, 1)

            def a_sum(b, j):
                if j == 0:
                    pe.wait_ge(p1t_v, 2 * b + 2)
                    pe.wait_ge(so_v, b + 1)
                    pe.wait_ge(sg_v, b + 1)
                if isinstance(b, int) and b == B - 1:
                    pe.wait_ge(dif_r, b * JT + j)
                elif j >= 2:
                    pe.wait_ge(dif_r, b * JT + (j - 1))
                t = slice(j * P, (j + 1) * P)
                first, second = sum_banks(b, j)
                mm(ps[:, first, :], P1T[:, t], of(VV, b), start=True, stop=False)
                mm(ps[:, first, D:2 * D], IT[:, t], SS[:, bass.ds(b, 1), D:2 * D].rearrange("p o c -> p (o c)"),
                   start=False, stop=True)
                mm(ps[:, second, 0:D], IT[:, t], SS[:, bass.ds(b, 1), 0:D].rearrange("p o c -> p (o c)"),
                   start=True, stop=True).then_inc(fin, 1)

            steps = [lambda c: a_turn(c, 0), lambda c: a_turn(c, 1), a_back_scores, a_scores_T, a_scores,
                     a_probs_back_T, a_pool, a_pooled_T, a_sub2char, a_probs_T, a_sub2char_gate]
            pe.wait_ge(map_v, 6)
            for k, f in enumerate(steps):
                f(0)
                for e in EXPERTS_AFTER.get(k, ()):
                    expert(e)
            pe.wait_ge(ex_l, E)
            pe.wait_ge(it_in, 16)
            pe.wait_ge(zero_ready, 4)
            with pe.Fori(1, B) as c:
                weave(c, a_sum, steps)
                pe.wait_ge(dif_r, c * JT)

            def b_turn(g, s, tiles, before):
                if before is not None:
                    pe.wait_ge(xupc, 1 + G * before)
                for j in tiles:
                    pe.wait_ge(xn_r, NT + 1 + j + G * g)
                    pe.wait_ge(xT_r, NT - 1 + j + G * g)
                    transposes(xn[:, s * G + j, :], j % 2, tp)

            def b_route_T(g, s):
                pe.wait_ge(xT_r, NT + G + G * g)
                n = 0
                for k in range(KC):
                    for a, c in ((xTh, wrh), (xTl, wrh), (xTh, wrl)):
                        last = mm(ps[0:E, 0, :], c[:, k, :], a[:, s, k, :], start=(n == 0), stop=(n == 3 * KC - 1))
                        n += 1
                last.then_inc(rt_ps, 1)

            def b_route(g):
                if not isinstance(g, int):
                    pe.compute_val(g + 1)
                pe.wait_ge(const_ready, 3)
                pe.wait_ge(rt_s, g + 1)
                for j in range(G):
                    last = pe.transpose(ps[:, 1, j * E:(j + 1) * E], lgT[:, j * P:(j + 1) * P], ident[0:E, 0:E])
                last.then_inc(rb_ps, 1)

            def b_experts(g, s, i):
                j, pair = pair_of(i)
                pe.wait_ge(y_free, 1 + i + 4 * G * g)
                n = 0
                for k in range(KC):
                    for a, c in ((xTh, wexp_h), (xTh, wexp_l), (xTl, wexp_h)):
                        last = mm(ps[:, 4 + i % 4, :], a[:, s, k, j * P:(j + 1) * P],
                                  c[:, k, pair * 2 * D:(pair + 1) * 2 * D],
                                  start=(n == 0), stop=(n == 3 * KC - 1))
                        n += 1
                last.then_inc(y_ps, 1)

            def c_turn(c, before):
                if before is not None:
                    pe.wait_ge(xupc, 1 + G * before)
                for j in range(G):
                    pe.wait_ge(xnc_r, 1 + j + G * c)
                    if j >= 2:
                        pe.wait_ge(xTc_r, G * c + (j - 1))
                    transposes(xnc[:, j, :], 2 + j % 2, tpc)

            def c_project(c):
                pe.wait_ge(xTc_r, G * c + G)
                for m in range(KC):
                    for k in range(KC):
                        last = mm(ps[:, 2 + m, :], wa("W1T")[:, k, m * P:(m + 1) * P], xcT[:, k, :],
                                  start=(k == 0), stop=(k == KC - 1))
                    last.then_inc(xp_ps, 1)

            def c_scores_T(c, b):
                pe.wait_ge(yb_r, b + 1)
                pe.wait_ge(xp_r, 2 * c + 2)
                for k in range(KC):
                    last = mm(ps[0:L, 2, :], yTb[:, k, :], xpT[:, k, :], start=(k == 0), stop=(k == KC - 1))
                last.then_inc(sc_ps, 1)

            def c_scores(c):
                pe.wait_ge(sc_s, c + 1)
                for j in range(G):
                    last = pe.transpose(ps[:, 3, j * L:(j + 1) * L], scT[:, j * P:(j + 1) * P], ident[0:L, 0:L])
                last.then_inc(sb_ps, 1)

            def c_probs_T(c):
                pe.wait_ge(ec_r, G * c + G)
                for j in range(G):
                    last = pe.transpose(ps[0:L, 2, j * P:(j + 1) * P], EC[:, j, :], ident[:])
                last.then_inc(pt_ps, 1)

            def c_attend(c, b, routed):
                pe.wait_ge(pt_r, c + 1)
                if routed is not None:
                    pe.wait_ge(lg_r, routed + 1)
                for j in range(G):
                    mm(ps[:, j, 0:D + 1], PT[:, j * P:(j + 1) * P], of(yk, b), start=True, stop=True
                       ).then_inc(o_ps, 1)

            def check_weights():
                pe.wait_ge(fl_v, 1)
                mm(ps[0:1, 1, 0:1], lowcol[:], onec[:], start=True, stop=True).then_inc(fl_ps, 1)

            def bc_pass(g, s, c, b, before, ahead):
                steps = {}
                if ahead:
                    steps[2] = [lambda: b_turn(g + 1, 1 - s, (0, 1), before)]
                    steps[4] = [lambda: b_turn(g + 1, 1 - s, (2, 3), None)]
                    steps[6] = [lambda: b_route_T(g + 1, 1 - s)]
                    steps[9] = [lambda: b_route(g + 1)]
                if c is not None:
                    steps[5] = [lambda: c_turn(c, None if ahead else before)]
                    steps[7] = [lambda: c_project(c)]
                    steps[8] = [lambda: c_scores_T(c, b)]
                    steps.setdefault(9, []).append(lambda: c_scores(c))
                    steps[11] = [lambda: c_probs_T(c)]
                    steps[13] = [lambda: c_attend(c, b, g + 1 if ahead else None)]
                if not ahead:
                    steps[5].append(check_weights)
                    steps[13].insert(0, lambda: pe.wait_ge(fl_r, 1))
                for i in range(G * E // 2):
                    b_experts(g, s, i)
                    if c is None and i % 2 == 0:
                        a_sum(B - 1, i // 2)
                    for step in steps.get(i, ()):
                        step()

            b_turn(0, 0, range(G), None)
            b_route_T(0, 0)
            b_route(0)
            bc_pass(0, 0, None, None, None, True)
            pe.wait_ge(dif_r, NT)
            with pe.Fori(0, NG // 2 - 1) as i:
                bc_pass(2 * i + 1, 1, 2 * i, i, 2 * i, True)
                bc_pass(2 * i + 2, 0, 2 * i + 1, i, 2 * i + 1, True)
            bc_pass(NG - 1, 1, NG - 2, B - 1, NG - 2, False)
            def stage_d(short):
                if short:
                    w = mlp_r
                    xT, ha, hb = (xdT_h, xdT_l), (ha_h, ha_l), (hb_h, hb_l)
                else:
                    w = mlp_f
                    xT, ha, hb = (xdT_f,), (ha_f,), (hb_f,)

                def product(o, stationary, moving, last_k, n_k, k):
                    parts = [(a, b) for a in stationary for b in moving]
                    for i, (a, b) in enumerate(parts):
                        last = mm(o, a, b, start=(k == 0 and i == 0), stop=(k == n_k - 1 and i == len(parts) - 1))
                    return last

                def turn(n):
                    for j in range(G):
                        pe.wait_ge(xn_r, 2 * NT + 1 + j + G * n)
                        pe.wait_ge(xT_r, 2 * NT - 1 + j + G * n)
                        transposes(xd[:, j, :], j % 2, tp)

                def hidden_ready(n, layer, k):
                    if short:
                        pe.wait_ge(lo_r, 3 * HC * n + HC * layer + k + 1)
                    elif layer == 0:
                        pe.wait_ge(h_r, HC * n + k + 1)
                    else:
                        pe.wait_ge(g_r, 2 * HC * n + HC * (layer - 1) + k + 1)

                def group(n, ahead, first=False):
                    chain = {0: lambda: c_turn(NG - 1, NG - 1), 1: lambda: c_project(NG - 1),
                             2: lambda: c_scores_T(NG - 1, B - 1), 3: lambda: c_scores(NG - 1),
                             5: lambda: c_probs_T(NG - 1), 7: lambda: c_attend(NG - 1, B - 1, None)}
                    pe.wait_ge(xT_r, 2 * NT + G + G * n)
                    if first:
                        pe.wait_ge(y_free, 4 * NT + 4)
                    for c in range(HC):
                        a = d_bank(c, first)
                        if c >= 2:
                            pe.wait_ge(h_r, HC * n + c - 1)
                        elif not first:
                            pe.wait_ge(up_r, UP_A + G * n - 2 + 2 * c)
                        for name, bank in (("w1", a), ("w2", a + 1)):
                            for k in range(KC):
                                last = product(ps[:, bank, :], [w[name][:, k, c * P:(c + 1) * P]],
                                               [t[:, k, :] for t in xT], None, KC, k)
                        last.then_inc(d1_ps, 1)
                        if first and c in chain:
                            chain[c]()
                    if first:
                        pe.wait_ge(h_r, HC)
                    for layer, (name, src) in enumerate((("h1", ha), ("h2", hb))):
                        if short and layer:
                            pe.wait_ge(h2_rd, n_h2 // SLICE)
                        for c in range(HC):
                            q = 2 * HC * n + HC * layer + c
                            if layer or c >= 2:
                                pe.wait_ge(g_r, q - 1)
                            for k in range(HC):
                                if c == 0:
                                    hidden_ready(n, layer, k)
                                last = product(ps[:, 6 + c % 2, :], [w[name][:, k, c * P:(c + 1) * P]],
                                               [t[:, k, :] for t in src], None, HC, k)
                            last.then_inc(d2_ps, 1)
                    if first:
                        pe.wait_ge(xupc, 1 + NT)
                    for j in range(G):
                        if j == 2 and ahead:
                            turn(n + 1)
                        for k in range(HC):
                            if j == 0:
                                hidden_ready(n, 2, k)
                            last = product(ps[:, 2 + j, 0:D], [t[:, k, j * P:(j + 1) * P] for t in ha],
                                           [w["w3"][:, k, :]], None, HC, k)
                        last.then_inc(d4_ps, 1)

                pe.wait_ge(xupc, 1 + G * (NG - 1))
                turn(0)
                group(0, True, first=True)
                with pe.Fori(1, NG - 1) as n:
                    group(n, True)
                group(NG - 1, False)

            pe.wait_ge(fl_r, 1)
            long = pe.value_load(flag[:].bitcast(I32))
            with pe.If(long == 0):
                stage_d(True)
            with pe.Else():
                pe.wait_ge(again_in, 16 * (len(REST) + 1))
                stage_d(False)

        @block.scalar
        def _(act):
            act.dma_start(aw[:, 0:1], d["aw"][:, 0:1]).then_inc(aw0_in, 16)
            act.dma_start(aw[:, 1:N_FIRST], d["aw"][:, 1:N_FIRST]).then_inc(aw1_in, 16)
            act.dma_start(aw[:, N_FIRST:], d["aw"][:, N_FIRST:]).then_inc(aw2_in, 16)
            act.dma_start(IT[:], d["interp"]).then_inc(it_in, 16)
            act.wait_ge(small_in, N_SMALL)
            act.activation(gt[:], graw[:], ACT.Tanh).then_inc(gate_ready, 1)
            for m in range(KC):
                act.wait_ge(proj, 7 + m)
                act.activation(ypT[:, m, :], ps[:, 6 + m, 0:BL], ACT.Relu, bias=col("b1", m)).then_inc(proj_s, 1)
            def expert(e):
                act.wait_ge(ex_ps, e + 1)
                act.activation(wexp_h[:, :, e * D:(e + 1) * D],
                               ps[:, e % 4, :].rearrange("p (m c) -> p m c", m=KC), ACT.Copy).then_inc(ex_h, 1)

            def a_turn(c, q):
                for j in range(q * G, (q + 1) * G):
                    act.wait_ge(tp, c * JT + (j + 1))
                    act.activation(xnT[:, :, j * P:(j + 1) * P],
                                   ps[:, 4 + j % 2, 0:D].rearrange("p (k c) -> p k c", k=KC), ACT.Copy
                                   ).then_inc(xT_r, 1)

            def a_scores_T(c):
                for h in range(2):
                    act.wait_ge(s1_ps, 2 * c + h + 1)
                    act.activation(s1s[:, h * 512:(h + 1) * 512], ps[0:L, 4 + h, :], ACT.Identity,
                                   bias=c1b[:, 0:1]).then_inc(s1_s, 1)

            def a_exp_back(c):
                act.wait_ge(s2_b, c + 1)
                for h in range(2):
                    act.activation(P2[:, h * 512:(h + 1) * 512], ps[0:L, 6 + h, :], ACT.Exp, bias=mx2[:, 2:3],
                                   scale=1.0, accum_out=rs2[:, h:h + 1]).then_inc(p2_r, 1)

            def a_exp(c):
                for j in range(JT):
                    if j % G == 0:
                        act.wait_ge(nm_r, 2 * c + (j // G + 1))
                    act.activation(E1[:, j, :], ps[:, 4 + j // G, (j % G) * L:(j % G + 1) * L], ACT.Exp,
                                   bias=nm1[:, j:j + 1], scale=1.0, accum_out=rs1[:, j:j + 1]).then_inc(e1_r, 1)

            def a_probs_T(c):
                for q in range(2):
                    act.wait_ge(p1t_ps, 2 * c + (q + 1))
                    act.activation(P1T[0:L, q * GN:(q + 1) * GN], ps[0:L, 4 + q, :], ACT.Copy).then_inc(p1t_v, 1)

            def a_sum(b, j):
                q = j % 2
                act.wait_ge(fin, b * JT + (j + 1))
                if j >= 2:
                    act.wait_ge(up_r, b * JT + (j - 1))
                first, second = sum_banks(b, j)
                act.activation(ssb[:, q, :], ps[:, second, 0:D], ACT.Copy).then_inc(ss_r, 1)
                act.activation(th[:, q, :], ps[:, first, D:2 * D], ACT.Tanh, scale=0.5).then_inc(th_r, 1)

            def nothing(c):
                pass

            steps = [lambda c: a_turn(c, 0), lambda c: a_turn(c, 1), nothing, a_scores_T, a_exp_back,
                     a_exp, nothing, nothing, nothing, a_probs_T, nothing]
            for k, f in enumerate(steps):
                if k == 9:
                    act.wait_ge(zero_ready, 4)
                f(0)
                for e in EXPERTS_AFTER.get(k, ()):
                    expert(e)
            with act.Fori(1, B) as c:
                weave(c, a_sum, steps)

            def examine(raw, column, before):
                low = raw.bitcast(U16).rearrange("p (n h) -> p n h", h=2)[:, :, 0:1]
                act.activation(dump[:], low.rearrange("p n o -> p (n o)"), ACT.Copy,
                               accum_out=lowsum[:, bass.ds(column, 1)]).then_inc(ck_r, 1)
                act.wait_ge(ck_r, before + 1)

            def rest_slice(i, before):
                part = slice(i * SLICE, (i + 1) * SLICE) if isinstance(i, int) else bass.ds(i * SLICE, SLICE)
                examine(rest_raw[:, part], i, before)
                act.activation(rest_round[:, part], rest_raw[:, part], ACT.Copy).then_inc(rd_r, 1)

            def h2_slice(i, before):
                act.wait_ge(part_in, 16 * i + 16)
                examine(h2_part[:], REST_SLICES + i, before)

            def b_high(g, s, tiles):
                for j in tiles:
                    act.wait_ge(tp, NT + 1 + j + G * g)
                    act.activation(xTh[:, s, :, j * P:(j + 1) * P],
                                   ps[:, j % 2, 0:D].rearrange("p (k c) -> p k c", k=KC), ACT.Copy
                                   ).then_inc(xh_r, 1)

            def b_logits(g):
                act.wait_ge(rt_ps, g + 1)
                act.activation(lgT[:], ps[0:E, 0, :], ACT.Copy).then_inc(rt_s, 1)

            def b_exp(g):
                act.wait_ge(lg_r, g + 1)
                act.activation(pex[:], lsub[:], ACT.Exp).then_inc(ee_r, 1)

            def c_turn(c):
                for j in range(G):
                    act.wait_ge(tpc, 1 + j + G * c)
                    act.activation(xcT[:, :, j * P:(j + 1) * P],
                                   ps[:, 2 + j % 2, 0:D].rearrange("p (k c) -> p k c", k=KC), ACT.Copy).then_inc(xTc_r, 1)

            def c_project(c):
                for m in range(KC):
                    act.wait_ge(xp_ps, 2 * c + m + 1)
                    act.activation(xpT[:, m, :], ps[:, 2 + m, :], ACT.Relu, bias=col("b1", m)).then_inc(xp_r, 1)

            def c_scores_T(c, b):
                act.wait_ge(sc_ps, c + 1)
                act.wait_ge(yb_r, b + 1)
                act.activation(scT[:], ps[0:L, 2, :], ACT.Identity, bias=mcolb[:, 0:1]).then_inc(sc_s, 1)

            def c_exp(c):
                act.wait_ge(mc_r, c + 1)
                for j in range(G):
                    act.activation(EC[:, j, :], ps[:, 3, j * L:(j + 1) * L], ACT.Exp, bias=nmc[:, j:j + 1],
                                   scale=1.0).then_inc(ec_r, 1)

            def c_probs_T(c):
                act.wait_ge(pt_ps, c + 1)
                act.activation(PT[0:L, :], ps[0:L, 2, :], ACT.Copy).then_inc(pt_r, 1)

            def bc_pass(g, s, c, b):
                if g is not None:
                    b_high(g, s, range(G))
                if c is not None:
                    c_turn(c)
                if g is not None:
                    b_logits(g)
                if c is not None:
                    c_project(c)
                    c_scores_T(c, b)
                    c_exp(c)
                    c_probs_T(c)
                if g is not None:
                    b_exp(g)

            bc_pass(0, 0, None, None)
            a_sum(B - 1, 0)
            b_high(1, 1, (0, 1))
            a_sum(B - 1, 1)
            b_high(1, 1, (2, 3))
            a_sum(B - 1, 2)
            b_logits(1)
            for j in (3, 4, 5):
                a_sum(B - 1, j)
            b_exp(1)
            a_sum(B - 1, 6)
            a_sum(B - 1, 7)
            act.wait_ge(zero_ready, 5)
            with act.Fori(0, NG // 2 - 1) as i:
                bc_pass(2 * i + 2, 0, 2 * i, i)
                h2_slice(i, 3 * i)
                bc_pass(2 * i + 3, 1, 2 * i + 1, i)
                act.wait_ge(rest_in, 16 * len(REST))
                rest_slice(2 * i, 3 * i + 1)
                rest_slice(2 * i + 1, 3 * i + 2)
            h2_slice(n_h2 // SLICE - 1, NCHECK - 2)
            rest_slice(REST_SLICES - 1, NCHECK - 1)
            c_turn(NG - 2)
            act.wait_ge(fl_ps, 1)
            act.activation(flag[:], ps[0:1, 1, 0:1], ACT.Copy).then_inc(fl_r, 1)
            c_project(NG - 2)
            c_scores_T(NG - 2, B - 1)
            c_exp(NG - 2)
            c_probs_T(NG - 2)

            def stage_d(short):
                def turn(n):
                    for j in range(G):
                        act.wait_ge(tp, 2 * NT + 1 + j + G * n)
                        dst, done = (xdT_h, xh_r) if short else (xdT_f, xT_r)
                        act.activation(dst[:, :, j * P:(j + 1) * P],
                                       ps[:, j % 2, 0:D].rearrange("p (k c) -> p k c", k=KC), ACT.Copy
                                       ).then_inc(done, 1)

                def high(c, full, part, ready, count):
                    if short:
                        act.wait_ge(ready, count)
                        act.activation(part[:, c, :], full[:, c, :], ACT.Copy).then_inc(hi_r, 1)

                def group(n, ahead, first=False):
                    chain = {0: lambda: c_turn(NG - 1), 1: lambda: c_project(NG - 1),
                             2: lambda: c_scores_T(NG - 1, B - 1), 4: lambda: c_exp(NG - 1),
                             6: lambda: c_probs_T(NG - 1)}
                    for c in range(HC):
                        act.wait_ge(d1_ps, HC * n + c + 1)
                        act.activation(ha_f[:, c, :], ps[:, d_bank(c, first), :], ACT.Silu,
                                       scale=sc1[:, 0, c:c + 1]).then_inc(sil_r, 1)
                        if first and c in chain:
                            chain[c]()
                        if c >= 1:
                            high(c - 1, ha_f, ha_h, h_r, HC * n + c)
                    high(HC - 1, ha_f, ha_h, h_r, HC * n + HC)
                    for layer, (full, part) in enumerate(((hb_f, hb_h), (ha_f, ha_h))):
                        for c in range(HC):
                            q = 2 * HC * n + HC * layer + c + 1
                            act.wait_ge(d2_ps, q)
                            act.activation(full[:, c, :], ps[:, 6 + c % 2, :], ACT.Gelu,
                                           scale=sc1[:, 2 + layer, c:c + 1]).then_inc(g_r, 1)
                            high(c, full, part, g_r, q)
                    if ahead:
                        turn(n + 1)

                turn(0)
                group(0, True, first=True)
                with act.Fori(1, NG - 1) as n:
                    group(n, True)
                group(NG - 1, False)

            act.wait_ge(fl_r, 1)
            long = act.value_load(flag[:].bitcast(I32))
            with act.If(long == 0):
                stage_d(True)
            with act.Else():
                act.wait_ge(rd_r, REST_SLICES)
                act.wait_ge(h2_rd, n_h2 // SLICE)
                for n in REST + ["h2"]:
                    act.dma_start(mlp_f[n], d[n]).then_inc(again_in, 16)
                stage_d(False)

        @block.vector
        def _(dve):
            st = Steps(dve, dstep)

            def wait_alone(s, value):
                if not isinstance(value, int):
                    dve.compute_val(value)
                dve.wait_ge(const_ready, 3)
                dve.wait_ge(s, value)

            def steps_alone():
                wait_alone(st.s, st.start + st.n)

            def measure(tile, k):
                st.mark(dve.bn_stats(stat[:, k, :], of(x, tile)))

            def aggregate(t0, n, k, done):
                steps_alone()
                for j in range(n):
                    st.mark(dve.bn_aggr(agg[:, k + j, :], stat[:, k + j, :]))
                steps_alone()
                dve.tensor_copy(mv[:, bass.ds(t0, n), :], agg[:, k:k + n, :]).then_inc(done, 1)

            def normalise(tile, dst, done=xn_r):
                dve.tensor_scalar(dst, of(x, tile), mv[:, bass.ds(tile, 1), 0:1].rearrange("p o c -> p (o c)"),
                                  rstd[:, bass.ds(tile, 1)], ALU.subtract, ALU.mult).then_inc(done, 1)

            dve.memset(eps_t[:], EPS).then_inc(const_ready, 1)
            dve.memset(half_t[:], -0.5).then_inc(const_ready, 1)
            dve.memset(onec[:], 1.0).then_inc(const_ready, 1)
            dve.memset(lowsum[:], 0.0).then_inc(xupc, 1)
            dve.memset(VV[64:LP], 0.0).then_inc(zero_ready, 1)
            dve.memset(yk[64:LP], 0.0).then_inc(zero_ready, 1)
            dve.wait_ge(zero_ready, 2)
            dve.wait_ge(small_in, N_SMALL)
            dve.wait_ge(gate_ready, 1)
            st.link(dve.tensor_scalar(gh[:], gt[:, 0:1], 0.5, None, ALU.mult))
            for n in ("bv_s", "bv_c"):
                st.link(dve.tensor_scalar(row(n), row(n), gh[0:L, 0:1], None, ALU.mult))
            st.link(dve.tensor_scalar(sc3[:], sc3[:], gt[:, 3:4], None, ALU.mult))
            st.link(dve.tensor_scalar(keep[:], maskT[:], -1.0, 1.0, ALU.mult, ALU.add))
            st.mark(dve.tensor_scalar(mcol[:], maskT[:], FAR, None, ALU.mult))
            for b in range(B):
                st.mark(dve.tensor_scalar(yk[0:L, b, 0:D], ctxr[:, b, :], keep[:, b:b + 1], gt[0:L, 1:2],
                                          ALU.mult, ALU.mult))
                st.mark(dve.tensor_copy(yk[0:L, b, D:D + 1], keep[:, b:b + 1]))
            for n, (dst, bias) in enumerate(((KT, "bk_s"), (QT, "bq_s"), (VT, "bv_s"))):
                for m in range(KC):
                    dve.wait_ge(proj, 2 * n + m + 1)
                    dve.tensor_scalar(dst[:, m, :], ps[:, 2 * n + m, 0:BL], col(bias, m), None, ALU.add
                                      ).then_inc(proj_v, 1)
            def batch_stats(b):
                dve.wait_ge(x_in[b], 16)
                for j in range(JT):
                    measure(b * JT + j, j)
                aggregate(b * JT, JT, 0, stats)

            batch_stats(0)
            for n, dst in enumerate((A1, A2)):
                for m in range(KC):
                    dve.wait_ge(map_ps, 2 * n + m + 1)
                    dve.tensor_scalar(dst[:, m, :], ps[:, 2 * n + m, 0:BL], SCALE, None, ALU.mult).then_inc(map_v, 1)
            for n, (bank, dst) in enumerate(((4, c1), (5, c2))):
                dve.wait_ge(map_ps, 5 + n)
                dve.tensor_scalar(dst[:], ps[0:L, bank, 0:B], SCALE, None, ALU.mult).then_inc(map_v, 1)
            for b in range(B):
                dve.wait_ge(val_ps, b + 1)
                dve.scalar_tensor_tensor(VV[0:L, b, 0:D], ps[0:L, 6 + b % 2, 0:D], gh[0:L, 0:1], row("bv_s"),
                                         ALU.mult, ALU.add).then_inc(val_v, 1)
                dve.tensor_tensor(VV[0:L, b, D:2 * D], ps[0:L, 6 + b % 2, D:2 * D], row("bg"), ALU.add
                                  ).then_inc(val_v, 1)
            def expert(e):
                dve.wait_ge(ex_h, e + 1)
                dve.tensor_tensor(wexp_l[:, :, e * D:(e + 1) * D], ps[:, e % 4, :].rearrange("p (m c) -> p m c", m=KC),
                                  wexp_h[:, :, e * D:(e + 1) * D].bitcast(F32), ALU.subtract).then_inc(ex_l, 1)

            dve.wait_ge(map_v, 6)

            def a_start(c):
                st.mark(dve.tensor_copy(c1b[:], c1[:, bass.ds(c, 1)]))
                st.wait()
                dve.tensor_copy(A1b[:], A1[:, :, bass.ds(c * L, L)]).then_inc(map_b, 1)
                dve.tensor_copy(A2b[:], A2[:, :, bass.ds(c * L, L)]).then_inc(map_b, 1)
                for j in range(JT):
                    normalise(c * JT + j, xn[:, j, :])

            def a_max_back(c):
                dve.wait_ge(s2_ps, c + 1)
                st.link(dve.tensor_reduce(mx2[:, 0:1], ps[0:L, 6:8, :], mybir.AxisListType.XY, ALU.max))
                st.link(dve.tensor_scalar(mx2[:, 1:2], mx2[:, 0:1], c2[:, bass.ds(c, 1)], None, ALU.add))
                dve.tensor_tensor(mx2[:, 2:3], c2[:, bass.ds(c, 1)], mx2[:, 1:2], ALU.subtract).then_inc(s2_b, 1)

            def a_max(c):
                for q in range(2):
                    dve.wait_ge(s1b_ps, 2 * c + (q + 1))
                    dve.tensor_reduce(nm1[:, q * G:(q + 1) * G],
                                      ps[:, 4 + q, 0:G * L].rearrange("p (j c) -> p j c", j=G), X, ALU.max,
                                      negate=True).then_inc(nm_r, 1)

            def a_probs_back_T(c):
                for q in range(2):
                    dve.wait_ge(p2t_ps, 2 * c + (q + 1))
                    dve.tensor_copy(P2T[:, q * G:(q + 1) * G, :],
                                    ps[:, 6 + q, 0:G * L].rearrange("p (j c) -> p j c", j=G)).then_inc(p2t_v, 1)
                st.link(dve.tensor_tensor(rs2[:, 2:3], rs2[:, 0:1], rs2[:, 1:2], ALU.add))
                st.link(dve.reciprocal(rs2[:, 3:4], rs2[:, 2:3]))

            def a_pool(c):
                for q in range(2):
                    dve.wait_ge(e1_r, c * JT + (q + 1) * G)
                    st.link(dve.reciprocal(ri1[:, q * G:(q + 1) * G], rs1[:, q * G:(q + 1) * G]))
                    for j in range(q * G, (q + 1) * G):
                        dve.tensor_scalar(E1[:, j, :], E1[:, j, :], ri1[:, j:j + 1], None, ALU.mult).then_inc(e1n, 1)
                dve.wait_ge(r2_ps, c + 1)
                dve.tensor_scalar(r2n[:], ps[0:L, 6, 0:D], rs2[:, 3:4], None, ALU.mult).then_inc(r2_v, 1)

            def a_pooled_T(c):
                dve.wait_ge(t2_ps, c + 1)
                dve.tensor_copy(t2T[:], ps[:, 7, 0:KC * L].rearrange("p (k c) -> p k c", k=KC)).then_inc(t2_v, 1)

            def a_sub2char(c):
                dve.wait_ge(st_ps, c + 1)
                for m in range(KC):
                    dve.tensor_scalar(sT[:, m, :], ps[:, 7, m * L:(m + 1) * L], col("bv_c", m), None, ALU.add
                                      ).then_inc(st_v, 1)
                dve.wait_ge(so_ps, c + 1)
                dve.scalar_tensor_tensor(SS[0:L, bass.ds(c, 1), 0:D].rearrange("p o c -> p (o c)"), ps[0:L, 6, 0:D],
                                         gh[0:L, 0:1], row("bv_c"), ALU.mult, ALU.add).then_inc(so_v, 1)

            def a_sub2char_gate(c):
                dve.wait_ge(sg_ps, c + 1)
                dve.tensor_copy(SS[0:L, bass.ds(c, 1), D:2 * D].rearrange("p o c -> p (o c)"), ps[0:L, 7, 0:D]
                                ).then_inc(sg_v, 1)

            def a_sum(b, j):
                q = j % 2
                dve.wait_ge(th_r, b * JT + (j + 1))
                if j >= 2:
                    wait_alone(xupd, b * JT + (j - 1))
                dve.tensor_tensor(u1[:, q, :], ps[:, sum_banks(b, j)[0], 0:D], ssb[:, q, :], ALU.subtract
                                  ).then_inc(dif_r, 1)
                dve.wait_ge(dif_r, b * JT + (j + 1))
                st.link(dve.scalar_tensor_tensor(u1[:, q, :], th[:, q, :], 1.0, u1[:, q, :], ALU.add, ALU.mult))
                dve.scalar_tensor_tensor(u1[:, q, :], ssb[:, q, :], 2.0, u1[:, q, :], ALU.mult, ALU.add
                                         ).then_inc(up_r, 1)
                if j >= 2:
                    measure(b * JT + (j - 2), G + (j - 2) % G)
                if j == G + 1:
                    aggregate(b * JT, G, G, stats)

            def a_sum_end(b):
                for i in range(JT - 2, JT):
                    wait_alone(xupd, b * JT + (i + 1))
                    measure(b * JT + i, G + i % G)
                aggregate(b * JT + G, G, G, stats)

            def nothing(c):
                pass

            steps = [nothing, nothing, a_max_back, nothing, a_max, a_probs_back_T, a_pool, a_pooled_T,
                     a_sub2char, nothing, a_sub2char_gate]
            dve.wait_ge(inv, 1)
            a_start(0)
            for k, f in enumerate(steps):
                if k == 8:
                    dve.wait_ge(zero_ready, 4)
                f(0)
                for e in EXPERTS_AFTER.get(k, ()):
                    expert(e)
                if k < B - 1:
                    batch_stats(k + 1)
            st.link(dve.tensor_copy(wrh[:], wr[:]))
            st.link(dve.tensor_tensor(wrl[:], wr[:], wrh[:].bitcast(F32), ALU.subtract))
            dve.wait_ge(inv, B)
            a_start(1)
            weave(1, a_sum, steps)
            with dve.Fori(2, B) as c:
                st.enter(c - 2, A_STEPS)
                a_start(c)
                a_sum_end(c - 2)
                weave(c, a_sum, steps)
            st.leave(B - 2)

            def b_norm(g, s, tiles):
                dve.wait_ge(tp, NT - G + G * g)
                for j in tiles:
                    normalise(G * g + j, xn[:, s * G + j, :])

            def b_low(g, s, tiles):
                for j in tiles:
                    dve.wait_ge(xh_r, G * g + j + 1)
                    t = slice(j * P, (j + 1) * P)
                    dve.tensor_tensor(xTl[:, s, :, t], ps[:, j % 2, 0:D].rearrange("p (k c) -> p k c", k=KC),
                                      xTh[:, s, :, t].bitcast(F32), ALU.subtract).then_inc(xT_r, 1)

            b_norm(0, 0, range(G))
            b_low(0, 0, range(G))
            a_sum_end(B - 2)
            dve.memset(lg[:, 0:2, :], FAR).then_inc(y_free, 1)
            dve.memset(lg[:, 2:4, :], FAR).then_inc(y_free, 1)
            dve.memset(want[:, 0:2, :], FAR).then_inc(y_free, 1)
            dve.memset(want[:, 2:4, :], FAR).then_inc(y_free, 1)
            dve.wait_ge(y_free, 4)

            def b_route(g, s):
                dve.wait_ge(rb_ps, g + 1)
                st.mark(dve.tensor_copy(lg[:, :, 0:E], ps[:, 1, 0:G * E].rearrange("p (j e) -> p j e", j=G)))
                steps_alone()
                for j in range(G):
                    st.mark(dve.max(top[:, j, :], lg[:, j, 0:E]))
                st.wait()
                dve.tensor_tensor(lsub[:], lg[:, :, 0:E], top[:, :, 0:1].broadcast_to([P, G, E]), ALU.subtract
                                  ).then_inc(lg_r, 1)
                st.mark(dve.tensor_copy(want[:, :, 0:2], top[:, :, 0:2]))
                steps_alone()
                for j in range(G):
                    st.mark(dve.match_replace(marked[:, j, :], want[:, j, :], lg[:, j, :], TAKEN))
                dve.wait_ge(ee_r, g + 1)
                st.link(dve.tensor_reduce(sme[:], pex[:], X, ALU.add))
                st.mark(dve.scalar_tensor_tensor(pm[:], marked[:, :, 0:E], TAKEN, pex[:], ALU.is_ge, ALU.mult))
                st.link(dve.reciprocal(rie[:], sme[:]))
                st.link(dve.tensor_scalar(rig[:], rie[:], gt[:, 2:3], None, ALU.mult))
                st.link(dve.tensor_tensor(coef[:, s], pm[:], rig[:].unsqueeze(2).broadcast_to([P, G, E]), ALU.mult))

            def b_add(g, s, m):
                for h in range(2):
                    for i in (2 * m, 2 * m + 1):
                        j, pair = pair_of(i)
                        e = 2 * pair + h
                        if h == 0:
                            dve.wait_ge(y_ps, 4 * G * g + i + 1)
                            dve.wait_ge(y_free, 4 * G * g + i + 3)
                        else:
                            st.wait(back=1 - i % 2)
                        ins = dve.scalar_tensor_tensor(of(x, G * g + j), ps[:, 4 + i % 4, h * D:(h + 1) * D],
                                                       coef[:, s, j, e:e + 1], of(x, G * g + j), ALU.mult, ALU.add)
                        if h == 0:
                            st.mark(ins)
                        else:
                            ins.then_inc(y_free, 1)

            def b_measure(g, half):
                wait_alone(y_free, 4 * G * g + 4 + (half + 1) * E)
                for j in (2 * half, 2 * half + 1):
                    measure(G * g + j, j)

            def b_end(g):
                b_measure(g, 1)
                aggregate(G * g, G, 0, stats)

            def c_batch(b):
                st.link(dve.tensor_copy(mcolb[:], mcol[:, bass.ds(b, 1)]))
                dve.tensor_copy(yTb[:], ypT[:, :, bass.ds(b * L, L)]).then_inc(yb_r, 1)

            def c_norm(c):
                dve.wait_ge(inv, INV_A + 1 + c)
                for j in range(G):
                    normalise(G * c + j, xnc[:, j, :], xnc_r)

            def c_max(c):
                dve.wait_ge(sb_ps, c + 1)
                dve.tensor_reduce(nmc[:], ps[:, 3, 0:G * L].rearrange("p (j c) -> p j c", j=G), X, ALU.max,
                                  negate=True).then_inc(mc_r, 1)

            def c_update(c):
                dve.wait_ge(o_ps, G * c + G)
                st.link(dve.reciprocal(ric[:], ps[:, 0:G, D:D + 1].rearrange("p j o -> p (j o)")))
                for j in range(G):
                    t = G * c + j
                    dve.scalar_tensor_tensor(of(x, t), ps[:, j, 0:D], ric[:, j:j + 1], of(x, t),
                                             ALU.mult, ALU.add).then_inc(xupc, 1)

            def c_stats(c):
                for j in range(G):
                    wait_alone(xupc, 2 + G * c + j)
                    measure(G * c + j, G + j)
                aggregate(G * c, G, G, stats_c)

            def check_weights():
                dve.wait_ge(ck_r, NCHECK)
                dve.tensor_reduce(lowcol[:], lowsum[:], X, ALU.add).then_inc(fl_v, 1)

            def bc_pass(g, s, c, b, ahead, c_before):
                steps = {m: [] for m in range(G * E // 4)}
                if ahead:
                    b_norm(g + 1, 1 - s, (0, 1))
                    steps[0].append(lambda: b_low(g + 1, 1 - s, (0, 1)))
                    steps[2].append(lambda: b_low(g + 1, 1 - s, (2, 3)))
                    steps[5].append(lambda: b_route(g + 1, 1 - s))
                if c is not None:
                    b_end(c)
                if ahead:
                    b_norm(g + 1, 1 - s, (2, 3))
                if c is not None:
                    steps[1].append(lambda: c_norm(c))
                    if b is not None:
                        steps[1].append(lambda: c_batch(b))
                    steps[4].append(lambda: c_max(c))
                    steps[6].append(lambda: c_update(c))
                if not ahead:
                    steps[1].append(check_weights)
                steps[3].append(lambda: b_measure(g, 0))
                if c_before is not None:
                    steps[3].append(lambda: c_stats(c_before))
                for m in range(G * E // 4):
                    if c is None:
                        a_sum(B - 1, m)
                    b_add(g, s, m)
                    for step in steps[m]:
                        step()

            dve.memset(PT[64:LP], 0.0).then_inc(zero_ready, 1)
            dve.wait_ge(zero_ready, 5)
            b_route(0, 0)
            bc_pass(0, 0, None, None, True, None)
            a_sum_end(B - 1)
            dve.wait_ge(inv, INV_A)
            bc_pass(1, 1, 0, 0, True, None)
            bc_pass(2, 0, 1, None, True, 0)
            with dve.Fori(1, NG // 2 - 1) as i:
                st.enter(i - 1, BC_STEPS)
                bc_pass(2 * i + 1, 1, 2 * i, i, True, 2 * i - 1)
                bc_pass(2 * i + 2, 0, 2 * i + 1, None, True, 2 * i)
            st.leave(NG // 2 - 2)
            bc_pass(NG - 1, 1, NG - 2, B - 1, False, NG - 3)

            def stage_d(short):
                def norm(n):
                    for j in range(G):
                        normalise(G * n + j, xd[:, j, :])

                def low_turn(n):
                    if short:
                        for j in range(G):
                            dve.wait_ge(xh_r, NT + G * n + j + 1)
                            t = slice(j * P, (j + 1) * P)
                            dve.tensor_tensor(xdT_l[:, :, t], ps[:, j % 2, 0:D].rearrange("p (k c) -> p k c", k=KC),
                                              xdT_h[:, :, t].bitcast(F32), ALU.subtract).then_inc(xT_r, 1)

                def low(c, full, part, rest, n_high):
                    if short:
                        dve.wait_ge(hi_r, n_high)
                        dve.tensor_tensor(rest[:, c, :], full[:, c, :], part[:, c, :].bitcast(F32), ALU.subtract
                                          ).then_inc(lo_r, 1)

                def update(n, j):
                    dve.wait_ge(d4_ps, G * n + j + 1)
                    dve.wait_ge(xupd, XUPD_A - 1 + j + G * n)
                    dve.tensor_tensor(ud[:, j % 2, :], ps[:, 2 + j, 0:D], sc3[:], ALU.mult).then_inc(up_r, 1)

                def group(n, ahead, first=False):
                    chain = {3: lambda: c_max(NG - 1)}
                    for c in range(HC):
                        dve.wait_ge(sil_r, HC * n + c + 1)
                        dve.scalar_tensor_tensor(ha_f[:, c, :], ps[:, d_bank(c, first) + 1, :], sc1[:, 1, c:c + 1],
                                                 ha_f[:, c, :], ALU.mult, ALU.mult).then_inc(h_r, 1)
                        if c:
                            low(c - 1, ha_f, ha_h, ha_l, 3 * HC * n + c)
                        if first and c in chain:
                            chain[c]()
                    low(HC - 1, ha_f, ha_h, ha_l, 3 * HC * n + HC)
                    if first:
                        c_update(NG - 1)
                        c_stats(NG - 1)
                        dve.wait_ge(inv_c, NG)
                    for layer, (full, part, rest) in enumerate(((hb_f, hb_h, hb_l), (ha_f, ha_h, ha_l))):
                        for c in range(HC):
                            low(c, full, part, rest, 3 * HC * n + HC * (layer + 1) + c + 1)
                    if ahead:
                        dve.wait_ge(d2_ps, 2 * HC * n + 2 * HC)
                        norm(n + 1)
                    update(n, 0)
                    update(n, 1)
                    if ahead:
                        low_turn(n + 1)
                    update(n, 2)
                    update(n, 3)

                norm(0)
                low_turn(0)
                b_end(NG - 1)
                dve.wait_ge(tp, 2 * NT + G)
                c_norm(NG - 1)
                c_stats(NG - 2)
                group(0, True, first=True)
                with dve.Fori(1, NG - 1) as n:
                    group(n, True)
                group(NG - 1, False)

            dve.wait_ge(inv_c, 1)
            dve.wait_ge(tpc, NT - G)
            steps_before = st.n
            dve.wait_ge(fl_r, 1)
            long = dve.value_load(flag[:].bitcast(I32))
            with dve.If(long == 0):
                stage_d(True)
            st.n = steps_before
            with dve.Else():
                stage_d(False)

        @block.gpsimd
        def _(pool):
            st = Steps(pool, pstep)

            def invert(t0, n, n_stats, ready=stats, done=inv):
                pool.wait_ge(ready, n_stats)
                v = mv[:, bass.ds(t0, n), 1:2].rearrange("p t o -> p (t o)")
                st.link(pool.tensor_tensor(veps[:, bass.ds(t0, n)], v, eps_t[:, 0:n], ALU.add))
                pool.tensor_tensor(rstd[:, bass.ds(t0, n)], veps[:, bass.ds(t0, n)], half_t[:, 0:n], ALU.pow
                                   ).then_inc(done, 1)

            pool.wait_ge(const_ready, 3)
            for b in range(B):
                invert(b * JT, JT, b + 1)
            pool.wait_ge(ex_ps, E)
            pool.wait_ge(inv, B)
            pool.memset(P1T[64:LP], 0.0).then_inc(zero_ready, 1)
            pool.wait_ge(zero_ready, 3)
            pool.memset(SS[64:LP], 0.0).then_inc(zero_ready, 1)
            pool.wait_ge(zero_ready, 4)
            with pool.Fori(0, B) as b:
                st.enter(b, 2)
                for j in range(JT):
                    pool.wait_ge(up_r, b * JT + (j + 1))
                    xt = of(x, b * JT + j)
                    pool.tensor_tensor(xt, xt, u1[:, j % 2, :], ALU.add).then_inc(xupd, 1)
                    if j == JT - 2:
                        invert(b * JT, G, 2 * b + B + 1)
                invert(b * JT + G, G, 2 * b + B + 2)
            st.leave(B)
            invert(0, G, STATS_A + 1)
            invert(G, G, STATS_A + 2)
            with pool.Fori(2, NG) as g:
                st.enter(g - 2, 2)
                invert(G * (g - 2), G, g - 1, stats_c, inv_c)
                invert(G * g, G, STATS_A + 1 + g)
            st.leave(NG - 2)
            pool.wait_ge(h2_in, 16)
            for i in range(n_h2 // SLICE):
                part = slice(i * SLICE, (i + 1) * SLICE)
                pool.tensor_copy(h2_round[:, part], h2_raw[:, part]).then_inc(h2_rd, 1)
            for c in (NG - 2, NG - 1):
                invert(G * c, G, c + 1, stats_c, inv_c)
            with pool.Fori(0, NG) as n:
                for j in range(G):
                    pool.wait_ge(up_r, UP_A + 1 + G * n + j)
                    xt = of(x, G * n + j)
                    pool.tensor_tensor(xt, xt, ud[:, j % 2, :], ALU.add).then_inc(xupd, 1)


INV_A = B + 2 * B
A_STEPS = 1 + 2 + 2 + 2 + JT + JT + JT
BC_STEPS = 2 * (1 + G + 1 + G + 5 + G * E // 2 + 2 * G + 1 + 2 * G) + 1


def interpolation():
    pos = (np.arange(S, dtype=np.float32) + np.float32(0.5)) * np.float32(L / S) - np.float32(0.5)
    pos = np.clip(pos, np.float32(0), np.float32(L - 1))
    lo = np.floor(pos).astype(np.int32)
    hi = np.minimum(lo + 1, L - 1)
    w = (pos - lo.astype(np.float32)).astype(np.float32)
    m = np.zeros((LP, S), np.float32)
    np.add.at(m, (lo, np.arange(S)), 1 - w)
    np.add.at(m, (hi, np.arange(S)), w)
    return np.ascontiguousarray(m.reshape(LP, P, JT).transpose(0, 2, 1).reshape(LP, S))


def kernel(**inputs):
    import concourse.bacc as bacc
    from concourse.bass_utils import run_bass_kernel_spmd as run

    a = {k: np.asarray(v) for k, v in inputs.items()}

    def chunks(w):
        return np.ascontiguousarray(w.reshape(-1, P, w.shape[-1]).transpose(1, 0, 2))

    def column(v):
        return np.ascontiguousarray(v.reshape(-1, P).T)

    pre = "L0_xattn_"
    wg = a[pre + "Wg"]
    weights = {"Wk_sT": a[pre + "Wk_s"].T, "Wq_sT": a[pre + "Wq_s"].T, "Wv_sT": a[pre + "Wv_s"].T,
               "Wq_c": a[pre + "Wq_c"], "Wk_c": a[pre + "Wk_c"], "Wv_cT": a[pre + "Wv_c"].T,
               "WgT0": wg[:, :D].T, "WgT1": wg[:, D:].T, "W1T": a["L1_xattn_W"].T}
    vectors = {n: a[pre + n] for n in COLS[:-1] + ["bg"]} | {"b1": a["L1_xattn_b"]}
    mask = a["mask_BxS2_bf0"]
    ctxt = a["ctx_1024"]
    f = "L1_ffn_"
    arrays = {
        "x": a["x"],
        "aw": np.stack([chunks(weights[n]) for n in AW], 1),
        "ctxT": chunks(ctxt.reshape(B * L, D).T),
        "ctx": np.ascontiguousarray(ctxt.transpose(1, 0, 2)),
        "cols": np.stack([column(vectors[n]) for n in COLS], 1),
        "rows": np.stack([vectors[n] for n in ROWS]),
        "ident": np.eye(P, dtype=np.float32),
        "maskT": np.ascontiguousarray(mask.T),
        "Wr": chunks(a["L0_ffn_Wr"]),
        "scales": np.stack([column(a[f + n]) for n in ("w1_s", "w2_s", "h1_s", "h2_s")], 1),
        "gates": np.concatenate([a["g_xattn"], a["g_ffn"]]),
        "w3_s": a[f + "w3_s"],
        "interp": interpolation(),
        "Wi": np.ascontiguousarray(a["L0_ffn_Wi"].transpose(2, 0, 1).reshape(KC, P, E, D).transpose(1, 0, 2, 3)),
        "Wo": np.ascontiguousarray(a["L0_ffn_Wo"].transpose(1, 0, 2).reshape(KC, P, E, D).transpose(1, 0, 2, 3)),
        "w1": chunks(a[f + "w1_w"].T), "w2": chunks(a[f + "w2_w"].T),
        "h1": chunks(a[f + "h1_w"].T), "h2": chunks(a[f + "h2_w"].T), "w3": chunks(a[f + "w3_w"].T),
    }
    nc = bacc.Bacc("TRN2", target_bir_lowering=False, num_devices=1)
    d = {n: nc.dram_tensor("in_" + n, v.shape, mybir.dt.from_np(v.dtype), kind="ExternalInput").ap()
         for n, v in arrays.items()}
    d["out"] = nc.dram_tensor("out", (NG, P, G, D), F32, kind="ExternalOutput").ap()
    program(nc, d)
    r = run(nc, [{"in_" + n: v for n, v in arrays.items()}], core_ids=[0])
    out = r.results[0]["out"].reshape(B, JT // G, P, G, D).transpose(0, 2, 1, 3, 4)
    return np.ascontiguousarray(out.reshape(B, S, D))
```
